# Optimizing a Trainium2 kernel written in Bass

```python
import numpy as np
import jax
import jax.numpy as jnp

def _softmax(x, axis=-1):
    return jax.nn.softmax(x, axis=axis)

def _gelu(x):
    return jax.nn.gelu(x, approximate=True)

def _silu(x):
    return jax.nn.silu(x)

def _sigmoid(x):
    return jax.nn.sigmoid(x)

def _layernorm(x, axis=-1, eps=1e-05):
    m = jnp.mean(x, axis=axis, keepdims=True)
    v = jnp.var(x, axis=axis, keepdims=True)
    return (x - m) / jnp.sqrt(v + eps)

def _scatter_add(tgt, idx, src, axis=0):
    return tgt.at[idx].add(src)

def _segment_sum(src, seg, n):
    return jax.ops.segment_sum(src, seg, n)
kernel_name = 'mk_flamingo_gated_d2_seqx_r8_f6c735'

def setup_inputs(seed: int=0):
    np.random.seed(seed)
    _w = jnp.asarray

    def _rec_inputs():
        import jax
        import jax.numpy as jnp
        _rk = jax.random.key(seed)
        x = 7.22e-05 + 1 * jax.random.normal(jax.random.fold_in(_rk, 1), (32, 64, 256), jnp.float32)
        _lenS = 64 - jax.random.randint(jax.random.fold_in(_rk, 7), (32,), 0, max(1, 64 // 4) + 1, jnp.int32)
        _lenS2 = 64 - jax.random.randint(jax.random.fold_in(_rk, 8), (32,), 0, max(1, 64 // 4) + 1, jnp.int32)
        _ctx_512P = jax.random.normal(jax.random.fold_in(_rk, 11), (32, 16, 64), jnp.float32)
        _ctx_512c = jax.random.dirichlet(jax.random.fold_in(_rk, 511), 0.3 * jnp.ones((16,), jnp.float32), (32, 64))
        _ctx_512t = jnp.einsum('bsk,bkd->bsd', _ctx_512c, _ctx_512P)
        _ctx_512t = _ctx_512t * jax.lax.rsqrt(jnp.mean(jnp.square(_ctx_512t)) + 1e-12) * 0.953939
        ctx_512 = -0.000514642 + 1.00011 * (_ctx_512t + 0.3 * jax.random.normal(jax.random.fold_in(_rk, 611), (32, 64, 64), jnp.float32))
        _g = jax.random.normal(jax.random.fold_in(_rk, 9001), (2, 2), jnp.float32)
        _g = jnp.sign(_g) * jnp.maximum(jnp.abs(_g), 1.0) + (_g == 0) * 1.0
        g_xattn = _g[0]
        g_ffn = _g[1]
        return (x, ctx_512, g_xattn, g_ffn)
    x, ctx_512, g_xattn, g_ffn = _rec_inputs()

    def _L0_xattn_setup():
        import jax, jax.numpy as jnp
        import numpy as np
        N_HEADS = 16
        N_KV_HEADS = 4
        ROPE_THETA = 10000.0
        EPS = 1e-05

        def _rms_norm(x, w):
            var = jnp.mean(x * x, axis=-1, keepdims=True)
            return x * jax.lax.rsqrt(var + EPS) * w

        def _rope_sin_cos(T, head_dim, dtype):
            inv_freq = 1.0 / ROPE_THETA ** (jnp.arange(0, head_dim, 2, dtype=jnp.float32) / head_dim)
            t = jnp.arange(T, dtype=jnp.float32)
            freqs = jnp.outer(t, inv_freq)
            emb = jnp.concatenate([freqs, freqs], -1)
            return (jnp.sin(emb).astype(dtype)[None, None], jnp.cos(emb).astype(dtype)[None, None])

        def _rotate_half(x):
            h = x.shape[-1] // 2
            x1, x2 = (x[..., :h], x[..., h:])
            return jnp.concatenate([-x2, x1], axis=-1)
        key = jax.random.key(seed)
        ks = jax.random.split(key, 6)
        B, T, C = (2, 256, 256)
        Ckv = C // N_HEADS * N_KV_HEADS
        return {'q': jax.random.normal(ks[0], (B, T, C), jnp.float32), 'k': jax.random.normal(ks[1], (B, T, Ckv), jnp.float32), 'v': jax.random.normal(ks[2], (B, T, Ckv), jnp.float32), 'q_norm_w': jnp.ones((C,), jnp.float32), 'k_norm_w': jnp.ones((Ckv,), jnp.float32), 'w_out': jax.random.normal(ks[3], (C, C), jnp.float32) * C ** (-0.5)}
    _L0_xattn_all = _L0_xattn_setup()
    _L0_xattn_in = {k: v for k, v in _L0_xattn_all.items() if k in ('q_norm_w', 'k_norm_w', 'w_out')}
    del _L0_xattn_all

    def _L0_ffn_setup():
        import jax, jax.numpy as jnp
        import numpy as np
        TOP_K = 2
        EPS = 1e-06
        key = jax.random.key(seed)
        ks = jax.random.split(key, 4)
        B, L, D, E, ED = (2, 256, 256, 8, 256)
        scale_gu = (6.0 / D) ** 0.5
        scale_dn = (6.0 / ED) ** 0.5
        return {'x': jax.random.normal(ks[0], (B, L, D), jnp.float32), 'router_scale': jnp.ones((D,), jnp.float32), 'gate_w': jax.random.normal(ks[1], (D, E), jnp.float32) * D ** (-0.5), 'gate_up': jax.random.uniform(ks[2], (E, D, 2 * ED), jnp.float32, -scale_gu, scale_gu), 'down': jax.random.uniform(ks[3], (E, ED, D), jnp.float32, -scale_dn, scale_dn), 'per_expert_scale': jnp.ones((E,), jnp.float32)}
    _L0_ffn_all = _L0_ffn_setup()
    _L0_ffn_in = {k: v for k, v in _L0_ffn_all.items() if k in ('router_scale', 'gate_w', 'gate_up', 'down', 'per_expert_scale')}
    del _L0_ffn_all

    def _L1_xattn_setup():
        import jax, jax.numpy as jnp
        import numpy as np
        B, S, L = (2, 128, 128)
        DIM_Q, H, K, D_C, D_CQ, R = (256, 16, 128, 64, 192, 64)

        def _rope_tables(seq_len, dim, dtype):
            inv_freq = 1.0 / 10000.0 ** (jnp.arange(0, dim, 2, dtype=dtype) / dim)
            t = jnp.arange(seq_len, dtype=dtype)
            freqs = t[:, None] * inv_freq[None, :]
            sin = jnp.repeat(jnp.sin(freqs), 2, axis=-1)
            cos = jnp.repeat(jnp.cos(freqs), 2, axis=-1)
            return (sin, cos)

        def _rotate_half(x):
            h = x.shape[-1] // 2
            return jnp.concatenate([-x[..., h:], x[..., :h]], axis=-1)
        key = jax.random.key(seed)
        ks = jax.random.split(key, 8)
        s_in = 1.0 / np.sqrt(DIM_Q)
        s_k = 1.0 / np.sqrt(K)
        s_cq = 1.0 / np.sqrt(D_CQ)
        s_c = 1.0 / np.sqrt(D_C)
        return {'hidden_q': jax.random.normal(ks[0], (B, S, DIM_Q), jnp.float32), 'kv_c': jax.random.normal(ks[1], (B, L, D_C), jnp.float32), 'Wq': jax.random.normal(ks[2], (H * K, DIM_Q), jnp.float32) * s_in, 'w_kc_q': jax.random.normal(ks[3], (H, K, D_CQ), jnp.float32) * s_k, 'w_kc_kv': jax.random.normal(ks[4], (H, K, D_C), jnp.float32) * s_k, 'W_qr': jax.random.normal(ks[5], (H, D_CQ, R), jnp.float32) * s_cq / np.sqrt(R), 'W_kr': jax.random.normal(ks[6], (H, D_C, R), jnp.float32) * s_c, 'Wo': jax.random.normal(ks[7], (DIM_Q, H * K), jnp.float32) * s_k}
    _L1_xattn_all = _L1_xattn_setup()
    _L1_xattn_in = {k: v for k, v in _L1_xattn_all.items() if k in ('Wq', 'w_kc_q', 'w_kc_kv', 'W_qr', 'W_kr', 'Wo')}
    del _L1_xattn_all

    def _L1_ffn_setup():
        import jax, jax.numpy as jnp
        import numpy as np
        B, S, H, I = (1, 64, 256, 768)

        def _quantized_matmul(x, w, scale):
            wq = w.astype(jnp.float8_e4m3fn).astype(x.dtype)
            y = jnp.einsum('bsi,io->bso', x, wq)
            return y * scale
        key = jax.random.key(seed)
        ks = jax.random.split(key, 7)
        return {'x': jax.random.normal(ks[0], (B, S, H), dtype=jnp.float32), 'gate_w': jax.random.normal(ks[1], (H, I), dtype=jnp.float32) * 0.02, 'up_w': jax.random.normal(ks[2], (H, I), dtype=jnp.float32) * 0.02, 'down_w': jax.random.normal(ks[3], (I, H), dtype=jnp.float32) * 0.02, 'gate_scale': jax.random.uniform(ks[4], (I,), dtype=jnp.float32, minval=0.5, maxval=1.5), 'up_scale': jax.random.uniform(ks[5], (I,), dtype=jnp.float32, minval=0.5, maxval=1.5), 'down_scale': jax.random.uniform(ks[6], (H,), dtype=jnp.float32, minval=0.5, maxval=1.5)}
    _L1_ffn_all = _L1_ffn_setup()
    _L1_ffn_in = {k: v for k, v in _L1_ffn_all.items() if k in ('gate_w', 'up_w', 'down_w', 'gate_scale', 'up_scale', 'down_scale')}
    del _L1_ffn_all
    return {'x': x, 'ctx_512': ctx_512, 'g_xattn': g_xattn, 'g_ffn': g_ffn, 'L0_xattn_q_norm_w': _L0_xattn_in['q_norm_w'], 'L0_xattn_k_norm_w': _L0_xattn_in['k_norm_w'], 'L0_xattn_w_out': _L0_xattn_in['w_out'], 'L0_ffn_router_scale': _L0_ffn_in['router_scale'], 'L0_ffn_gate_w': _L0_ffn_in['gate_w'], 'L0_ffn_gate_up': _L0_ffn_in['gate_up'], 'L0_ffn_down': _L0_ffn_in['down'], 'L0_ffn_per_expert_scale': _L0_ffn_in['per_expert_scale'], 'L1_xattn_Wq': _L1_xattn_in['Wq'], 'L1_xattn_w_kc_q': _L1_xattn_in['w_kc_q'], 'L1_xattn_w_kc_kv': _L1_xattn_in['w_kc_kv'], 'L1_xattn_W_qr': _L1_xattn_in['W_qr'], 'L1_xattn_W_kr': _L1_xattn_in['W_kr'], 'L1_xattn_Wo': _L1_xattn_in['Wo'], 'L1_ffn_gate_w': _L1_ffn_in['gate_w'], 'L1_ffn_up_w': _L1_ffn_in['up_w'], 'L1_ffn_down_w': _L1_ffn_in['down_w'], 'L1_ffn_gate_scale': _L1_ffn_in['gate_scale'], 'L1_ffn_up_scale': _L1_ffn_in['up_scale'], 'L1_ffn_down_scale': _L1_ffn_in['down_scale']}

def reference(x, ctx_512, g_xattn, g_ffn, L0_xattn_q_norm_w, L0_xattn_k_norm_w, L0_xattn_w_out, L0_ffn_router_scale, L0_ffn_gate_w, L0_ffn_gate_up, L0_ffn_down, L0_ffn_per_expert_scale, L1_xattn_Wq, L1_xattn_w_kc_q, L1_xattn_w_kc_kv, L1_xattn_W_qr, L1_xattn_W_kr, L1_xattn_Wo, L1_ffn_gate_w, L1_ffn_up_w, L1_ffn_down_w, L1_ffn_gate_scale, L1_ffn_up_scale, L1_ffn_down_scale):
    import jax
    import jax.numpy as jnp

    def _L0_xattn_ref(q, k, v, q_norm_w, k_norm_w, w_out):
        import jax, jax.numpy as jnp
        import numpy as np
        N_HEADS = 16
        N_KV_HEADS = 4
        ROPE_THETA = 10000.0
        EPS = 1e-05

        def _rms_norm(x, w):
            var = jnp.mean(x * x, axis=-1, keepdims=True)
            return x * jax.lax.rsqrt(var + EPS) * w

        def _rope_sin_cos(T, head_dim, dtype):
            inv_freq = 1.0 / ROPE_THETA ** (jnp.arange(0, head_dim, 2, dtype=jnp.float32) / head_dim)
            t = jnp.arange(T, dtype=jnp.float32)
            freqs = jnp.outer(t, inv_freq)
            emb = jnp.concatenate([freqs, freqs], -1)
            return (jnp.sin(emb).astype(dtype)[None, None], jnp.cos(emb).astype(dtype)[None, None])

        def _rotate_half(x):
            h = x.shape[-1] // 2
            x1, x2 = (x[..., :h], x[..., h:])
            return jnp.concatenate([-x2, x1], axis=-1)
        B, T, C = q.shape
        hd = C // N_HEADS
        g = N_HEADS // N_KV_HEADS
        q = _rms_norm(q, q_norm_w)
        k = _rms_norm(k, k_norm_w)
        q = q.reshape(B, T, N_HEADS, hd).transpose(0, 2, 1, 3)
        k = k.reshape(B, T, N_KV_HEADS, hd).transpose(0, 2, 1, 3)
        v = v.reshape(B, T, N_KV_HEADS, hd).transpose(0, 2, 1, 3)
        sin, cos = _rope_sin_cos(T, hd, q.dtype)
        q = q * cos + _rotate_half(q) * sin
        k = k * cos + _rotate_half(k) * sin
        qg = q.reshape(B, N_KV_HEADS, g, T, hd)
        scale = 1.0 / jnp.sqrt(jnp.asarray(hd, q.dtype))
        scores = jnp.einsum('bgnqd,bgkd->bgnqk', qg, k) * scale
        causal = jnp.tril(jnp.ones((T, T), bool))
        scores = jnp.where(causal, scores, jnp.asarray(-1e+30, scores.dtype))
        attn = jax.nn.softmax(scores, axis=-1)
        out = jnp.einsum('bgnqk,bgkd->bgnqd', attn, v)
        out = out.reshape(B, N_HEADS, T, hd).transpose(0, 2, 1, 3).reshape(B, T, C)
        return out @ w_out.T

    def _L0_ffn_ref(x, router_scale, gate_w, gate_up, down, per_expert_scale):
        import jax, jax.numpy as jnp
        import numpy as np
        TOP_K = 2
        EPS = 1e-06
        B, L, D = x.shape
        E = gate_up.shape[0]
        h = x * jax.lax.rsqrt(jnp.mean(x * x, axis=-1, keepdims=True) + EPS)
        h = h * D ** (-0.5) * router_scale
        logits = (h @ gate_w).astype(jnp.float32)
        probs = jax.nn.softmax(logits, axis=-1)
        w, idx = jax.lax.top_k(probs, TOP_K)
        w = w / jnp.clip(jnp.sum(w, axis=-1, keepdims=True), 1e-12)
        w = w.astype(x.dtype)
        N = B * L
        xf = x.reshape(N, D)
        idxf = idx.reshape(N, TOP_K)
        wf = w.reshape(N, TOP_K)
        combine = jnp.zeros((N, E), x.dtype).at[jnp.arange(N)[:, None], idxf].add(wf)
        hh = jnp.einsum('nd,edf->nef', xf, gate_up)
        gate, up = jnp.split(hh, 2, axis=-1)
        act = jax.nn.gelu(gate, approximate=False) * up
        y = jnp.einsum('nef,efd->ned', act, down)
        out = jnp.einsum('ne,ned->nd', combine * per_expert_scale, y)
        return out.reshape(B, L, D)

    def _L1_xattn_ref(hidden_q, kv_c, Wq, w_kc_q, w_kc_kv, W_qr, W_kr, Wo):
        import jax, jax.numpy as jnp
        import numpy as np
        B, S, L = (2, 128, 128)
        DIM_Q, H, K, D_C, D_CQ, R = (256, 16, 128, 64, 192, 64)

        def _rope_tables(seq_len, dim, dtype):
            inv_freq = 1.0 / 10000.0 ** (jnp.arange(0, dim, 2, dtype=dtype) / dim)
            t = jnp.arange(seq_len, dtype=dtype)
            freqs = t[:, None] * inv_freq[None, :]
            sin = jnp.repeat(jnp.sin(freqs), 2, axis=-1)
            cos = jnp.repeat(jnp.cos(freqs), 2, axis=-1)
            return (sin, cos)

        def _rotate_half(x):
            h = x.shape[-1] // 2
            return jnp.concatenate([-x[..., h:], x[..., :h]], axis=-1)
        b, s, _ = hidden_q.shape
        l = kv_c.shape[1]
        q_hk = (hidden_q @ Wq.T).reshape(b, s, H, K)
        q_big = jnp.einsum('bshk,hkq->bshq', q_hk, w_kc_q)
        sin, cos = _rope_tables(l, D_C, kv_c.dtype)
        kv_rope = kv_c * cos[None] + _rotate_half(kv_c) * sin[None]
        q_r = jnp.einsum('bshq,hqr->bhsr', q_big, W_qr)
        k_r = jnp.einsum('bld,hdr->bhlr', kv_rope, W_kr)
        scores = jnp.einsum('bhsr,bhlr->bhsl', q_r, k_r)
        attn = jax.nn.softmax(scores, axis=-1)
        ctx_c = jnp.einsum('bhsl,bld->bhsd', attn, kv_rope)
        ctx_lat = jnp.einsum('bhsd,hkd->bshk', ctx_c, w_kc_kv)
        out = ctx_lat.reshape(b, s, H * K) @ Wo.T
        return out

    def _L1_ffn_ref(x, gate_w, up_w, down_w, gate_scale, up_scale, down_scale):
        import jax, jax.numpy as jnp
        import numpy as np
        B, S, H, I = (1, 64, 256, 768)

        def _quantized_matmul(x, w, scale):
            wq = w.astype(jnp.float8_e4m3fn).astype(x.dtype)
            y = jnp.einsum('bsi,io->bso', x, wq)
            return y * scale
        gate = jax.nn.silu(_quantized_matmul(x, gate_w, gate_scale))
        up = _quantized_matmul(x, up_w, up_scale)
        fuse = gate * up
        return _quantized_matmul(fuse, down_w, down_scale)
    x = x + jnp.tanh(g_xattn[0]) * _L0_xattn_ref(_layernorm(x, axis=-1), ctx_512, ctx_512, L0_xattn_q_norm_w, L0_xattn_k_norm_w, L0_xattn_w_out)
    x = x + jnp.tanh(g_ffn[0]) * _L0_ffn_ref(_layernorm(x, axis=-1), L0_ffn_router_scale, L0_ffn_gate_w, L0_ffn_gate_up, L0_ffn_down, L0_ffn_per_expert_scale)
    x = x + jnp.tanh(g_xattn[1]) * _L1_xattn_ref(_layernorm(x, axis=-1), ctx_512, L1_xattn_Wq, L1_xattn_w_kc_q, L1_xattn_w_kc_kv, L1_xattn_W_qr, L1_xattn_W_kr, L1_xattn_Wo)
    x = x + jnp.tanh(g_ffn[1]) * _L1_ffn_ref(_layernorm(x, axis=-1), L1_ffn_gate_w, L1_ffn_up_w, L1_ffn_down_w, L1_ffn_gate_scale, L1_ffn_up_scale, L1_ffn_down_scale)
    return x

_drawn_inputs = setup_inputs


def setup_inputs(seed=0):
    import zlib

    import numpy as np

    out = dict(_drawn_inputs(seed))
    spreads = {'g_ffn': (-1.0, 0.6),
     'L0_xattn_q_norm_w': (1.0, 0.2),
     'L0_xattn_k_norm_w': (1.0, 0.2),
     'L0_ffn_router_scale': (1.0, 0.2),
     'L0_ffn_per_expert_scale': (1.0, 0.2)}
    factors = {'L1_ffn_gate_w': 4.031,
     'L1_ffn_up_w': 3.988,
     'L1_ffn_down_w': 4.013,
     'L1_ffn_gate_scale': 8.0,
     'L1_ffn_up_scale': 8.0,
     'L1_ffn_down_scale': 8.0}
    for name, (base, spread) in spreads.items():
        noise = np.random.default_rng([zlib.crc32(name.encode()), seed]).standard_normal(out[name].shape)
        drawn = base * np.exp(spread * noise) if base else spread * noise
        out[name] = jnp.asarray(drawn.astype(out[name].dtype))
    for name, factor in factors.items():
        out[name] = (out[name] * factor).astype(out[name].dtype)
    return out
```

```python
import concourse.bass as bass
from concourse import mybir
from contextlib import ExitStack

FP32 = mybir.dt.float32
F32R = mybir.dt.float32r
BF16 = mybir.dt.bfloat16
I32 = mybir.dt.int32
U32 = mybir.dt.uint32
ALU = mybir.AluOpType
ACT = mybir.ActivationFunctionType
AX = mybir.AxisListType

B, S, C, DCTX = 32, 64, 256, 64
P = 128
NT = B * S // P
NBLK, TPB = NT // 4, 4
BT = TPB * P
CT = C // P
H, HD, KVH = 16, 16, 4
NE, ED = 8, 256
KD, DCQ, R = 128, 192, 64
FI, FT = 768, 768 // 128
GH = 4
LN_EPS, RMS_EPS, ROUTER_EPS = 1e-5, 1e-5, 1e-6
FP8_EDGE = 464.0

C_ID, C_MASK, C_NSEL, C_COS0, C_SIN0, C_COS1, C_SIN1, C_IOTA, C_HALF = 0, 128, 640, 644, 660, 676, 740, 804, 812
C_END = 814


def bc(ap, axis, n):
    shape = list(ap.shape)
    shape.insert(axis, n)
    return ap.unsqueeze(axis).broadcast_to(shape)


class Link:

    def __init__(self, eng, sem, base=0):
        self.eng, self.sem, self.base, self.n = eng, sem, base, 0

    def __call__(self, ins):
        ins.then_inc(self.sem, 1)
        self.n += 1
        self.eng.wait_ge(self.sem, self.base + self.n)


def rsqrt(nc, link, y, v, tmp):
    link(nc.vector.tensor_scalar(tmp.bitcast(I32), v.bitcast(I32), 1, None, ALU.logical_shift_right))
    link(nc.vector.tensor_scalar(y.bitcast(I32), tmp.bitcast(I32), -1.0, float(0x5F3759DF), ALU.mult, ALU.add))
    for _ in range(4):
        link(nc.vector.tensor_tensor(tmp, v, y, ALU.mult))
        link(nc.vector.tensor_tensor(tmp, tmp, y, ALU.mult))
        link(nc.vector.tensor_scalar(tmp, tmp, -0.5, 1.5, ALU.mult, ALU.add))
        link(nc.vector.tensor_tensor(y, y, tmp, ALU.mult))


def stack_kernel(nc, a, out):
    top = ExitStack()

    def scope(stack, phase=""):
        def sb(name, shape, dt=FP32):
            return stack.enter_context(nc.sbuf_tensor(phase + name, shape, dt))

        def pb(name, shape, dt=FP32):
            return stack.enter_context(nc.psum_tensor(phase + name, shape, dt))

        def sem(name):
            return stack.enter_context(nc.semaphore(phase + name))

        return sb, pb, sem

    with top:
        sb, _, _ = scope(top)
        g = {
            "x": sb("x_res", [P, NT, C]),
            "const": sb("const", [P, C_END]),
            "identb": sb("identb", [P, P], BF16),
            "maskb": sb("maskb", [P, 512], BF16),
            "kr": sb("k_roped", [P, NT, DCTX]),
            "ctxdup": sb("ctxdup", [P, B, DCTX]),
            "kvr": sb("kv_roped_dup", [P, B, DCTX]),
            "mhi": sb("m_hi", [P, CT, H * DCTX], F32R),
            "mlo": sb("m_lo", [P, CT, H * DCTX], F32R),
            "pm": sb("p_out", [P, H // 2, C]),
            "woutT": sb("woutT", [P, 2, C]),
            "cqw": sb("cos_qw", [P, C]),
            "sqw": sb("sin_qw", [P, C]),
            "tg": sb("tanh_gates", [P, 4]),
            "gwhi": sb("router_hi", [P, CT, NE], F32R),
            "gwlo": sb("router_lo", [P, CT, NE], F32R),
            "pes": sb("expert_scale", [P, NE]),
            "fgs": sb("ffn_gate_scale", [P, FT]),
            "fus": sb("ffn_up_scale", [P, FT]),
            "dsg": sb("ffn_down_scale", [P, C]),
            "bn": sb("bn_stats", [P, NT, 6]),
            "mean": sb("mean", [P, NT]),
            "var": sb("variance", [P, NT]),
            "r": sb("ln_rstd", [P, NT]),
            "r2": sb("second_rstd", [P, NT]),
            "ta": sb("small_a", [P, NT]),
            "tb": sb("small_b", [P, NT]),
        }
        with ExitStack() as es:
            setup_phase(nc, a, g, *scope(es, "setup_"))
        with ExitStack() as es:
            sbm, _, _ = scope(es)
            g["whi"] = sbm("moe_hi", [P, NE, 1536], F32R)
            g["wlo"] = sbm("moe_lo", [P, NE, 1536], F32R)
            with ExitStack() as es2:
                attn0_phase(nc, a, g, *scope(es2, "attn0_"))
            with ExitStack() as es2:
                moe_phase(nc, a, g, *scope(es2, "moe_"))
        g["wq8"] = sb("ffn_w", [P, 3 * 1536], F32R)
        with ExitStack() as es:
            attn1_phase(nc, a, g, *scope(es, "attn1_"))
        with ExitStack() as es:
            ffn_phase(nc, a, g, out, *scope(es, "ffn_"))


def setup_phase(nc, a, g, sb, pb, sem):
    ident = g["const"][:, C_ID:C_ID + P]
    ctx = sb("ctx_tok", [P, NT, DCTX])
    sq = sb("ctx_sq", [P, NT, DCTX])
    rk = sb("k_rstd", [P, NT])
    kt1 = sb("k_cos", [P, NT, DCTX])
    kt2 = sb("k_sin", [P, NT, DCTX])
    kv1 = sb("kv_cos", [P, B, DCTX])
    qw = sb("q_norm_b", [P, C])
    kw = sb("k_norm_b", [P, DCTX])
    ckw = sb("cos_kw", [P, DCTX])
    skw = sb("sin_kw", [P, DCTX])
    wout = sb("w_out", [P, 2, C])
    graw = sb("gates_raw", [P, 4])
    gw = sb("router_w", [P, CT, NE])
    rsc = sb("router_scale", [P, CT])
    wkcq = sb("w_kc_q", [P, 2, GH, DCQ])
    wqr = sb("w_qr", [96, 2, 2, GH, R])
    wkr = sb("w_kr", [DCTX, 2, GH, R])
    wq = sb("w_q", [P, 2, GH, C])
    wkv = sb("w_kc_kv", [P, 2, GH, DCTX])
    wo = sb("w_o", [P, 2, 2, GH * KD])
    kcqT = sb("kcqT", [96, 2, GH, KD])
    krT = sb("krT", [P, 2, DCTX])
    woT = sb("woT", [P, GH, C])
    a1T = sb("a1T", [P, 2, KD])
    a2 = sb("a2", [P, 2, 2, DCTX])
    T1 = [pb(f"ps_kcqT{t}", [P, 512]) for t in range(2)]
    T2 = pb("ps_small", [P, 512])
    T3 = pb("ps_woT", [P, GH, C])
    A1 = pb("ps_a1", [P, 512])
    A2 = pb("ps_a2", [P, 2, 512])

    s_const, s_ctx, s_dup, s_x = sem("const_in"), sem("ctx_in"), sem("ctxdup_in"), sem("x_in")
    s_nw, s_small = sem("norm_w_in"), sem("small_in")
    s_w = [sem(f"w_in{u}") for u in range(2)]
    s_t1, s_t2, s_t3 = sem("kcqT_ps"), sem("krT_ps"), sem("woT_ps")
    s_t1e, s_t2e, s_t3e = sem("kcqT_sb"), sem("krT_sb"), sem("woT_sb")
    s_a1, s_a1e, s_a2, s_a2e = sem("a1_ps"), sem("a1_sb"), sem("a2_ps"), sem("a2_sb")
    s_m, s_mhi, s_mlo, s_p, s_pe = sem("m_ps"), sem("m_hi_sb"), sem("m_lo_sb"), sem("p_ps"), sem("p_sb")
    s_wt, s_wte = sem("woutT_ps"), sem("woutT_sb")
    s_v, s_g, s_bn = sem("dve_step"), sem("pool_step"), sem("bn_step")
    s_rk, s_tab, s_tg = sem("rk_ready"), sem("tables_ready"), sem("gates_ready")
    LOADS = 7

    with nc.Block() as block:

        @block.sync
        def _(sp):
            def load(gr):
                u, hs = gr % 2, slice(GH * gr, GH * gr + GH)
                n = s_w[u]
                sp.dma_start(wkcq[:, u], a["L1_xattn_w_kc_q"][hs].rearrange("h k q -> k h q")).then_inc(n, 16)
                for t in range(2):
                    src = a["L1_xattn_W_qr"][hs, 96 * t:96 * t + 96, :].rearrange("h q r -> q h r")
                    sp.dma_start(wqr[:, u, t], src).then_inc(n, 16)
                sp.dma_start(wkr[:, u], a["L1_xattn_W_kr"][hs].rearrange("h d r -> d h r")).then_inc(n, 16)
                src = a["L1_xattn_Wq"][KD * GH * gr:KD * GH * (gr + 1), :].rearrange("(h k) c -> k h c", k=KD)
                sp.dma_start(wq[:, u], src).then_inc(n, 16)
                sp.dma_start(wkv[:, u], a["L1_xattn_w_kc_kv"][hs].rearrange("h k d -> k h d")).then_inc(n, 16)
                src = a["L1_xattn_Wo"][:, KD * GH * gr:KD * GH * (gr + 1)].rearrange("(t o) n -> o t n", o=P)
                sp.dma_start(wo[:, u], src).then_inc(n, 16)

            sp.dma_start(g["const"][:], a["const"]).then_inc(s_const, 16)
            load(0)
            load(1)
            for gr in (2, 3):
                sp.wait_ge(s_mlo, gr - 1)
                load(gr)

        @block.scalar
        def _(act):
            act.dma_start(ctx[:], a["ctx_512"].rearrange("(t b) s c -> (b s) t c", b=2)).then_inc(s_ctx, 16)
            act.dma_start(qw[:], a["L0_xattn_q_norm_w"].partition_broadcast(P)).then_inc(s_nw, 16)
            act.dma_start(kw[:], a["L0_xattn_k_norm_w"].partition_broadcast(P)).then_inc(s_nw, 16)
            for d in range(2):
                act.dma_start(g["ctxdup"][64 * d:64 * d + 64], a["ctx_512"].rearrange("b k c -> k b c")).then_inc(s_dup, 16)
            wv = a["L0_xattn_w_out"].rearrange("(t o) (ct g2 nd) -> t g2 o ct nd", o=P, ct=2, g2=2)
            for ot in range(2):
                for g2 in range(2):
                    dst = wout[:, ot, g2 * P:(g2 + 1) * P].rearrange("p (ct nd) -> p ct nd", ct=2)
                    act.dma_start(dst, wv[ot, g2]).then_inc(s_small, 16)
            act.dma_start(graw[:, 0:2], a["g_xattn"].partition_broadcast(P)).then_inc(s_small, 16)
            act.dma_start(graw[:, 2:4], a["g_ffn"].partition_broadcast(P)).then_inc(s_small, 16)
            act.dma_start(gw[:], a["L0_ffn_gate_w"].rearrange("(t p) e -> p t e", p=P)).then_inc(s_small, 16)
            act.dma_start(rsc[:], a["L0_ffn_router_scale"].rearrange("(t p) -> p t", p=P),
                          allow_slow_non_contiguous=True).then_inc(s_small, 16)
            act.dma_start(g["pes"][:], a["L0_ffn_per_expert_scale"].partition_broadcast(P)).then_inc(s_small, 16)
            act.dma_start(g["fgs"][:], a["L1_ffn_gate_scale"].rearrange("(t p) -> p t", p=P),
                          allow_slow_non_contiguous=True).then_inc(s_small, 16)
            act.dma_start(g["fus"][:], a["L1_ffn_up_scale"].rearrange("(t p) -> p t", p=P),
                          allow_slow_non_contiguous=True).then_inc(s_small, 16)
            act.dma_start(g["dsg"][:], a["L1_ffn_down_scale"].partition_broadcast(P)).then_inc(s_small, 16)
            xv = a["x"].rearrange("(t b) s c -> (b s) t c", b=2)
            for q in range(4):
                act.dma_start(g["x"][:, 4 * q:4 * q + 4], xv[:, 4 * q:4 * q + 4]).then_inc(s_x, 16)
            act.wait_ge(s_small, 12 * 16)
            act.activation(g["tg"][:], graw[:], ACT.Tanh).then_inc(s_tg, 1)
            act.wait_ge(s_wt, 1)
            act.activation(g["woutT"][:], T2[:], ACT.Copy).then_inc(s_wte, 1)
            with act.Fori(0, 4) as gr:
                n = act.snap(gr + 1)
                act.wait_ge(s_t2, n)
                act.activation(krT[:], T2[:, 0:2 * DCTX], ACT.Copy).then_inc(s_t2e, 1)
                act.wait_ge(s_t3, n)
                act.activation(woT[:], T3[:], ACT.Copy).then_inc(s_t3e, 1)
                act.wait_ge(s_m, n)
                act.activation(g["mhi"][:, :, bass.ds(gr * 256, 256)], T1[0][:].rearrange("p (t n) -> p t n", t=CT),
                               ACT.Copy).then_inc(s_mhi, 1)
                act.wait_ge(s_p, n)
                act.activation(g["pm"][:, bass.ds(gr * 2, 2), :], T1[1][:].rearrange("p (t n) -> p t n", t=2),
                               ACT.Copy).then_inc(s_pe, 1)

        @block.tensor
        def _(pe):
            pe.wait_ge(s_const, 16)
            pe.wait_ge(s_small, 12 * 16)
            for g2 in range(2):
                for ot in range(2):
                    last = nc.tensor.transpose(T2[:, (2 * g2 + ot) * P:(2 * g2 + ot + 1) * P], wout[:, ot, g2 * P:(g2 + 1) * P], ident)
            last.then_inc(s_wt, 1)
            pe.wait_ge(s_wte, 1)
            with pe.Fori(0, 2) as i:
                for u in range(2):
                    gr = 2 * i + u
                    n = pe.snap(gr + 1)
                    pe.wait_ge(s_w[u], (i + 1) * (16 * LOADS))
                    for t in range(2):
                        for h in range(GH):
                            last = nc.tensor.transpose(T1[t][0:96, h * KD:(h + 1) * KD],
                                                       wkcq[:, u, h, 96 * t:96 * t + 96], ident)
                    last.then_inc(s_t1, 1)
                    for pr in range(2):
                        last = nc.tensor.transpose(T2[:, pr * DCTX:(pr + 1) * DCTX],
                                                   wkr[:, u, 2 * pr:2 * pr + 2, :].rearrange("p h r -> p (h r)"),
                                                   ident[0:DCTX, 0:DCTX])
                    last.then_inc(s_t2, 1)
                    for h in range(GH):
                        for ot in range(2):
                            last = nc.tensor.transpose(T3[:, h, ot * P:(ot + 1) * P],
                                                       wo[:, u, ot, h * KD:(h + 1) * KD], ident)
                    last.then_inc(s_t3, 1)
                    pe.wait_ge(s_t1e, n)
                    for pr in range(2):
                        for h2 in range(2):
                            h = 2 * pr + h2
                            for t in range(2):
                                last = nc.tensor.matmul(A1[64 * h2:64 * h2 + 64, pr * KD:(pr + 1) * KD],
                                                        wqr[:, u, t, h], kcqT[:, t, h], start=(t == 0), stop=(t == 1))
                    last.then_inc(s_a1, 1)
                    pe.wait_ge(s_t3e, n)
                    for pr in range(2):
                        for h2 in range(2):
                            h = 2 * pr + h2
                            last = nc.tensor.matmul(T1[1][64 * h2:64 * h2 + 64, pr * C:(pr + 1) * C],
                                                    wkv[:, u, h], woT[:, h], start=True, stop=True)
                    last.then_inc(s_p, 1)
                    pe.wait_ge(s_a1e, n)
                    pe.wait_ge(s_t2e, n)
                    for h2 in range(2):
                        for pr in range(2):
                            last = nc.tensor.matmul(A2[:, h2, pr * DCTX:(pr + 1) * DCTX],
                                                    a1T[64 * h2:64 * h2 + 64, pr], krT[64 * h2:64 * h2 + 64, pr],
                                                    start=True, stop=True)
                    last.then_inc(s_a2, 1)
                    pe.wait_ge(s_a2e, n)
                    for ct in range(CT):
                        for h in range(GH):
                            o = (ct * GH + h) * DCTX
                            last = nc.tensor.matmul(T1[0][:, o:o + DCTX], wq[:, u, h, ct * P:(ct + 1) * P],
                                                    a2[:, h % 2, h // 2], start=True, stop=True)
                    last.then_inc(s_m, 1)
                    pe.wait_ge(s_mlo, n)
                    pe.wait_ge(s_pe, n)

        @block.vector
        def _(dve):
            link = Link(dve, s_v)
            dve.wait_ge(s_const, 16)
            link(nc.vector.tensor_copy(g["identb"][:], ident))
            link(nc.vector.tensor_copy(g["maskb"][:], g["const"][:, C_MASK:C_MASK + 512]))
            dve.wait_ge(s_ctx, 16)
            link(nc.vector.tensor_tensor(sq[:], ctx[:], ctx[:], ALU.mult))
            link(nc.vector.tensor_reduce(g["ta"][:], sq[:], AX.X, ALU.add))
            link(nc.vector.tensor_scalar(g["ta"][:], g["ta"][:], 1.0 / DCTX, RMS_EPS, ALU.mult, ALU.add))
            rsqrt(nc, link, rk[:], g["ta"][:], g["tb"][:])
            dve.wait_ge(s_nw, 32)
            cos0, sin0 = g["const"][:, C_COS0:C_COS0 + HD], g["const"][:, C_SIN0:C_SIN0 + HD]
            for w, nh, cw, sw in ((qw, H, g["cqw"], g["sqw"]), (kw, KVH, ckw, skw)):
                wv, cv, sv = (t[:].rearrange("p (h d) -> p h d", d=HD) for t in (w, cw, sw))
                nc.vector.tensor_tensor(cv, wv, bc(cos0, 1, nh), ALU.mult)
                nc.vector.tensor_tensor(sv[:, :, 0:8], wv[:, :, 8:16], bc(sin0[:, 0:8], 1, nh), ALU.mult)
                link(nc.vector.tensor_tensor(sv[:, :, 8:16], wv[:, :, 0:8], bc(sin0[:, 8:16], 1, nh), ALU.mult))
            dve.sem_inc(s_rk, 1)
            dve.wait_ge(s_small, 12 * 16)
            for t in range(CT):
                link(nc.vector.tensor_scalar(gw[:, t], gw[:, t], rsc[:, t:t + 1], None, ALU.mult))
            link(nc.vector.tensor_copy(g["gwhi"][:], gw[:]))
            link(nc.vector.tensor_tensor(g["gwlo"][:], gw[:], g["gwhi"][:].bitcast(FP32), ALU.subtract))
            dve.wait_ge(s_tg, 1)
            link(nc.vector.tensor_scalar(g["pes"][:], g["pes"][:], g["tg"][:, 2:3], None, ALU.mult))
            link(nc.vector.tensor_scalar(g["dsg"][:], g["dsg"][:], g["tg"][:, 3:4], None, ALU.mult))
            with dve.Fori(0, 4) as gr:
                n = dve.snap(gr + 1)
                dve.wait_ge(s_t1, n)
                nc.vector.tensor_copy(kcqT[:, 0], T1[0][0:96, :].rearrange("p (h k) -> p h k", h=GH))
                nc.vector.tensor_copy(kcqT[:, 1], T1[1][0:96, :].rearrange("p (h k) -> p h k", h=GH)).then_inc(s_t1e, 1)
                dve.wait_ge(s_a1, n)
                nc.vector.tensor_copy(a1T[:], A1[:, 0:2 * KD].rearrange("p (h k) -> p h k", h=2)).then_inc(s_a1e, 1)
                dve.wait_ge(s_a2, n)
                nc.vector.tensor_copy(a2[:], A2[:, :, 0:2 * DCTX].rearrange("p h (q d) -> p h q d", q=2)).then_inc(s_a2e, 1)
                dve.wait_ge(s_mhi, n)
                nc.vector.tensor_tensor(g["mlo"][:, :, bass.ds(gr * 256, 256)], T1[0][:].rearrange("p (t n) -> p t n", t=CT),
                                        g["mhi"][:, :, bass.ds(gr * 256, 256)].bitcast(FP32),
                                        ALU.subtract).then_inc(s_mlo, 1)
            dve.wait_ge(s_x, 64)
            with dve.Fori(0, NT) as t:
                nc.vector.bn_stats(g["bn"][:, t, :], g["x"][:, t, :]).then_inc(s_bn, 1)

        @block.gpsimd
        def _(pool):
            link = Link(pool, s_g)
            pool.wait_ge(s_rk, 1)
            link(nc.gpsimd.tensor_tensor(sq[:], ctx[:], bc(rk[:], 2, DCTX), ALU.mult))
            link(nc.gpsimd.tensor_tensor(kt1[:], sq[:], bc(ckw[:], 1, NT), ALU.mult))
            kn, k2, sw = sq[:], kt2[:], skw[:]
            for h in range(KVH):
                o = h * HD
                link(nc.gpsimd.tensor_tensor(k2[:, :, o:o + 8], kn[:, :, o + 8:o + 16], bc(sw[:, o:o + 8], 1, NT), ALU.mult))
                link(nc.gpsimd.tensor_tensor(k2[:, :, o + 8:o + 16], kn[:, :, o:o + 8], bc(sw[:, o + 8:o + 16], 1, NT), ALU.mult))
            link(nc.gpsimd.tensor_tensor(g["kr"][:], kt1[:], kt2[:], ALU.add))
            pool.wait_ge(s_dup, 32)
            cos1, sin1 = g["const"][:, C_COS1:C_COS1 + DCTX], g["const"][:, C_SIN1:C_SIN1 + DCTX]
            link(nc.gpsimd.tensor_tensor(kv1[:], g["ctxdup"][:], bc(cos1, 1, B), ALU.mult))
            link(nc.gpsimd.tensor_tensor(g["kvr"][:, :, 0:32], g["ctxdup"][:, :, 32:64], bc(sin1[:, 0:32], 1, B), ALU.mult))
            link(nc.gpsimd.tensor_tensor(g["kvr"][:, :, 32:64], g["ctxdup"][:, :, 0:32], bc(sin1[:, 32:64], 1, B), ALU.mult))
            link(nc.gpsimd.tensor_tensor(g["kvr"][:], kv1[:], g["kvr"][:], ALU.add))


def ln_rstd(nc, g, link, second_eps=None, scale=1.0):
    bn, mean, var, d = g["bn"], g["mean"][:], g["var"][:], g["ta"][:]
    link(nc.vector.tensor_tensor(mean, bn[:, :, 1], bn[:, :, 4], ALU.add))
    link(nc.vector.tensor_tensor(d, bn[:, :, 1], bn[:, :, 4], ALU.subtract))
    link(nc.vector.tensor_scalar(mean, mean, 0.5, None, ALU.mult))
    link(nc.vector.tensor_tensor(var, bn[:, :, 2], bn[:, :, 5], ALU.add))
    link(nc.vector.tensor_tensor(d, d, d, ALU.mult))
    link(nc.vector.tensor_scalar(var, var, 1.0 / C, None, ALU.mult))
    link(nc.vector.scalar_tensor_tensor(var, d, 0.25, var, ALU.mult, ALU.add))
    link(nc.vector.tensor_scalar(g["ta"][:], var, LN_EPS, None, ALU.add))
    rsqrt(nc, link, g["r"][:], g["ta"][:], g["tb"][:])
    if second_eps is not None:
        link(nc.vector.tensor_tensor(g["ta"][:], var, g["r"][:], ALU.mult))
        link(nc.vector.tensor_tensor(g["ta"][:], g["ta"][:], g["r"][:], ALU.mult))
        link(nc.vector.tensor_scalar(g["ta"][:], g["ta"][:], second_eps, None, ALU.add))
        rsqrt(nc, link, g["r2"][:], g["ta"][:], g["tb"][:])
        link(nc.vector.tensor_scalar(g["r2"][:], g["r2"][:], scale, None, ALU.mult))


def attn0_phase(nc, a, g, sb, pb, sem):
    ident = g["const"][:, C_ID:C_ID + P]
    VW = HD + 1
    qn = sb("q_normed", [P, C])
    qc = sb("q_cos", [P, C])
    qs = sb("q_sin", [P, C])
    qr = sb("q_roped", [P, C])
    krep = sb("k_repeated", [P, KVH, 4, HD])
    qT = sb("qT", [P, 2, P])
    kbd = sb("k_blockdiag", [P, 4, 4, S])
    pr_ = sb("probs", [P, H, S])
    pT = sb("probsT", [P, H // 2, P])
    vbd = sb("v_blockdiag", [P, 2, KVH, 2 * VW])
    on = sb("heads_out", [P, H, HD])
    oT = sb("heads_outT", [P, 2, P])
    mx = sb("score_max", [P, H])
    rec = sb("sum_recip", [P, H])
    rq = sb("q_rstd", [P, NT])
    stage = sb("moe_stage", [P, 1536])
    ps_s = pb("ps_scores", [P, 2, 512])
    ps_pT = pb("ps_probsT", [P, H // 2, P])
    ps_qk = pb("ps_qkT", [P, 4, P])
    ps_o = pb("ps_heads", [P, H, VW + 15])
    ps_oT = pb("ps_headsT", [P, 512])
    ps_y = pb("ps_y", [P, 512])
    pso = ps_o[:].rearrange("p h w -> p (h w)")[:, 0:H * VW]

    s_v = sem("dve_step")
    s_rq, s_qn, s_qc, s_rot, s_qr = sem("rstd_ready"), sem("q_normed"), sem("q_cos"), sem("q_rotated"), sem("q_roped")
    s_k, s_vb, s_v0 = sem("k_repeated"), sem("v_ready"), sem("v_ones")
    s_qkT, s_qkE, s_sc, s_mx = sem("qk_transposed"), sem("qk_in_sbuf"), sem("scores_ready"), sem("max_ready")
    s_sh, s_pr, s_pT, s_pTe = sem("scores_shifted"), sem("probs_ready"), sem("probs_transposed"), sem("probsT_in_sbuf")
    s_pv, s_rec, s_on = sem("heads_ready"), sem("recip_ready"), sem("heads_normed")
    s_oT, s_oTe, s_y, s_x, s_bn = sem("heads_transposed"), sem("headsT_in_sbuf"), sem("y_ready"), sem("x_updated"), sem("bn_ready")
    s_wl, s_whi, s_wlo = sem("expert_loaded"), sem("expert_hi"), sem("expert_lo")

    with nc.Block() as block:

        @block.sync
        def _(sp):
            def load(e):
                gu = a["L0_ffn_gate_up"].rearrange("e (t p) f -> e p t f", p=P)
                dn = a["L0_ffn_down"].rearrange("e (t p) f -> e p t f", p=P)
                st = stage[:, 0:1024].rearrange("p (t f) -> p t f", t=2)
                sp.dma_start(st, gu[bass.ds(e, 1)].rearrange("e p t f -> (e p) t f")).then_inc(s_wl, 16)
                st = stage[:, 1024:1536].rearrange("p (t f) -> p t f", t=2)
                sp.dma_start(st, dn[bass.ds(e, 1)].rearrange("e p t f -> (e p) t f")).then_inc(s_wl, 16)

            load(0)
            with sp.Fori(1, NE) as e:
                sp.wait_ge(s_wlo, e)
                load(e)

        @block.gpsimd
        def _(pool):
            def rotate(t, n, n2):
                pool.wait_ge(s_qn, n)
                if t is not None:
                    pool.wait_ge(s_qr, t)
                q, s, w = (v[:].rearrange("p (h d) -> p h d", d=HD) for v in (qn, qs, g["sqw"]))
                nc.gpsimd.tensor_tensor(s[:, :, 0:8], q[:, :, 8:16], w[:, :, 0:8], ALU.mult).then_inc(s_rot, 1)
                nc.gpsimd.tensor_tensor(s[:, :, 8:16], q[:, :, 0:8], w[:, :, 8:16], ALU.mult).then_inc(s_rot, 1)

            def repeat_k(t, qk):
                if qk is not None:
                    pool.wait_ge(s_qkT, qk)
                kv = g["kr"][:, t, :].rearrange("p (g d) -> p g d", d=HD)
                nc.gpsimd.tensor_copy(krep[:], bc(kv, 2, 4)).then_inc(s_k, 1)

            def values(t, pv):
                if pv is not None:
                    pool.wait_ge(s_pv, pv)
                dst = vbd[:].rearrange("p b g (h w) -> p (b g) h w", w=VW)[:, :, :, 0:HD]
                src = g["ctxdup"][:, bass.ds(2 * t, 2), :].rearrange("p b (g d) -> p (b g) d", d=HD)
                nc.gpsimd.tensor_tensor(dst, bc(src, 2, 2), bc(bc(half, 1, 2 * KVH), 3, HD), ALU.mult).then_inc(s_vb, 1)

            half = g["const"][:, C_HALF:C_HALF + 2]
            ones = vbd[:].rearrange("p b g (h w) -> p (b g) h w", w=VW)[:, :, :, HD]
            nc.gpsimd.tensor_copy(ones, bc(half, 1, 2 * KVH)).then_inc(s_v0, 1)
            repeat_k(0, None)
            rotate(None, 1, None)
            repeat_k(1, 1)
            rotate(1, 2, None)
            values(0, None)

            def expert(e):
                pool.wait_ge(s_whi, e + 1)
                nc.gpsimd.tensor_tensor(g["wlo"][:, e, :], stage[:], g["whi"][:, e, :].bitcast(FP32),
                                        ALU.subtract).then_inc(s_wlo, 1)

            with pool.Fori(0, NE - 1) as i:
                for u in range(2):
                    t = 2 * i + u
                    repeat_k(t + 2, t + 2)
                    rotate(t + 2, t + 3, None)
                    values(t + 1, t + 1)
                expert(i)
            expert(NE - 1)
            values(NT - 1, NT - 1)

        @block.vector
        def _(dve):
            link = Link(dve, s_v)
            ln_rstd(nc, g, link, RMS_EPS)
            link(nc.vector.tensor_tensor(rq[:], g["r"][:], g["r2"][:], ALU.mult))
            dve.sem_inc(s_rq, 1)

            def rope(t, first=False):
                n = dve.snap(t + 1) if not isinstance(t, int) else t + 1
                if not first:
                    dve.wait_ge(s_rot, 2 * t)
                nc.vector.tensor_scalar(qn[:], g["x"][:, t, :], g["mean"][:, bass.ds(t, 1)], rq[:, bass.ds(t, 1)],
                                        ALU.subtract, ALU.mult).then_inc(s_qn, 1)
                dve.wait_ge(s_qn, n)
                nc.vector.tensor_tensor(qc[:], qn[:], g["cqw"][:], ALU.mult).then_inc(s_qc, 1)
                dve.wait_ge(s_qc, n)
                dve.wait_ge(s_rot, 2 * (t + 1))
                if not first:
                    dve.wait_ge(s_qkT, t)
                nc.vector.tensor_tensor(qr[:], qc[:], qs[:], ALU.add).then_inc(s_qr, 1)

            def softmax_shift(t):
                n = dve.snap(t + 1) if not isinstance(t, int) else t + 1
                dve.wait_ge(s_sc, n)
                sv = ps_s[:].rearrange("p b (h k) -> p (b h) k", k=S)
                nc.vector.tensor_reduce(mx[:], sv, AX.X, ALU.max).then_inc(s_mx, 1)
                dve.wait_ge(s_mx, n)
                nc.vector.tensor_tensor(pr_[:], sv, bc(mx[:], 2, S), ALU.subtract).then_inc(s_sh, 1)

            def finish(t):
                n = dve.snap(t + 1) if not isinstance(t, int) else t + 1
                dve.wait_ge(s_pv, n)
                ov = pso.rearrange("p (h w) -> p h w", w=VW)
                nc.vector.reciprocal(rec[:], ov[:, :, HD]).then_inc(s_rec, 1)
                dve.wait_ge(s_rec, n)
                nc.vector.tensor_tensor(on[:], ov[:, :, 0:HD], bc(rec[:], 2, HD), ALU.mult).then_inc(s_on, 1)

            def residual(t):
                n = dve.snap(t + 1) if not isinstance(t, int) else t + 1
                dve.wait_ge(s_y, n)
                nc.vector.scalar_tensor_tensor(g["x"][:, t, :], ps_y[:, 0:C], g["tg"][:, 0:1], g["x"][:, t, :],
                                               ALU.mult, ALU.add).then_inc(s_x, 1)
                dve.wait_ge(s_x, n)
                nc.vector.bn_stats(g["bn"][:, t, :], g["x"][:, t, :]).then_inc(s_bn, 1)

            rope(0, True)
            rope(1)
            softmax_shift(0)
            with dve.Fori(0, NT - 2) as t:
                softmax_shift(t + 1)
                finish(t)
                rope(t + 2)
                residual(t)
            softmax_shift(NT - 1)
            for t in (NT - 2, NT - 1):
                finish(t)
                residual(t)

        @block.scalar
        def _(act):
            def qk(t):
                act.wait_ge(s_qkT, t + 1)
                nc.scalar.activation(qT[:], ps_qk[:, 0:2], ACT.Copy)
                for n in range(4):
                    sel = g["const"][:, C_NSEL + n:C_NSEL + n + 1]
                    last = nc.scalar.activation(kbd[:, :, n, :], ps_qk[:, 2:4].rearrange("p c (b k) -> p (c b) k", b=2),
                                                ACT.Copy, scale=sel)
                last.then_inc(s_qkE, 1)

            def exps(t):
                act.wait_ge(s_sh, t + 1)
                nc.scalar.activation(pr_[:], pr_[:], ACT.Exp, scale=float(HD) ** -0.5).then_inc(s_pr, 1)

            def probsT(t):
                act.wait_ge(s_pT, t + 1)
                nc.scalar.activation(pT[:], ps_pT[:], ACT.Copy).then_inc(s_pTe, 1)

            def headsT(t):
                act.wait_ge(s_oT, t + 1)
                nc.scalar.activation(oT[:], ps_oT[:, 0:2 * P], ACT.Copy).then_inc(s_oTe, 1)

            def expert(e):
                act.wait_ge(s_wl, 32 * (e + 1))
                nc.scalar.activation(g["whi"][:, e, :], stage[:], ACT.Copy).then_inc(s_whi, 1)

            qk(0)
            exps(0)
            qk(1)
            with act.Fori(0, NE - 1) as i:
                for u in range(2):
                    t = 2 * i + u
                    probsT(t)
                    exps(t + 1)
                    headsT(t)
                    qk(t + 2)
                expert(i)
            expert(NE - 1)
            probsT(NT - 2)
            exps(NT - 1)
            headsT(NT - 2)
            probsT(NT - 1)
            headsT(NT - 1)

        @block.tensor
        def _(pe):
            def qkT(t):
                pe.wait_ge(s_qr, t + 1)
                pe.wait_ge(s_k, t + 1)
                kr = krep[:].rearrange("p g n d -> p (g n d)")
                for c in range(2):
                    nc.tensor.transpose(ps_qk[:, c], qr[:, c * P:(c + 1) * P], ident)
                for c in range(2):
                    last = nc.tensor.transpose(ps_qk[:, 2 + c], kr[:, c * P:(c + 1) * P], ident)
                last.then_inc(s_qkT, 1)

            def scores(t):
                pe.wait_ge(s_qkE, t + 1)
                for g2 in range(2):
                    nc.tensor.matmul(ps_s[:, g2], g["identb"][:], g["maskb"][:], start=True, stop=False,
                                     skip_group_check=True)
                for g2 in range(2):
                    for b2 in range(2):
                        for ct in range(2):
                            o = ct * 256
                            last = nc.tensor.matmul(ps_s[64 * b2:64 * b2 + 64, g2, o:o + 256],
                                                    qT[64 * g2:64 * g2 + 64, ct, 64 * b2:64 * b2 + 64],
                                                    kbd[64 * g2:64 * g2 + 64, 2 * ct + b2],
                                                    start=False, stop=True, skip_group_check=True)
                last.then_inc(s_sc, 1)

            def probsT(t):
                pe.wait_ge(s_pr, t + 1)
                for q in range(H // 2):
                    last = nc.tensor.transpose(ps_pT[:, q], pr_[:, 2 * q:2 * q + 2].rearrange("p h k -> p (h k)"), ident)
                last.then_inc(s_pT, 1)

            def heads(t):
                pe.wait_ge(s_pTe, t + 1)
                pe.wait_ge(s_vb, t + 1)
                for b2 in range(2):
                    for q in range(H // 2):
                        kvh = 2 * ((q // 2) % 2) + q // 4
                        last = nc.tensor.matmul(pso[64 * b2:64 * b2 + 64, q * 2 * VW:(q + 1) * 2 * VW],
                                                pT[:, q, 64 * b2:64 * b2 + 64], vbd[:, b2, kvh],
                                                start=True, stop=True)
                last.then_inc(s_pv, 1)

            def project(t):
                pe.wait_ge(s_on, t + 1)
                ov = on[:].rearrange("p (c h) d -> p c (h d)", c=2)
                for c in range(2):
                    last = nc.tensor.transpose(ps_oT[:, c * P:(c + 1) * P], ov[:, c], ident)
                last.then_inc(s_oT, 1)
                pe.wait_ge(s_oTe, t + 1)
                for c in range(2):
                    last = nc.tensor.matmul(ps_y[:, 0:C], oT[:, c], g["woutT"][:, c], start=(c == 0), stop=(c == 1))
                last.then_inc(s_y, 1)

            pe.wait_ge(s_v0, 1)
            qkT(0)
            scores(0)
            qkT(1)
            with pe.Fori(0, NT - 2) as t:
                probsT(t)
                scores(t + 1)
                heads(t)
                project(t)
                qkT(t + 2)
            probsT(NT - 2)
            scores(NT - 1)
            heads(NT - 2)
            project(NT - 2)
            probsT(NT - 1)
            heads(NT - 1)
            project(NT - 1)


def split_passes(hi, lo):
    return ((hi[0], hi[1]), (lo[0], hi[1]), (hi[0], lo[1]))


def moe_phase(nc, a, g, sb, pb, sem):
    ident = g["const"][:, C_ID:C_ID + P]
    y = sb("y", [P, TPB, C])
    yhi = sb("yT_hi", [P, CT, BT], F32R)
    ylo = sb("yT_lo", [P, CT, BT], F32R)
    gl = sb("gelu", [P, 2, BT])
    ac = sb("act", [P, 2, BT])
    ahi = sb("act_hi", [P, 2, 2, BT], F32R)
    alo = sb("act_lo", [P, 2, 2, BT], F32R)
    lg = sb("logits", [P, TPB, NE])
    pb_ = sb("router_probs", [P, TPB, NE])
    m4 = sb("router_max", [P, TPB])
    s4 = sb("router_sum", [P, TPB])
    top8 = sb("top8", [P, TPB, 8])
    ix8 = sb("top8_index", [P, TPB, 8], U32)
    ixf = sb("top8_indexf", [P, TPB, 8])
    tw = sb("top_w", [P, TPB, 2])
    c0 = sb("comb0", [P, TPB, NE])
    c1 = sb("comb1", [P, TPB, NE])
    comb = sb("comb", [P, TPB, NE])
    ps_g = [pb(f"ps_gate{f}", [P, BT]) for f in range(2)]
    ps_u = [pb(f"ps_up{f}", [P, BT]) for f in range(2)]
    ps_t = pb("ps_yT", [P, CT, BT])
    ps_d = pb("ps_down", [P, TPB, C])

    s_v = sem("dve_step")
    s_yn, s_yt, s_yh, s_yl = sem("y_normed"), sem("y_transposed"), sem("y_hi"), sem("y_lo")
    s_lg, s_rx, s_re = sem("logits_ready"), sem("router_shifted"), sem("router_exp")
    s_gu, s_gl, s_ac, s_ah, s_al = sem("gate_up_ready"), sem("gelu_ready"), sem("act_ready"), sem("act_hi"), sem("act_lo")
    s_dn, s_mix = sem("down_ready"), sem("mixed")
    s_bn, s_rt, s_pw = sem("bn_ready"), sem("router_step"), sem("router_wait")
    STEPS = 18

    with nc.Block() as block:

        @block.vector
        def _(dve):
            ln_rstd(nc, g, Link(dve, s_v), ROUTER_EPS, float(C) ** -0.5)
            with dve.Fori(0, NBLK) as k:
                n = dve.snap(k + 1)
                for u in range(TPB):
                    t = TPB * k + u
                    nc.vector.tensor_scalar(y[:, u], g["x"][:, t, :], g["mean"][:, bass.ds(t, 1)], g["r"][:, bass.ds(t, 1)],
                                            ALU.subtract, ALU.mult).then_inc(s_yn, 1)
                dve.wait_ge(s_yh, n)
                nc.vector.tensor_tensor(ylo[:], ps_t[:], yhi[:].bitcast(FP32), ALU.subtract).then_inc(s_yl, 1)
                link = Link(dve, s_rt, k * STEPS)
                r2 = bc(g["r2"][:, bass.ds(TPB * k, TPB)], 2, NE)
                dve.wait_ge(s_lg, n)
                link(nc.vector.tensor_tensor(lg[:], ps_d[:, 0, 0:TPB * NE].rearrange("p (u e) -> p u e", e=NE), r2, ALU.mult))
                link(nc.vector.tensor_reduce(m4[:], lg[:], AX.X, ALU.max))
                nc.vector.tensor_tensor(lg[:], lg[:], bc(m4[:], 2, NE), ALU.subtract).then_inc(s_rx, 1)
                dve.wait_ge(s_re, n)
                link(nc.vector.tensor_reduce(s4[:], pb_[:], AX.X, ALU.add))
                link(nc.vector.reciprocal(m4[:], s4[:]))
                link(nc.vector.tensor_tensor(pb_[:], pb_[:], bc(m4[:], 2, NE), ALU.mult))
                dve.sem_inc(s_pw, 1)
                for u in range(TPB):
                    last = nc.vector.max(top8[:, u], pb_[:, u])
                link(last)
                link(nc.vector.tensor_tensor(s4[:], top8[:, :, 0], top8[:, :, 1], ALU.add))
                dve.sem_inc(s_pw, 1)
                for u in range(TPB):
                    last = nc.vector.max_index(ix8[:, u], top8[:, u], pb_[:, u])
                link(last)
                link(nc.vector.tensor_copy(ixf[:], ix8[:]))
                link(nc.vector.tensor_scalar(s4[:], s4[:], 1e-12, None, ALU.max))
                link(nc.vector.reciprocal(m4[:], s4[:]))
                link(nc.vector.tensor_tensor(tw[:], top8[:, :, 0:2], bc(m4[:], 2, 2), ALU.mult))
                iota = bc(g["const"][:, C_IOTA:C_IOTA + NE], 1, TPB)
                for c, j in ((c0, 0), (c1, 1)):
                    link(nc.vector.tensor_tensor(c[:], iota, bc(ixf[:, :, j], 2, NE), ALU.is_equal))
                    link(nc.vector.tensor_tensor(c[:], c[:], bc(tw[:, :, j], 2, NE), ALU.mult))
                link(nc.vector.tensor_tensor(comb[:], c0[:], c1[:], ALU.add))
                link(nc.vector.tensor_tensor(comb[:], comb[:], bc(g["pes"][:], 1, TPB), ALU.mult))
                assert link.n == STEPS, link.n

                def mix(e):
                    for u in range(TPB):
                        t = TPB * k + u
                        i = TPB * e + u
                        if u % 2 == 0:
                            dve.wait_ge(s_dn, 2 * NE * k + (2 * e + u // 2 + 1))
                        if e:
                            dve.wait_ge(s_mix, TPB * NE * k + (i + 1 - TPB))
                        nc.vector.scalar_tensor_tensor(g["x"][:, t, :], ps_d[:, u], comb[:, u, e:e + 1], g["x"][:, t, :],
                                                       ALU.mult, ALU.add).then_inc(s_mix, 1)

                for e in range(NE):
                    for f in range(2):
                        m = dve.snap(2 * NE * k + (2 * e + f + 1))
                        dve.wait_ge(s_gl, m)
                        nc.vector.tensor_tensor(ac[:, f], gl[:, f], ps_u[f][:], ALU.mult).then_inc(s_ac, 1)
                        dve.wait_ge(s_ah, m)
                        nc.vector.tensor_tensor(alo[:, e % 2, f], ac[:, f], ahi[:, e % 2, f].bitcast(FP32), ALU.subtract).then_inc(s_al, 1)
                    if e:
                        mix(e - 1)
                mix(NE - 1)
                for u in range(TPB):
                    t = TPB * k + u
                    dve.wait_ge(s_mix, TPB * NE * k + (TPB * (NE - 1) + u + 1))
                    nc.vector.bn_stats(g["bn"][:, t, :], g["x"][:, t, :]).then_inc(s_bn, 1)
                for u in range(TPB):
                    t = TPB * k + u

        @block.scalar
        def _(act):
            with act.Fori(0, NBLK) as k:
                n = act.snap(k + 1)
                act.wait_ge(s_yt, n)
                nc.scalar.activation(yhi[:], ps_t[:], ACT.Copy).then_inc(s_yh, 1)
                act.wait_ge(s_rx, n)
                nc.scalar.activation(pb_[:], lg[:], ACT.Exp).then_inc(s_re, 1)
                for e in range(NE):
                    for f in range(2):
                        m = act.snap(2 * NE * k + (2 * e + f + 1))
                        act.wait_ge(s_gu, m)
                        nc.scalar.activation(gl[:, f], ps_g[f][:], ACT.Gelu).then_inc(s_gl, 1)
                        act.wait_ge(s_ac, m)
                        nc.scalar.activation(ahi[:, e % 2, f], ac[:, f], ACT.Copy).then_inc(s_ah, 1)

        @block.tensor
        def _(pe):
            whi, wlo = g["whi"], g["wlo"]
            with pe.Fori(0, NBLK) as k:
                n = pe.snap(k + 1)
                for u in range(TPB):
                    pe.wait_ge(s_yn, TPB * k + (u + 1))
                    for c in range(CT):
                        last = nc.tensor.transpose(ps_t[:, c, u * P:(u + 1) * P], y[:, u, c * P:(c + 1) * P], ident)
                last.then_inc(s_yt, 1)
                pe.wait_ge(s_yl, n)
                for u in range(TPB):
                    parts = [(yy, ww) for yy in (yhi, ylo) for ww in (g["gwhi"], g["gwlo"])]
                    for j, (yy, ww) in enumerate(parts):
                        for c in range(CT):
                            last = nc.tensor.matmul(ps_d[:, 0, u * NE:(u + 1) * NE], yy[:, c, u * P:(u + 1) * P], ww[:, c],
                                                    start=(j + c == 0), stop=(j == 3 and c == 1))
                last.then_inc(s_lg, 1)

                def up(e):
                    for f in range(2):
                        if e:
                            pe.wait_ge(s_ac, 2 * NE * k + (2 * (e - 1) + f + 1))
                        for ps, o in ((ps_g[f], f * P), (ps_u[f], ED + f * P)):
                            for j, (w, yy) in enumerate(split_passes((whi, yhi), (wlo, ylo))):
                                for c in range(CT):
                                    last = nc.tensor.matmul(ps[:], w[:, e, c * 512 + o:c * 512 + o + P], yy[:, c],
                                                            start=(j + c == 0), stop=(j == 2 and c == 1))
                        last.then_inc(s_gu, 1)

                def down(e):
                    pe.wait_ge(s_al, 2 * NE * k + 2 * (e + 1))
                    for u in range(TPB):
                        if e:
                            pe.wait_ge(s_mix, TPB * NE * k + (TPB * (e - 1) + 2 * (u // 2) + 2))
                        else:
                            pe.wait_ge(s_rx, n)
                        for j, (w, aa) in enumerate(split_passes((whi, ahi), (wlo, alo))):
                            for f in range(2):
                                last = nc.tensor.matmul(ps_d[:, u], aa[:, e % 2, f, u * P:(u + 1) * P],
                                                        w[:, e, 1024 + f * C:1024 + (f + 1) * C],
                                                        start=(j + f == 0), stop=(j == 2 and f == 1))
                        if u % 2:
                            last.then_inc(s_dn, 1)

                up(0)
                for e in range(NE):
                    if e + 1 < NE:
                        up(e + 1)
                    down(e)


def attn1_phase(nc, a, g, sb, pb, sem):
    ident = g["const"][:, C_ID:C_ID + P]
    NP = H // 2
    y = sb("y", [P, TPB, C])
    yhi = sb("yT_hi", [P, CT, BT], F32R)
    ylo = sb("yT_lo", [P, CT, BT], F32R)
    qt = sb("q_tilT", [P, NP, BT])
    kvbd = [sb(f"kv_blockdiag{u}", [P, 2, P]) for u in range(2)]
    kvbT = sb("kv_blockdiagT", [P, 2, P])
    z = sb("probs", [P, H, S])
    pT = sb("probsT", [P, NP, P])
    cT = sb("ctxT", [P, NP, 2, S])
    mx = sb("score_max", [P, H])
    sm = sb("prob_sum", [P, H])
    rec = sb("sum_recip", [P, H])
    raw = sb("ffn_raw", [P, 3 * 1536])
    QN = 3 * 1536 // NBLK
    p2 = sb("power_of_two", [P, QN])
    rnd = sb("rounded", [P, QN])
    ps_s = pb("ps_scores", [P, 2, 512])
    ps_pT = pb("ps_probsT", [P, NP, P])
    ps_c = pb("ps_ctxT", [P, 2, 512])
    ps_y = pb("ps_y", [P, 512])
    ps_k = pb("ps_kvT", [P, 512])

    s_v, s_raw, s_q8 = sem("dve_step"), sem("raw_loaded"), sem("fp8_step")
    s_yn, s_yt, s_yh, s_yl = sem("y_normed"), sem("y_transposed"), sem("y_hi"), sem("y_lo")
    s_q, s_qe = sem("q_ready"), sem("q_in_sbuf")
    s_kb, s_kT, s_kTe = sem("kv_ready"), sem("kv_transposed"), sem("kvT_in_sbuf")
    s_sc, s_mx, s_sh, s_ex, s_sum, s_rec, s_pr = (sem("scores_ready"), sem("max_ready"), sem("scores_shifted"),
                                                  sem("exp_ready"), sem("sum_ready"), sem("recip_ready"), sem("probs_ready"))
    s_pT, s_pTe, s_c, s_ce, s_y = (sem("probs_transposed"), sem("probsT_in_sbuf"), sem("ctx_ready"),
                                   sem("ctx_in_sbuf"), sem("y_ready"))
    s_x, s_bn = sem("x_updated"), sem("bn_ready")
    QSTEPS = 6

    with nc.Block() as block:

        @block.sync
        def _(sp):
            for j, (name, t) in enumerate((("L1_ffn_gate_w", 2), ("L1_ffn_up_w", 2), ("L1_ffn_down_w", 6))):
                dst = raw[:, j * 1536:(j + 1) * 1536].rearrange("p (t n) -> p t n", t=t)
                sp.dma_start(dst, a[name].rearrange("(t p) n -> p t n", p=P)).then_inc(s_raw, 16)

        @block.gpsimd
        def _(pool):
            half = g["const"][:, C_HALF:C_HALF + 2]

            def keys(t, u, free):
                if free is not None:
                    pool.wait_ge(s_c, free)
                src = g["kvr"][:, bass.ds(2 * t, 2), :]
                nc.gpsimd.tensor_tensor(kvbd[u][:].rearrange("p b (h d) -> p b h d", h=2), bc(src, 2, 2),
                                        bc(bc(half, 1, 2), 3, DCTX), ALU.mult).then_inc(s_kb, 1)

            for u in range(2):
                keys(u, u, None)
            with pool.Fori(1, NT // 2) as i:
                for u in range(2):
                    keys(2 * i + u, u, 2 * i + (u - 1))

        @block.vector
        def _(dve):
            ln_rstd(nc, g, Link(dve, s_v))
            dve.wait_ge(s_raw, 48)

            def shift(t):
                n = dve.snap(t + 1)
                dve.wait_ge(s_sc, n)
                sv = ps_s[:].rearrange("p b (h k) -> p (b h) k", k=S)
                nc.vector.tensor_reduce(mx[:], sv, AX.X, ALU.max).then_inc(s_mx, 1)
                dve.wait_ge(s_mx, n)
                nc.vector.tensor_tensor(z[:], sv, bc(mx[:], 2, S), ALU.subtract).then_inc(s_sh, 1)

            def normalise(t):
                n = dve.snap(t + 1)
                dve.wait_ge(s_ex, n)
                nc.vector.tensor_reduce(sm[:], z[:], AX.X, ALU.add).then_inc(s_sum, 1)
                dve.wait_ge(s_sum, n)
                nc.vector.reciprocal(rec[:], sm[:]).then_inc(s_rec, 1)
                dve.wait_ge(s_rec, n)
                nc.vector.tensor_tensor(z[:], z[:], bc(rec[:], 2, S), ALU.mult).then_inc(s_pr, 1)

            def residual(t):
                n = dve.snap(t + 1)
                dve.wait_ge(s_y, n)
                nc.vector.scalar_tensor_tensor(g["x"][:, t, :], ps_y[:, 0:C], g["tg"][:, 1:2], g["x"][:, t, :],
                                               ALU.mult, ALU.add).then_inc(s_x, 1)
                dve.wait_ge(s_x, n)
                nc.vector.bn_stats(g["bn"][:, t, :], g["x"][:, t, :]).then_inc(s_bn, 1)

            with dve.Fori(0, NBLK) as k:
                n = dve.snap(k + 1)
                for u in range(TPB):
                    t = TPB * k + u
                    nc.vector.tensor_scalar(y[:, u], g["x"][:, t, :], g["mean"][:, bass.ds(t, 1)], g["r"][:, bass.ds(t, 1)],
                                            ALU.subtract, ALU.mult).then_inc(s_yn, 1)
                dve.wait_ge(s_yh, n)
                nc.vector.tensor_tensor(ylo[:], ps_c[:], yhi[:].bitcast(FP32), ALU.subtract).then_inc(s_yl, 1)
                link = Link(dve, s_q8, k * QSTEPS)
                w = raw[:, bass.ds(k * QN, QN)]
                link(nc.vector.tensor_scalar(p2[:].bitcast(I32), w.bitcast(I32), 0x7F800000, None, ALU.bitwise_and))
                link(nc.vector.tensor_scalar(p2[:], p2[:], 2.0 ** -6, 1.5 * 2.0 ** 20, ALU.max, ALU.mult))
                link(nc.vector.tensor_tensor(rnd[:], w, p2[:], ALU.add))
                link(nc.vector.tensor_tensor(rnd[:], rnd[:], p2[:], ALU.subtract))
                link(nc.vector.tensor_scalar(p2[:], rnd[:], OVERFLOW, 0.0, ALU.mult, ALU.mult))
                link(nc.vector.tensor_tensor(g["wq8"][:, bass.ds(k * QN, QN)], rnd[:], p2[:], ALU.add))
                assert link.n == QSTEPS
                for u in range(TPB):
                    t = TPB * k + u
                    shift(t)
                    normalise(t)
                    if u:
                        residual(t - 1)
                residual(TPB * k + (TPB - 1))

        @block.scalar
        def _(act):
            def probsT(m):
                act.wait_ge(s_pT, m)
                nc.scalar.activation(pT[:], ps_pT[:], ACT.Copy).then_inc(s_pTe, 1)

            with act.Fori(0, NBLK) as k:
                n = act.snap(k + 1)
                act.wait_ge(s_yt, n)
                nc.scalar.activation(yhi[:], ps_c[:], ACT.Copy).then_inc(s_yh, 1)
                for p in range(NP):
                    act.wait_ge(s_q, NP * k + (p + 1))
                    nc.scalar.activation(qt[:, p], ps_c[:, p % 2], ACT.Copy).then_inc(s_qe, 1)
                for u in range(TPB):
                    m = act.snap(TPB * k + (u + 1))
                    act.wait_ge(s_kT, m)
                    nc.scalar.activation(kvbT[:], ps_k[:, 0:2 * P], ACT.Copy).then_inc(s_kTe, 1)
                    if u:
                        probsT(TPB * k + u)
                    act.wait_ge(s_sh, m)
                    nc.scalar.activation(z[:], z[:], ACT.Exp).then_inc(s_ex, 1)
                    if u:
                        act.wait_ge(s_c, TPB * k + u)
                        nc.scalar.activation(cT[:].rearrange("p q b s -> p b q s"), ps_c[:].rearrange("p b (q s) -> p b q s", q=NP), ACT.Copy).then_inc(s_ce, 1)
                probsT(TPB * k + TPB)
                act.wait_ge(s_c, TPB * k + TPB)
                nc.scalar.activation(cT[:].rearrange("p q b s -> p b q s"), ps_c[:].rearrange("p b (q s) -> p b q s", q=NP), ACT.Copy).then_inc(s_ce, 1)

        @block.tensor
        def _(pe):
            def scores(k, u):
                t = TPB * k + u
                pe.wait_ge(s_kb, t + 1)
                for b2 in range(2):
                    last = nc.tensor.transpose(ps_k[:, b2 * P:(b2 + 1) * P], kvbd[u % 2][:, b2], ident)
                last.then_inc(s_kT, 1)
                pe.wait_ge(s_kTe, t + 1)
                if u == 0:
                    pe.wait_ge(s_qe, NP * (k + 1))
                for p in range(NP):
                    for b2 in range(2):
                        c = u * P + 64 * b2
                        last = nc.tensor.matmul(ps_s[64 * b2:64 * b2 + 64, p // 4, (p % 4) * P:(p % 4 + 1) * P],
                                                qt[:, p, c:c + 64], kvbT[:, b2], start=True, stop=True)
                last.then_inc(s_sc, 1)

            def probsT(t):
                pe.wait_ge(s_pr, t + 1)
                for p in range(NP):
                    last = nc.tensor.transpose(ps_pT[:, p], z[:, 2 * p:2 * p + 2].rearrange("p h k -> p (h k)"), ident)
                last.then_inc(s_pT, 1)

            def ctxT(t, u):
                pe.wait_ge(s_pTe, t + 1)
                for b2 in range(2):
                    last = nc.tensor.matmul(ps_c[:, b2], kvbd[u % 2][:, b2], pT[:, :, 64 * b2:64 * b2 + 64],
                                            start=True, stop=True)
                last.then_inc(s_c, 1)

            def project(t, u):
                pe.wait_ge(s_ce, t + 1)
                if u:
                    pe.wait_ge(s_x, t)
                for p in range(NP):
                    last = nc.tensor.matmul(ps_y[:, 0:C], cT[:, p].rearrange("p b s -> p (b s)"), g["pm"][:, p], start=(p == 0), stop=(p == NP - 1))
                last.then_inc(s_y, 1)

            with pe.Fori(0, NBLK) as k:
                n = pe.snap(k + 1)
                for u in range(TPB):
                    pe.wait_ge(s_yn, TPB * k + (u + 1))
                    for c in range(CT):
                        last = nc.tensor.transpose(ps_c[:, c, u * P:(u + 1) * P], y[:, u, c * P:(c + 1) * P], ident)
                last.then_inc(s_yt, 1)
                pe.wait_ge(s_yl, n)
                for p in range(NP):
                    if p >= 2:
                        pe.wait_ge(s_qe, NP * k + (p - 1))
                    parts = split_passes((g["mhi"], yhi), (g["mlo"], ylo))
                    for j, (w, yy) in enumerate(parts):
                        for c in range(CT):
                            last = nc.tensor.matmul(ps_c[:, p % 2], w[:, c, p * P:(p + 1) * P], yy[:, c],
                                                    start=(j + c == 0), stop=(j == 2 and c == 1))
                    last.then_inc(s_q, 1)
                scores(k, 0)
                for u in range(TPB):
                    t = TPB * k + u
                    probsT(t)
                    if u + 1 < TPB:
                        scores(k, u + 1)
                    ctxT(t, u)
                    project(t, u)


def ffn_phase(nc, a, g, out, sb, pb, sem):
    ident = g["const"][:, C_ID:C_ID + P]
    wg, wu, wd = (g["wq8"][:, j * 1536:(j + 1) * 1536] for j in range(3))
    y = sb("y", [P, TPB, C])
    yhi = sb("yT_hi", [P, CT, BT], F32R)
    ylo = sb("yT_lo", [P, CT, BT], F32R)
    sg = sb("silu", [P, 2, BT])
    ac = sb("act", [P, 2, BT])
    ahi = sb("act_hi", [P, FT, BT], F32R)
    alo = sb("act_lo", [P, FT, BT], F32R)
    ot = sb("scaled", [P, TPB, C])
    ps_g = [pb(f"ps_gate{f}", [P, BT]) for f in range(2)]
    ps_u = [pb(f"ps_up{f}", [P, BT]) for f in range(2)]
    ps_t = pb("ps_yT", [P, CT, BT])
    ps_d = pb("ps_down", [P, TPB, C])
    s_v = sem("dve_step")
    s_yn, s_yt, s_yh, s_yl = sem("y_normed"), sem("y_transposed"), sem("y_hi"), sem("y_lo")
    s_gu, s_sg, s_ac, s_ah, s_al = sem("gate_up_ready"), sem("silu_ready"), sem("act_ready"), sem("act_hi"), sem("act_lo")
    s_dn, s_sc, s_x, s_out = sem("down_ready"), sem("scaled"), sem("x_final"), sem("stored")

    with nc.Block() as block:

        @block.sync
        def _(sp):
            ov = out.rearrange("(t b) s c -> t (b s) c", b=2)
            with sp.Fori(0, NT) as t:
                sp.wait_ge(s_x, t + 1)
                sp.dma_start(ov[bass.ds(t, 1)].rearrange("t p c -> (t p) c"), g["x"][:, t, :]).then_inc(s_out, 16)
            sp.wait_ge(s_out, 16 * NT)

        @block.vector
        def _(dve):
            ln_rstd(nc, g, Link(dve, s_v))
            with dve.Fori(0, NBLK) as k:
                n = dve.snap(k + 1)
                for u in range(TPB):
                    t = TPB * k + u
                    nc.vector.tensor_scalar(y[:, u], g["x"][:, t, :], g["mean"][:, bass.ds(t, 1)], g["r"][:, bass.ds(t, 1)],
                                            ALU.subtract, ALU.mult).then_inc(s_yn, 1)
                dve.wait_ge(s_yh, n)
                nc.vector.tensor_tensor(ylo[:], ps_t[:], yhi[:].bitcast(FP32), ALU.subtract).then_inc(s_yl, 1)
                for f in range(FT):
                    m = dve.snap(FT * k + (f + 1))
                    dve.wait_ge(s_sg, m)
                    nc.vector.scalar_tensor_tensor(ac[:, f % 2], ps_u[f % 2][:], g["fus"][:, f:f + 1], sg[:, f % 2],
                                                   ALU.mult, ALU.mult).then_inc(s_ac, 1)
                    dve.wait_ge(s_ah, m)
                    nc.vector.tensor_tensor(alo[:, f], ac[:, f % 2], ahi[:, f].bitcast(FP32), ALU.subtract).then_inc(s_al, 1)
                for u in range(TPB):
                    t = TPB * k + u
                    m = dve.snap(TPB * k + (u + 1))
                    if u % 2 == 0:
                        dve.wait_ge(s_dn, 2 * k + (u // 2 + 1))
                    nc.vector.tensor_tensor(ot[:, u], ps_d[:, u], g["dsg"][:], ALU.mult).then_inc(s_sc, 1)
                    dve.wait_ge(s_sc, m)
                    nc.vector.tensor_tensor(g["x"][:, t, :], g["x"][:, t, :], ot[:, u], ALU.add).then_inc(s_x, 1)

        @block.scalar
        def _(act):
            with act.Fori(0, NBLK) as k:
                n = act.snap(k + 1)
                act.wait_ge(s_yt, n)
                nc.scalar.activation(yhi[:], ps_t[:], ACT.Copy).then_inc(s_yh, 1)
                for f in range(FT):
                    m = act.snap(FT * k + (f + 1))
                    act.wait_ge(s_gu, m)
                    nc.scalar.activation(sg[:, f % 2], ps_g[f % 2][:], ACT.Silu, scale=g["fgs"][:, f:f + 1]).then_inc(s_sg, 1)
                    act.wait_ge(s_ac, m)
                    nc.scalar.activation(ahi[:, f], ac[:, f % 2], ACT.Copy).then_inc(s_ah, 1)

        @block.tensor
        def _(pe):
            with pe.Fori(0, NBLK) as k:
                n = pe.snap(k + 1)
                for u in range(TPB):
                    pe.wait_ge(s_yn, TPB * k + (u + 1))
                    for c in range(CT):
                        last = nc.tensor.transpose(ps_t[:, c, u * P:(u + 1) * P], y[:, u, c * P:(c + 1) * P], ident)
                last.then_inc(s_yt, 1)
                pe.wait_ge(s_yl, n)
                for f in range(FT):
                    if f >= 2:
                        pe.wait_ge(s_ac, FT * k + (f - 1))
                    for ps, w in ((ps_g[f % 2], wg), (ps_u[f % 2], wu)):
                        for j, yy in enumerate((yhi, ylo)):
                            for c in range(CT):
                                last = nc.tensor.matmul(ps[:], w[:, c * FI + f * P:c * FI + (f + 1) * P], yy[:, c],
                                                        start=(j + c == 0), stop=(j + c == 2))
                    last.then_inc(s_gu, 1)
                pe.wait_ge(s_al, FT * (k + 1))
                for u in range(TPB):
                    for f in range(FT):
                        for j, aa in enumerate((ahi, alo)):
                            last = nc.tensor.matmul(ps_d[:, u], aa[:, f, u * P:(u + 1) * P], wd[:, f * C:(f + 1) * C],
                                                    start=(j + f == 0), stop=(j + f == FT))
                    if u % 2:
                        last.then_inc(s_dn, 1)


OVERFLOW = 3.4028234663852886e38 / FP8_EDGE


_INS = ['x', 'ctx_512', 'g_xattn', 'g_ffn', 'L0_xattn_q_norm_w', 'L0_xattn_k_norm_w', 'L0_xattn_w_out',
        'L0_ffn_router_scale', 'L0_ffn_gate_w', 'L0_ffn_gate_up', 'L0_ffn_down', 'L0_ffn_per_expert_scale',
        'L1_xattn_Wq', 'L1_xattn_w_kc_q', 'L1_xattn_w_kc_kv', 'L1_xattn_W_qr', 'L1_xattn_W_kr', 'L1_xattn_Wo',
        'L1_ffn_gate_w', 'L1_ffn_up_w', 'L1_ffn_down_w', 'L1_ffn_gate_scale', 'L1_ffn_up_scale', 'L1_ffn_down_scale']


def constants():
    import numpy as np

    c = np.zeros((P, C_END), np.float32)
    p = np.arange(P)
    c[:, C_ID:C_ID + P] = np.eye(P, dtype=np.float32)
    causal = np.arange(S)[None, :] > (p % S)[:, None]
    c[:, C_MASK:C_MASK + 512] = np.tile(np.where(causal, np.float32(-1e30), np.float32(0)), (1, 8))
    c[p, C_NSEL + (p // HD) % 4] = 1
    c[p, C_HALF + p // S] = 1
    pos = np.arange(S, dtype=np.float32)

    def table(dim, order):
        inv = (np.float32(1) / np.float32(10000.0) ** (np.arange(0, dim, 2, dtype=np.float32) / np.float32(dim)))
        f = pos[:, None] * inv.astype(np.float32)[None, :]
        cos, sin = np.cos(f)[:, order], np.sin(f)[:, order]
        sin[:, :dim // 2] = -sin[:, :dim // 2]
        return np.tile(cos, (2, 1)), np.tile(sin, (2, 1))

    c[:, C_COS0:C_COS0 + HD], c[:, C_SIN0:C_SIN0 + HD] = table(HD, np.tile(np.arange(HD // 2), 2))
    c[:, C_COS1:C_COS1 + DCTX], c[:, C_SIN1:C_SIN1 + DCTX] = table(DCTX, np.repeat(np.arange(DCTX // 2), 2))
    c[:, C_IOTA:C_IOTA + NE] = np.arange(NE)
    return c


def kernel(**inputs):
    import numpy as _np
    import concourse.bacc as _bacc
    from concourse import mybir as _mybir
    from concourse.bass_utils import run_bass_kernel_spmd as _run

    nc = _bacc.Bacc("TRN2", target_bir_lowering=False, num_devices=1)
    arrays, aps = {}, {}
    for name in _INS + ["const"]:
        v = constants() if name == "const" else _np.ascontiguousarray(inputs[name])
        arrays[f"in_{name}_dram"] = v
        aps[name] = nc.dram_tensor(f"in_{name}_dram", v.shape, _mybir.dt.from_np(v.dtype), kind="ExternalInput").ap()
    out = nc.dram_tensor("out_0_dram", (B, S, C), FP32, kind="ExternalOutput").ap()
    stack_kernel(nc, aps, out)
    r = _run(nc, [arrays], core_ids=[0])
    return r.results[0]["out_0_dram"]
```

```python
import concourse.bass as bass
from concourse import mybir
from contextlib import ExitStack

FP32 = mybir.dt.float32
F32R = mybir.dt.float32r
BF16 = mybir.dt.bfloat16
I32 = mybir.dt.int32
U32 = mybir.dt.uint32
ALU = mybir.AluOpType
ACT = mybir.ActivationFunctionType
AX = mybir.AxisListType

B, S, C, DCTX = 32, 64, 256, 64
P = 128
NT = B * S // P
NBLK, TPB = NT // 4, 4
BT = TPB * P
CT = C // P
H, HD, KVH = 16, 16, 4
NE, ED = 8, 256
KD, DCQ, R = 128, 192, 64
FI, FT = 768, 768 // 128
GH = 4
LN_EPS, RMS_EPS, ROUTER_EPS = 1e-5, 1e-5, 1e-6
FP8_EDGE = 464.0

C_ID, C_NSEL, C_COS0, C_SIN0, C_COS1, C_SIN1, C_IOTA, C_HALF, C_MASK = 0, 128, 132, 148, 164, 228, 292, 300, 302
C_END = C_MASK + 512


def bc(ap, axis, n):
    shape = list(ap.shape)
    shape.insert(axis, n)
    return ap.unsqueeze(axis).broadcast_to(shape)


class Link:

    def __init__(self, eng, sem, base=0):
        self.eng, self.sem, self.base, self.n = eng, sem, base, 0

    def __call__(self, ins):
        ins.then_inc(self.sem, 1)
        self.n += 1
        self.eng.wait_ge(self.sem, self.base + self.n)


def rsqrt(nc, link, y, v, tmp):
    link(nc.vector.tensor_scalar(tmp.bitcast(I32), v.bitcast(I32), 1, None, ALU.logical_shift_right))
    link(nc.vector.tensor_scalar(y.bitcast(I32), tmp.bitcast(I32), -1.0, float(0x5F3759DF), ALU.mult, ALU.add))
    for _ in range(3):
        link(nc.vector.tensor_tensor(tmp, v, y, ALU.mult))
        link(nc.vector.tensor_tensor(tmp, tmp, y, ALU.mult))
        link(nc.vector.tensor_scalar(tmp, tmp, -0.5, 1.5, ALU.mult, ALU.add))
        link(nc.vector.tensor_tensor(y, y, tmp, ALU.mult))


def split_passes(hi, lo):
    return ((hi[0], hi[1]), (lo[0], hi[1]), (hi[0], lo[1]))


def ln_rstd(nc, g, link, second_eps=None):
    bn, mean, var, d = g["bn"], g["mean"][:], g["var"][:], g["ta"][:, 0]
    link(nc.vector.tensor_tensor(d, bn[:, :, 1], bn[:, :, 4], ALU.subtract))
    link(nc.vector.tensor_tensor(var, bn[:, :, 2], bn[:, :, 5], ALU.add))
    nc.vector.tensor_tensor(mean, bn[:, :, 1], bn[:, :, 4], ALU.add)
    link(nc.vector.tensor_tensor(d, d, d, ALU.mult))
    nc.vector.tensor_scalar(mean, mean, 0.5, None, ALU.mult)
    link(nc.vector.tensor_scalar(var, var, 1.0 / C, None, ALU.mult))
    link(nc.vector.scalar_tensor_tensor(var, d, 0.25, var, ALU.mult, ALU.add))
    v = g["ta"]
    if second_eps is None:
        link(nc.vector.tensor_scalar(v[:, 0], var, LN_EPS, None, ALU.add))
        rsqrt(nc, link, g["r"][:, 0], v[:, 0], g["tb"][:, 0])
    else:
        nc.vector.tensor_scalar(v[:, 0], var, LN_EPS, None, ALU.add)
        link(nc.vector.tensor_scalar(v[:, 1], var, 1.0 + second_eps, LN_EPS * second_eps, ALU.mult, ALU.add))
        rsqrt(nc, link, g["r"][:], v[:], g["tb"][:])
        link(nc.vector.tensor_tensor(v[:, 0], v[:, 0], g["r"][:, 0], ALU.mult))
        link(nc.vector.tensor_tensor(g["r2"][:], v[:, 0], g["r"][:, 1], ALU.mult))


def stack_kernel(nc, a, out):
    top = ExitStack()

    def scope(stack, phase=""):
        def sb(name, shape, dt=FP32):
            return stack.enter_context(nc.sbuf_tensor(phase + name, shape, dt))

        def pb(name, shape, dt=FP32):
            return stack.enter_context(nc.psum_tensor(phase + name, shape, dt))

        def sem(name):
            return stack.enter_context(nc.semaphore(phase + name))

        return sb, pb, sem

    with top:
        sb, _, _ = scope(top)
        g = {
            "x": sb("x_res", [P, NT, C]),
            "const": sb("const", [P, C_MASK]),
            "kvr": sb("kv_roped_dup", [P, B, DCTX]),
            "mhi": sb("m_hi", [P, CT, H * DCTX], F32R),
            "mlo": sb("m_lo", [P, CT, H * DCTX], F32R),
            "pm": sb("p_out", [P, H // 2, C]),
            "tg": sb("tanh_gates", [P, 4]),
            "gwhi": sb("router_hi", [P, CT, NE], F32R),
            "gwlo": sb("router_lo", [P, CT, NE], F32R),
            "pes": sb("expert_scale", [P, NE]),
            "fgs": sb("ffn_gate_scale", [P, FT]),
            "fus": sb("ffn_up_scale", [P, FT]),
            "dsg": sb("ffn_down_scale", [P, C]),
            "bn": sb("bn_stats", [P, NT, 6]),
            "mean": sb("mean", [P, NT]),
            "var": sb("variance", [P, NT]),
            "r": sb("rstd", [P, 2, NT]),
            "r2": sb("second_rstd", [P, NT]),
            "ta": sb("small_a", [P, 2, NT]),
            "tb": sb("small_b", [P, 2, NT]),
        }
        with ExitStack() as es:
            sbm, _, _ = scope(es)
            g["whi"] = sbm("moe_hi", [P, NE, 1536], F32R)
            g["wlo"] = sbm("moe_lo", [P, NE, 1536], F32R)
            with ExitStack() as es0:
                sb0, _, _ = scope(es0)
                g["identb"] = sb0("identb", [P, P], BF16)
                g["maskb"] = sb0("maskb", [P, 512], BF16)
                g["kr"] = sb0("k_roped", [P, NT, DCTX])
                g["ctxdup"] = sb0("ctxdup", [P, B, DCTX])
                g["woutT"] = sb0("woutT", [P, 2, C])
                g["cqw"] = sb0("cos_qw", [P, C])
                g["sqw"] = sb0("sin_qw", [P, C])
                with ExitStack() as es2:
                    setup_phase(nc, a, g, *scope(es2, "setup_"))
                with ExitStack() as es2:
                    attn0_phase(nc, a, g, *scope(es2, "attn0_"))
            with ExitStack() as es2:
                moe_phase(nc, a, g, *scope(es2, "moe_"))
        g["wq8"] = sb("ffn_w", [P, 3 * 1536], F32R)
        with ExitStack() as es:
            attn1_phase(nc, a, g, *scope(es, "attn1_"))
        with ExitStack() as es:
            ffn_phase(nc, a, g, out, *scope(es, "ffn_"))


def setup_phase(nc, a, g, sb, pb, sem):
    ident = g["const"][:, C_ID:C_ID + P]
    ctx = sb("ctx_tok", [P, NT, DCTX])
    kn = sb("k_normed", [P, NT, DCTX])
    rk = sb("k_rstd", [P, NT])
    ms = sb("k_mean_sq", [P, NT])
    tmp = sb("newton", [P, NT])
    kt1 = sb("k_cos", [P, NT, DCTX])
    kt2 = sb("k_sin", [P, NT, DCTX])
    kv1 = sb("kv_cos", [P, B, DCTX])
    qw = sb("q_norm_b", [P, C])
    kw = sb("k_norm_b", [P, DCTX])
    ckw = sb("cos_kw", [P, DCTX])
    skw = sb("sin_kw", [P, DCTX])
    wout = sb("w_out", [P, 2, C])
    graw = sb("gates_raw", [P, 4])
    gw = sb("router_w", [P, CT, NE])
    rsc = sb("router_scale", [P, CT])
    mask = sb("mask", [P, 512])
    ps_w = pb("ps_woutT", [P, 512])

    s_const, s_ctx, s_dup = sem("const_in"), sem("ctx_in"), sem("ctxdup_in")
    s_x, s_mask = [sem(f"x_in{q}") for q in range(4)], sem("mask_in")
    s_nw, s_wo, s_small = sem("norm_w_in"), sem("w_out_in"), sem("small_in")
    s_wt, s_v, s_g, s_tg = sem("woutT_ps"), sem("dve_step"), sem("pool_step"), sem("gates_ready")

    with nc.Block() as block:

        @block.sync
        def _(sp):
            sp.dma_start(ctx[:], a["ctx_512"].rearrange("(t b) s c -> (b s) t c", b=2)).then_inc(s_ctx, 16)
            xv = a["x"].rearrange("(t b) s c -> (b s) t c", b=2)
            for q in range(4):
                sp.dma_start(g["x"][:, 4 * q:4 * q + 4], xv[:, 4 * q:4 * q + 4]).then_inc(s_x[q], 16)
            for d in range(2):
                sp.dma_start(g["ctxdup"][64 * d:64 * d + 64], a["ctx_512"].rearrange("b k c -> k b c")).then_inc(s_dup, 16)

        @block.scalar
        def _(act):
            act.dma_start(g["const"][:], a["const"][:, 0:C_MASK]).then_inc(s_const, 16)
            act.dma_start(qw[:], a["L0_xattn_q_norm_w"].partition_broadcast(P)).then_inc(s_nw, 16)
            act.dma_start(kw[:], a["L0_xattn_k_norm_w"].partition_broadcast(P)).then_inc(s_nw, 16)
            wv = a["L0_xattn_w_out"].rearrange("(t o) (ct g2 nd) -> t g2 o ct nd", o=P, ct=2, g2=2)
            for ot in range(2):
                for g2 in range(2):
                    dst = wout[:, ot, g2 * P:(g2 + 1) * P].rearrange("p (ct nd) -> p ct nd", ct=2)
                    act.dma_start(dst, wv[ot, g2]).then_inc(s_wo, 16)
            act.dma_start(mask[:], a["const"][:, C_MASK:C_END]).then_inc(s_mask, 16)
            act.dma_start(graw[:, 0:2], a["g_xattn"].partition_broadcast(P)).then_inc(s_small, 16)
            act.dma_start(graw[:, 2:4], a["g_ffn"].partition_broadcast(P)).then_inc(s_small, 16)
            act.dma_start(gw[:], a["L0_ffn_gate_w"].rearrange("(t p) e -> p t e", p=P)).then_inc(s_small, 16)
            act.dma_start(rsc[:], a["L0_ffn_router_scale"].rearrange("(t p) -> p t", p=P),
                          allow_slow_non_contiguous=True).then_inc(s_small, 16)
            act.dma_start(g["pes"][:], a["L0_ffn_per_expert_scale"].partition_broadcast(P)).then_inc(s_small, 16)
            act.dma_start(g["fgs"][:], a["L1_ffn_gate_scale"].rearrange("(t p) -> p t", p=P),
                          allow_slow_non_contiguous=True).then_inc(s_small, 16)
            act.dma_start(g["fus"][:], a["L1_ffn_up_scale"].rearrange("(t p) -> p t", p=P),
                          allow_slow_non_contiguous=True).then_inc(s_small, 16)
            act.dma_start(g["dsg"][:], a["L1_ffn_down_scale"].partition_broadcast(P)).then_inc(s_small, 16)
            act.wait_ge(s_wt, 1)
            act.activation(g["woutT"][:], ps_w[:], ACT.Copy)
            act.wait_ge(s_small, 8 * 16)
            act.activation(g["tg"][:], graw[:], ACT.Tanh).then_inc(s_tg, 1)

        @block.tensor
        def _(pe):
            pe.wait_ge(s_const, 16)
            pe.wait_ge(s_wo, 4 * 16)
            for g2 in range(2):
                for ot in range(2):
                    last = nc.tensor.transpose(ps_w[:, (2 * g2 + ot) * P:(2 * g2 + ot + 1) * P],
                                               wout[:, ot, g2 * P:(g2 + 1) * P], ident)
            last.then_inc(s_wt, 1)

        @block.vector
        def _(dve):
            link = Link(dve, s_v)
            dve.wait_ge(s_ctx, 16)
            link(nc.vector.tensor_tensor(kn[:], ctx[:], ctx[:], ALU.mult))
            link(nc.vector.tensor_reduce(ms[:], kn[:], AX.X, ALU.add))
            link(nc.vector.tensor_scalar(ms[:], ms[:], 1.0 / DCTX, RMS_EPS, ALU.mult, ALU.add))
            rsqrt(nc, link, rk[:], ms[:], tmp[:])
            dve.wait_ge(s_const, 16)
            dve.wait_ge(s_nw, 32)
            cos0, sin0 = g["const"][:, C_COS0:C_COS0 + HD], g["const"][:, C_SIN0:C_SIN0 + HD]
            for w, nh, cw, sw in ((qw, H, g["cqw"], g["sqw"]), (kw, KVH, ckw, skw)):
                wv, cv, sv = (t[:].rearrange("p (h d) -> p h d", d=HD) for t in (w, cw, sw))
                nc.vector.tensor_tensor(cv, wv, bc(cos0, 1, nh), ALU.mult)
                nc.vector.tensor_tensor(sv[:, :, 0:8], wv[:, :, 8:16], bc(sin0[:, 0:8], 1, nh), ALU.mult)
                link(nc.vector.tensor_tensor(sv[:, :, 8:16], wv[:, :, 0:8], bc(sin0[:, 8:16], 1, nh), ALU.mult))
            link(nc.vector.tensor_tensor(kn[:], ctx[:], bc(rk[:], 2, DCTX), ALU.mult))
            nc.vector.tensor_tensor(kt1[:], kn[:], bc(ckw[:], 1, NT), ALU.mult)
            k4, s4 = (v.rearrange("p t (h d) -> p t h d", d=HD) for v in (kn[:], kt2[:]))
            w4 = bc(skw[:].rearrange("p (h d) -> p h d", d=HD), 1, NT)
            nc.vector.tensor_tensor(s4[:, :, :, 0:8], k4[:, :, :, 8:16], w4[:, :, :, 0:8], ALU.mult)
            link(nc.vector.tensor_tensor(s4[:, :, :, 8:16], k4[:, :, :, 0:8], w4[:, :, :, 8:16], ALU.mult))
            link(nc.vector.tensor_tensor(g["kr"][:], kt1[:], kt2[:], ALU.add))
            nc.vector.tensor_copy(g["identb"][:], ident)
            dve.wait_ge(s_mask, 16)
            nc.vector.tensor_copy(g["maskb"][:], mask[:])
            for q in range(4):
                dve.wait_ge(s_x[q], 16)
                for t in range(4 * q, 4 * q + 4):
                    last = nc.vector.bn_stats(g["bn"][:, t, :], g["x"][:, t, :])
            dve.wait_ge(s_small, 8 * 16)
            link(last)
            for t in range(CT):
                nc.vector.tensor_scalar(gw[:, t], gw[:, t], rsc[:, t:t + 1], float(C) ** -0.5,
                                        ALU.mult, ALU.mult).then_inc(s_v, 1)
            link.n += CT
            dve.wait_ge(s_v, link.n)
            link(nc.vector.tensor_copy(g["gwhi"][:], gw[:]))
            nc.vector.tensor_tensor(g["gwlo"][:], gw[:], g["gwhi"][:].bitcast(FP32), ALU.subtract)
            dve.wait_ge(s_tg, 1)
            nc.vector.tensor_scalar(g["pes"][:], g["pes"][:], g["tg"][:, 2:3], None, ALU.mult)
            nc.vector.tensor_scalar(g["dsg"][:], g["dsg"][:], g["tg"][:, 3:4], None, ALU.mult)
            ln_rstd(nc, g, link, RMS_EPS)

        @block.gpsimd
        def _(pool):
            link = Link(pool, s_g)
            pool.wait_ge(s_const, 16)
            pool.wait_ge(s_dup, 32)
            cos1, sin1 = g["const"][:, C_COS1:C_COS1 + DCTX], g["const"][:, C_SIN1:C_SIN1 + DCTX]
            link(nc.gpsimd.tensor_tensor(kv1[:], g["ctxdup"][:], bc(cos1, 1, B), ALU.mult))
            link(nc.gpsimd.tensor_tensor(g["kvr"][:, :, 0:32], g["ctxdup"][:, :, 32:64], bc(sin1[:, 0:32], 1, B), ALU.mult))
            link(nc.gpsimd.tensor_tensor(g["kvr"][:, :, 32:64], g["ctxdup"][:, :, 0:32], bc(sin1[:, 32:64], 1, B), ALU.mult))
            link(nc.gpsimd.tensor_tensor(g["kvr"][:], kv1[:], g["kvr"][:], ALU.add))


def attn0_phase(nc, a, g, sb, pb, sem):
    ident = g["const"][:, C_ID:C_ID + P]
    VW = HD + 1
    HH = H // 2
    qn = sb("q_normed", [P, C])
    qc = sb("q_cos", [P, C])
    qs = sb("q_sin", [P, C])
    qr = sb("q_roped", [P, C])
    krep = sb("k_repeated", [P, KVH, 4, HD])
    qT = sb("qT", [P, 2, P])
    kbd = sb("k_blockdiag", [P, 4, 4, S])
    pr_ = sb("probs", [P, H, S])
    pT = sb("probsT", [P, H // 2, P])
    vbd = sb("v_blockdiag", [P, 2, KVH, 2 * VW])
    on = sb("heads_out", [P, H, HD])
    oT = sb("heads_outT", [P, 2, P])
    mx = sb("score_max", [P, H])
    rec = sb("sum_recip", [P, H])
    stage = sb("moe_stage", [P, 1536])
    ps_s = pb("ps_scores", [P, 2, 512])
    ps_pT = pb("ps_probsT", [P, H // 2, P])
    ps_qk = pb("ps_qkT", [P, 4, P])
    ps_o = pb("ps_heads", [P, 512])
    ps_oT = pb("ps_headsT", [P, 512])
    ps_y = pb("ps_y", [P, 512])
    pso = ps_o[:, 0:H * VW]

    s_qn, s_qc, s_rot, s_qr = sem("q_normed"), sem("q_cos"), sem("q_rotated"), sem("q_roped")
    s_k, s_vb, s_v0 = sem("k_repeated"), sem("v_ready"), sem("v_ones")
    s_qkT, s_qkE, s_sc, s_mx = sem("qk_transposed"), sem("qk_in_sbuf"), sem("scores_ready"), sem("max_ready")
    s_sh, s_pr, s_pT, s_pTe = sem("scores_shifted"), sem("probs_ready"), sem("probs_transposed"), sem("probsT_in_sbuf")
    s_pv, s_rec, s_on = sem("heads_ready"), sem("recip_ready"), sem("heads_normed")
    s_oT, s_oTe, s_y, s_x = sem("heads_transposed"), sem("headsT_in_sbuf"), sem("y_ready"), sem("x_updated")
    s_wl, s_whi, s_wlo = sem("expert_loaded"), sem("expert_hi"), sem("expert_lo")

    with nc.Block() as block:

        @block.sync
        def _(sp):
            def load(e):
                gu = a["L0_ffn_gate_up"].rearrange("e (t p) f -> e p t f", p=P)
                dn = a["L0_ffn_down"].rearrange("e (t p) f -> e p t f", p=P)
                st = stage[:, 0:1024].rearrange("p (t f) -> p t f", t=2)
                sp.dma_start(st, gu[bass.ds(e, 1)].rearrange("e p t f -> (e p) t f")).then_inc(s_wl, 16)
                st = stage[:, 1024:1536].rearrange("p (t f) -> p t f", t=2)
                sp.dma_start(st, dn[bass.ds(e, 1)].rearrange("e p t f -> (e p) t f")).then_inc(s_wl, 16)

            load(0)
            with sp.Fori(1, NE) as e:
                sp.wait_ge(s_wlo, e)
                load(e)

        @block.gpsimd
        def _(pool):
            half = g["const"][:, C_HALF:C_HALF + 2]

            def rotate(t):
                pool.wait_ge(s_qn, t + 1)
                q, s, w = (v[:].rearrange("p (h d) -> p h d", d=HD) for v in (qn, qs, g["sqw"]))
                nc.gpsimd.tensor_tensor(s[:, :, 0:8], q[:, :, 8:16], w[:, :, 0:8], ALU.mult).then_inc(s_rot, 1)
                nc.gpsimd.tensor_tensor(s[:, :, 8:16], q[:, :, 0:8], w[:, :, 8:16], ALU.mult).then_inc(s_rot, 1)

            def repeat_k(t, first=False):
                if not first:
                    pool.wait_ge(s_qkT, t)
                kv = g["kr"][:, t, :].rearrange("p (g d) -> p g d", d=HD)
                nc.gpsimd.tensor_copy(krep[:], bc(kv, 2, 4)).then_inc(s_k, 1)

            def values(t, first=False):
                if not first:
                    pool.wait_ge(s_pv, t)
                dst = vbd[:].rearrange("p b g (h w) -> p (b g) h w", w=VW)[:, :, :, 0:HD]
                src = g["ctxdup"][:, bass.ds(2 * t, 2), :].rearrange("p b (g d) -> p (b g) d", d=HD)
                nc.gpsimd.tensor_tensor(dst, bc(src, 2, 2), bc(bc(half, 1, 2 * KVH), 3, HD), ALU.mult).then_inc(s_vb, 1)

            def expert(e):
                pool.wait_ge(s_whi, e + 1)
                nc.gpsimd.tensor_tensor(g["wlo"][:, e, :], stage[:], g["whi"][:, e, :].bitcast(FP32),
                                        ALU.subtract).then_inc(s_wlo, 1)

            ones = vbd[:].rearrange("p b g (h w) -> p (b g) h w", w=VW)[:, :, :, HD]
            nc.gpsimd.tensor_copy(ones, bc(half, 1, 2 * KVH)).then_inc(s_v0, 1)
            repeat_k(0, first=True)
            rotate(0)
            repeat_k(1)
            rotate(1)

            def step(t, first=False):
                repeat_k(t + 2)
                rotate(t + 2)
                values(t, first)

            step(0, first=True)
            with pool.Fori(0, 6) as i:
                step(2 * i + 1)
                step(2 * i + 2)
                expert(i)
            step(13)
            expert(6)
            values(14)
            expert(7)
            values(15)

        @block.vector
        def _(dve):
            def rope_norm(t):
                nc.vector.tensor_scalar(qn[:], g["x"][:, t, :], g["mean"][:, bass.ds(t, 1)], g["r"][:, 1, bass.ds(t, 1)],
                                        ALU.subtract, ALU.mult).then_inc(s_qn, 1)
                dve.wait_ge(s_qn, t + 1)
                nc.vector.tensor_tensor(qc[:], qn[:], g["cqw"][:], ALU.mult).then_inc(s_qc, 1)

            def rope_sum(t, first=False):
                dve.wait_ge(s_qc, t + 1)
                dve.wait_ge(s_rot, 2 * (t + 1))
                if not first:
                    dve.wait_ge(s_qkT, t)
                nc.vector.tensor_tensor(qr[:], qc[:], qs[:], ALU.add).then_inc(s_qr, 1)

            def shift(t, j):
                n = 2 * t + j + 1
                if not isinstance(n, int):
                    n = dve.snap(n)
                dve.wait_ge(s_sc, n)
                hs = slice(HH * j, HH * (j + 1))
                sv = ps_s[:, j].rearrange("p (h k) -> p h k", k=S)
                nc.vector.tensor_reduce(mx[:, hs], sv, AX.X, ALU.max).then_inc(s_mx, 1)
                dve.wait_ge(s_mx, n)
                nc.vector.tensor_tensor(pr_[:, hs], sv, bc(mx[:, hs], 2, S), ALU.subtract).then_inc(s_sh, 1)

            def finish(t):
                dve.wait_ge(s_pv, t + 1)
                ov = pso.rearrange("p (h w) -> p h w", w=VW)
                nc.vector.reciprocal(rec[:], ov[:, :, HD]).then_inc(s_rec, 1)
                dve.wait_ge(s_rec, t + 1)
                nc.vector.tensor_tensor(on[:], ov[:, :, 0:HD], bc(rec[:], 2, HD), ALU.mult).then_inc(s_on, 1)

            def residual(t):
                dve.wait_ge(s_y, t + 1)
                nc.vector.scalar_tensor_tensor(g["x"][:, t, :], ps_y[:, 0:C], g["tg"][:, 0:1], g["x"][:, t, :],
                                               ALU.mult, ALU.add).then_inc(s_x, 1)
                dve.wait_ge(s_x, t + 1)
                nc.vector.bn_stats(g["bn"][:, t, :], g["x"][:, t, :])

            rope_norm(0)
            rope_sum(0, first=True)
            rope_norm(1)
            rope_sum(1)
            shift(0, 0)
            shift(0, 1)

            def step(t, first=False, rope=True, scores=True):
                if rope:
                    rope_norm(t + 2)
                if scores:
                    shift(t + 1, 0)
                if rope:
                    rope_sum(t + 2)
                if scores:
                    shift(t + 1, 1)
                if not first:
                    residual(t - 1)
                finish(t)

            step(0, first=True)
            with dve.Fori(1, NT - 2) as t:
                step(t)
            step(NT - 2, rope=False)
            step(NT - 1, rope=False, scores=False)
            residual(NT - 1)

        @block.scalar
        def _(act):
            def qk(t):
                act.wait_ge(s_qkT, t + 1)
                nc.scalar.activation(qT[:], ps_qk[:, 0:2], ACT.Copy)
                for n in range(4):
                    sel = g["const"][:, C_NSEL + n:C_NSEL + n + 1]
                    last = nc.scalar.activation(kbd[:, :, n, :], ps_qk[:, 2:4].rearrange("p c (b k) -> p (c b) k", b=2),
                                                ACT.Copy, scale=sel)
                last.then_inc(s_qkE, 1)

            def exps(t, j):
                act.wait_ge(s_sh, 2 * t + j + 1)
                hs = slice(HH * j, HH * (j + 1))
                nc.scalar.activation(pr_[:, hs], pr_[:, hs], ACT.Exp, scale=float(HD) ** -0.5).then_inc(s_pr, 1)

            def probsT(t):
                act.wait_ge(s_pT, t + 1)
                nc.scalar.activation(pT[:], ps_pT[:], ACT.Copy).then_inc(s_pTe, 1)

            def headsT(t):
                act.wait_ge(s_oT, t + 1)
                nc.scalar.activation(oT[:], ps_oT[:, 0:2 * P], ACT.Copy).then_inc(s_oTe, 1)

            def expert(e):
                act.wait_ge(s_wl, 32 * (e + 1))
                nc.scalar.activation(g["whi"][:, e, :], stage[:], ACT.Copy).then_inc(s_whi, 1)

            def step(t, first=False, scores=True, keys=True):
                probsT(t)
                if not first:
                    headsT(t - 1)
                if scores:
                    exps(t + 1, 0)
                    exps(t + 1, 1)
                if keys:
                    qk(t + 2)

            qk(0)
            exps(0, 0)
            exps(0, 1)
            qk(1)
            step(0, first=True)
            with act.Fori(0, 6) as i:
                step(2 * i + 1)
                expert(i)
                step(2 * i + 2)
            step(13)
            expert(6)
            step(14, keys=False)
            expert(7)
            step(15, scores=False, keys=False)
            headsT(15)

        @block.tensor
        def _(pe):
            def qkT(t):
                pe.wait_ge(s_qr, t + 1)
                pe.wait_ge(s_k, t + 1)
                kr = krep[:].rearrange("p g n d -> p (g n d)")
                for c in range(2):
                    nc.tensor.transpose(ps_qk[:, c], qr[:, c * P:(c + 1) * P], ident)
                for c in range(2):
                    last = nc.tensor.transpose(ps_qk[:, 2 + c], kr[:, c * P:(c + 1) * P], ident)
                last.then_inc(s_qkT, 1)

            def scores(t):
                pe.wait_ge(s_qkE, t + 1)
                for g2 in range(2):
                    nc.tensor.matmul(ps_s[:, g2], g["identb"][:], g["maskb"][:], start=True, stop=False,
                                     skip_group_check=True)
                    for b2 in range(2):
                        for ct in range(2):
                            o = ct * 256
                            last = nc.tensor.matmul(ps_s[64 * b2:64 * b2 + 64, g2, o:o + 256],
                                                    qT[64 * g2:64 * g2 + 64, ct, 64 * b2:64 * b2 + 64],
                                                    kbd[64 * g2:64 * g2 + 64, 2 * ct + b2],
                                                    start=False, stop=True, skip_group_check=True)
                    last.then_inc(s_sc, 1)

            def probsT(t):
                pe.wait_ge(s_pr, 2 * t + 2)
                for q in range(H // 2):
                    last = nc.tensor.transpose(ps_pT[:, q], pr_[:, 2 * q:2 * q + 2].rearrange("p h k -> p (h k)"), ident)
                last.then_inc(s_pT, 1)

            def heads(t):
                pe.wait_ge(s_pTe, t + 1)
                pe.wait_ge(s_vb, t + 1)
                for b2 in range(2):
                    for q in range(H // 2):
                        kvh = 2 * ((q // 2) % 2) + q // 4
                        last = nc.tensor.matmul(pso[64 * b2:64 * b2 + 64, q * 2 * VW:(q + 1) * 2 * VW],
                                                pT[:, q, 64 * b2:64 * b2 + 64], vbd[:, b2, kvh],
                                                start=True, stop=True)
                last.then_inc(s_pv, 1)

            def headsT(t):
                pe.wait_ge(s_on, t + 1)
                ov = on[:].rearrange("p (c h) d -> p c (h d)", c=2)
                for c in range(2):
                    last = nc.tensor.transpose(ps_oT[:, c * P:(c + 1) * P], ov[:, c], ident)
                last.then_inc(s_oT, 1)

            def project(t):
                pe.wait_ge(s_oTe, t + 1)
                for c in range(2):
                    last = nc.tensor.matmul(ps_y[:, 0:C], oT[:, c], g["woutT"][:, c], start=(c == 0), stop=(c == 1))
                last.then_inc(s_y, 1)

            def step(t, first=False, next_scores=True, keys=True):
                probsT(t)
                if not first:
                    headsT(t - 1)
                if next_scores:
                    scores(t + 1)
                if not first:
                    project(t - 1)
                if keys:
                    qkT(t + 2)
                heads(t)

            pe.wait_ge(s_v0, 1)
            qkT(0)
            scores(0)
            qkT(1)
            step(0, first=True)
            with pe.Fori(1, NT - 2) as t:
                step(t)
            step(NT - 2, keys=False)
            step(NT - 1, next_scores=False, keys=False)
            headsT(NT - 1)
            project(NT - 1)


def moe_phase(nc, a, g, sb, pb, sem):
    ident = g["const"][:, C_ID:C_ID + P]
    y = sb("y", [P, TPB, C])
    yhi = sb("yT_hi", [P, CT, BT], F32R)
    ylo = sb("yT_lo", [P, CT, BT], F32R)
    gl = sb("gelu", [P, 2, BT])
    ac = sb("act", [P, 2, BT])
    ahi = sb("act_hi", [P, 2, 2, BT], F32R)
    alo = sb("act_lo", [P, 2, 2, BT], F32R)
    lg = sb("logits", [P, TPB, NE])
    pb_ = sb("router_probs", [P, TPB, NE])
    m4 = sb("router_max", [P, TPB])
    s4 = sb("router_sum", [P, TPB])
    top8 = sb("top8", [P, TPB, 8])
    ix8 = sb("top8_index", [P, TPB, 8], U32)
    ixf = sb("top8_indexf", [P, TPB, 8])
    tw = sb("top_w", [P, TPB, 2])
    c0 = sb("comb0", [P, TPB, NE])
    c1 = sb("comb1", [P, TPB, NE])
    comb = sb("comb", [P, TPB, NE])
    wkcq = sb("w_kc_q", [P, GH, DCQ])
    wqr = sb("w_qr", [96, 2, GH, R])
    wkr = sb("w_kr", [DCTX, GH, R])
    wq = sb("w_q", [P, GH, C])
    wkv = sb("w_kc_kv", [P, GH, DCTX])
    wo = sb("w_o", [P, 2, GH * KD])
    derived = sb("products", [P, 1024])
    kcqT = derived[0:96, :].rearrange("p (t h k) -> p t h k", t=2, h=GH)
    woT = derived[:].rearrange("p (h c) -> p h c", h=GH)
    krT = sb("krT", [P, 2, DCTX])
    a1T = sb("a1T", [P, 2, KD])
    a2 = sb("a2", [P, 2, 2, DCTX])
    ps_g = [pb(f"ps_gate{f}", [P, BT]) for f in range(2)]
    ps_u = [pb(f"ps_up{f}", [P, BT]) for f in range(2)]
    ps_t = pb("ps_yT", [P, CT, BT])
    ps_d = pb("ps_down", [P, TPB, C])

    s_v = sem("dve_step")
    s_yn, s_yt, s_yh, s_yl = sem("y_normed"), sem("y_transposed"), sem("y_hi"), sem("y_lo")
    s_lg, s_rx, s_re = sem("logits_ready"), sem("router_shifted"), sem("router_exp")
    s_gu, s_gl, s_ac, s_ah, s_al = sem("gate_up_ready"), sem("gelu_ready"), sem("act_ready"), sem("act_hi"), sem("act_lo")
    s_dn, s_mix = sem("down_ready"), sem("mixed")
    s_rt, s_pw, s_wl = sem("router_step"), sem("router_wait"), sem("weights_loaded")
    s_mt, s_me = sem("products_ready"), sem("products_read")
    STEPS = 18
    LOADS = 7
    MT, ME = 5, 7

    with nc.Block() as block:

        @block.sync
        def _(sp):
            def load(gr):
                hs = bass.ds(GH * gr, GH)
                hk = bass.ds(KD * GH * gr, KD * GH)
                sp.dma_start(wkcq[:], a["L1_xattn_w_kc_q"][hs].rearrange("h k q -> k h q")).then_inc(s_wl, 16)
                for t in range(2):
                    src = a["L1_xattn_W_qr"][hs, 96 * t:96 * t + 96, :].rearrange("h q r -> q h r")
                    sp.dma_start(wqr[:, t], src).then_inc(s_wl, 16)
                sp.dma_start(wkr[:], a["L1_xattn_W_kr"][hs].rearrange("h d r -> d h r")).then_inc(s_wl, 16)
                src = a["L1_xattn_Wq"].rearrange("(h k) c -> k h c", k=KD)[:, hs, :]
                sp.dma_start(wq[:], src).then_inc(s_wl, 16)
                sp.dma_start(wkv[:], a["L1_xattn_w_kc_kv"][hs].rearrange("h k d -> k h d")).then_inc(s_wl, 16)
                src = a["L1_xattn_Wo"].rearrange("(t o) n -> o t n", o=P)[:, :, hk]
                sp.dma_start(wo[:], src).then_inc(s_wl, 16)

            load(0)
            with sp.Fori(1, NBLK) as k:
                sp.wait_ge(s_mt, MT * k)
                load(k)

        @block.vector
        def _(dve):
            def normed(k):
                for u in range(TPB):
                    t = TPB * k + u
                    nc.vector.tensor_scalar(y[:, u], g["x"][:, t, :], g["mean"][:, bass.ds(t, 1)], g["r"][:, 0, bass.ds(t, 1)],
                                            ALU.subtract, ALU.mult).then_inc(s_yn, 1)

            def low(k):
                dve.wait_ge(s_yh, k + 1)
                nc.vector.tensor_tensor(ylo[:], ps_t[:], yhi[:].bitcast(FP32), ALU.subtract).then_inc(s_yl, 1)

            def router(k):
                link = Link(dve, s_rt, k * STEPS)
                r2 = bc(g["r2"][:, bass.ds(TPB * k, TPB)], 2, NE)
                dve.wait_ge(s_lg, k + 1)
                link(nc.vector.tensor_tensor(lg[:], ps_t[:, 0, 0:TPB * NE].rearrange("p (u e) -> p u e", e=NE), r2, ALU.mult))
                link(nc.vector.tensor_reduce(m4[:], lg[:], AX.X, ALU.max))
                nc.vector.tensor_tensor(lg[:], lg[:], bc(m4[:], 2, NE), ALU.subtract).then_inc(s_rx, 1)
                dve.wait_ge(s_re, k + 1)
                link(nc.vector.tensor_reduce(s4[:], pb_[:], AX.X, ALU.add))
                link(nc.vector.reciprocal(m4[:], s4[:]))
                link(nc.vector.tensor_tensor(pb_[:], pb_[:], bc(m4[:], 2, NE), ALU.mult))
                dve.sem_inc(s_pw, 1)
                for u in range(TPB):
                    last = nc.vector.max(top8[:, u], pb_[:, u])
                link(last)
                link(nc.vector.tensor_tensor(s4[:], top8[:, :, 0], top8[:, :, 1], ALU.add))
                dve.sem_inc(s_pw, 1)
                for u in range(TPB):
                    last = nc.vector.max_index(ix8[:, u], top8[:, u], pb_[:, u])
                link(last)
                link(nc.vector.tensor_copy(ixf[:], ix8[:]))
                link(nc.vector.tensor_scalar(s4[:], s4[:], 1e-12, None, ALU.max))
                link(nc.vector.reciprocal(m4[:], s4[:]))
                link(nc.vector.tensor_tensor(tw[:], top8[:, :, 0:2], bc(m4[:], 2, 2), ALU.mult))
                iota = bc(g["const"][:, C_IOTA:C_IOTA + NE], 1, TPB)
                for c, j in ((c0, 0), (c1, 1)):
                    link(nc.vector.tensor_tensor(c[:], iota, bc(ixf[:, :, j], 2, NE), ALU.is_equal))
                    link(nc.vector.tensor_tensor(c[:], c[:], bc(tw[:, :, j], 2, NE), ALU.mult))
                link(nc.vector.tensor_tensor(c0[:], c0[:], c1[:], ALU.add))
                link(nc.vector.tensor_tensor(comb[:], c0[:], bc(g["pes"][:], 1, TPB), ALU.mult))
                assert link.n == STEPS, link.n

            def mix(k, e):
                for u in range(TPB):
                    t = TPB * k + u
                    if u % 2 == 0:
                        dve.wait_ge(s_dn, 2 * NE * k + (2 * e + u // 2 + 1))
                    if e:
                        dve.wait_ge(s_mix, TPB * NE * k + (TPB * (e - 1) + u + 1))
                    nc.vector.scalar_tensor_tensor(g["x"][:, t, :], ps_d[:, u], comb[:, u, e:e + 1], g["x"][:, t, :],
                                                   ALU.mult, ALU.add).then_inc(s_mix, 1)

            def statistics(k):
                for u in range(TPB):
                    t = TPB * k + u
                    dve.wait_ge(s_mix, TPB * NE * k + (TPB * (NE - 1) + u + 1))
                    nc.vector.bn_stats(g["bn"][:, t, :], g["x"][:, t, :])

            def products(k, e):
                n = MT * k + (e + 1)
                if e == 0:
                    dve.wait_ge(s_mt, n)
                    nc.vector.tensor_copy(kcqT, ps_t[0:96].rearrange("p t (h k) -> p t h k", h=GH)).then_inc(s_me, 1)
                elif e == 1:
                    dve.wait_ge(s_mt, n)
                    nc.vector.tensor_copy(a1T[:], ps_t[:, 0, 0:2 * KD].rearrange("p (h k) -> p h k", h=2)).then_inc(s_me, 1)
                elif e == 3:
                    dve.wait_ge(s_mt, n)
                    nc.vector.tensor_copy(a2[:], ps_t[:, :, 0:2 * DCTX].rearrange("p h (q d) -> p h q d", q=2)).then_inc(s_me, 1)
                elif e == 4:
                    dve.wait_ge(s_me, ME * k + 6)
                    nc.vector.tensor_tensor(g["mlo"][:, :, bass.ds(k * 256, 256)], ps_t[:, 0].rearrange("p (t n) -> p t n", t=CT),
                                            g["mhi"][:, :, bass.ds(k * 256, 256)].bitcast(FP32),
                                            ALU.subtract).then_inc(s_me, 1)

            def block_(k, last=False):
                for e in range(NE):
                    for f in range(2):
                        m = 2 * NE * k + (2 * e + f + 1)
                        if not isinstance(m, int):
                            m = dve.snap(m)
                        dve.wait_ge(s_gl, m)
                        nc.vector.tensor_tensor(ac[:, f], gl[:, f], ps_u[f][:], ALU.mult).then_inc(s_ac, 1)
                        dve.wait_ge(s_ah, m)
                        nc.vector.tensor_tensor(alo[:, e % 2, f], ac[:, f], ahi[:, e % 2, f].bitcast(FP32),
                                                ALU.subtract).then_inc(s_al, 1)
                    if e:
                        if e == NE - 1 and not last:
                            low(k + 1)
                        products(k, e - 1)
                        mix(k, e - 1)
                        if e == 5 and not last:
                            normed(k + 1)
                mix(k, NE - 1)
                if not last:
                    router(k + 1)
                statistics(k)

            ln_rstd(nc, g, Link(dve, s_v), ROUTER_EPS)
            normed(0)
            low(0)
            router(0)
            with dve.Fori(0, NBLK - 1) as k:
                block_(k)
            block_(NBLK - 1, last=True)

        @block.scalar
        def _(act):
            def high(k):
                act.wait_ge(s_yt, k + 1)
                nc.scalar.activation(yhi[:], ps_t[:], ACT.Copy).then_inc(s_yh, 1)

            def router(k):
                act.wait_ge(s_rx, k + 1)
                nc.scalar.activation(pb_[:], lg[:], ACT.Exp).then_inc(s_re, 1)

            def products(k, e):
                n = MT * k + (e + 1)
                if e == 1:
                    act.wait_ge(s_mt, n)
                    nc.scalar.activation(krT[:], ps_t[:, 1, 0:2 * DCTX], ACT.Copy).then_inc(s_me, 1)
                elif e == 2:
                    act.wait_ge(s_mt, n)
                    nc.scalar.activation(woT, ps_t[:].rearrange("p t (h c) -> p (t h) c", h=2), ACT.Copy).then_inc(s_me, 1)
                elif e == 4:
                    act.wait_ge(s_mt, n)
                    nc.scalar.activation(g["pm"][:, bass.ds(k * 2, 2), :], ps_t[:, 1].rearrange("p (t n) -> p t n", t=2), ACT.Copy)
                    nc.scalar.activation(g["mhi"][:, :, bass.ds(k * 256, 256)], ps_t[:, 0].rearrange("p (t n) -> p t n", t=CT),
                                         ACT.Copy).then_inc(s_me, 1)

            def block_(k, last=False):
                for e in range(NE):
                    for f in range(2):
                        m = 2 * NE * k + (2 * e + f + 1)
                        if not isinstance(m, int):
                            m = act.snap(m)
                        act.wait_ge(s_gu, m)
                        nc.scalar.activation(gl[:, f], ps_g[f][:], ACT.Gelu).then_inc(s_gl, 1)
                        act.wait_ge(s_ac, m)
                        nc.scalar.activation(ahi[:, e % 2, f], ac[:, f], ACT.Copy).then_inc(s_ah, 1)
                    if e:
                        products(k, e - 1)
                if not last:
                    high(k + 1)
                    router(k + 1)

            high(0)
            router(0)
            with act.Fori(0, NBLK - 1) as k:
                block_(k)
            block_(NBLK - 1, last=True)

        @block.tensor
        def _(pe):
            whi, wlo = g["whi"], g["wlo"]

            def yT(k):
                for u in range(TPB):
                    pe.wait_ge(s_yn, TPB * k + (u + 1))
                    for c in range(CT):
                        last = nc.tensor.transpose(ps_t[:, c, u * P:(u + 1) * P], y[:, u, c * P:(c + 1) * P], ident)
                last.then_inc(s_yt, 1)

            def logits(k):
                pe.wait_ge(s_yl, k + 1)
                for u in range(TPB):
                    parts = [(yy, ww) for yy in (yhi, ylo) for ww in (g["gwhi"], g["gwlo"])]
                    for j, (yy, ww) in enumerate(parts):
                        for c in range(CT):
                            last = nc.tensor.matmul(ps_t[:, 0, u * NE:(u + 1) * NE], yy[:, c, u * P:(u + 1) * P], ww[:, c],
                                                    start=(j + c == 0), stop=(j == 3 and c == 1))
                last.then_inc(s_lg, 1)

            def up(k, e):
                for f in range(2):
                    if e:
                        pe.wait_ge(s_ac, 2 * NE * k + (2 * (e - 1) + f + 1))
                    for ps, o in ((ps_g[f], f * P), (ps_u[f], ED + f * P)):
                        for j, (w, yy) in enumerate(split_passes((whi, yhi), (wlo, ylo))):
                            for c in range(CT):
                                last = nc.tensor.matmul(ps[:], w[:, e, c * 512 + o:c * 512 + o + P], yy[:, c],
                                                        start=(j + c == 0), stop=(j == 2 and c == 1))
                    last.then_inc(s_gu, 1)

            def down(k, e):
                pe.wait_ge(s_al, 2 * NE * k + 2 * (e + 1))
                for u in range(TPB):
                    if e and u % 2 == 0:
                        pe.wait_ge(s_mix, TPB * NE * k + (TPB * (e - 1) + u + 2))
                    for j, (w, aa) in enumerate(split_passes((whi, ahi), (wlo, alo))):
                        for f in range(2):
                            last = nc.tensor.matmul(ps_d[:, u], aa[:, e % 2, f, u * P:(u + 1) * P],
                                                    w[:, e, 1024 + f * C:1024 + (f + 1) * C],
                                                    start=(j + f == 0), stop=(j == 2 and f == 1))
                    if u % 2:
                        last.then_inc(s_dn, 1)

            def products(k, e):
                heads = [(h, h // 2, h % 2) for h in range(GH)]
                if e == 0:
                    pe.wait_ge(s_wl, 16 * LOADS * (k + 1))
                    for t in range(2):
                        for h in range(GH):
                            last = nc.tensor.transpose(ps_t[0:96, t, h * KD:(h + 1) * KD],
                                                       wkcq[:, h, 96 * t:96 * t + 96], ident)
                elif e == 1:
                    pe.wait_ge(s_me, ME * k + 1)
                    for h, pr, h2 in heads:
                        for t in range(2):
                            nc.tensor.matmul(ps_t[64 * h2:64 * h2 + 64, 0, pr * KD:(pr + 1) * KD],
                                                    wqr[:, t, h], kcqT[:, t, h], start=(t == 0), stop=(t == 1))
                    for pr in range(2):
                        last = nc.tensor.transpose(ps_t[:, 1, pr * DCTX:(pr + 1) * DCTX],
                                                   wkr[:, 2 * pr:2 * pr + 2, :].rearrange("p h r -> p (h r)"),
                                                   ident[0:DCTX, 0:DCTX])
                elif e == 2:
                    pe.wait_ge(s_me, ME * k + 3)
                    for h in range(GH):
                        for ot in range(2):
                            o = (h % 2) * C + ot * P
                            last = nc.tensor.transpose(ps_t[:, h // 2, o:o + P], wo[:, ot, h * KD:(h + 1) * KD], ident)
                elif e == 3:
                    pe.wait_ge(s_me, ME * k + 4)
                    for h, pr, h2 in sorted(heads, key=lambda v: v[2]):
                        last = nc.tensor.matmul(ps_t[:, h2, pr * DCTX:(pr + 1) * DCTX], a1T[64 * h2:64 * h2 + 64, pr],
                                                krT[64 * h2:64 * h2 + 64, pr], start=True, stop=True)
                elif e == 4:
                    pe.wait_ge(s_me, ME * k + 5)
                    for h, pr, h2 in heads:
                        nc.tensor.matmul(ps_t[64 * h2:64 * h2 + 64, 1, pr * C:(pr + 1) * C], wkv[:, h], woT[:, h],
                                         start=True, stop=True)
                    for ct in range(CT):
                        for h, pr, h2 in heads:
                            o = (ct * GH + h) * DCTX
                            last = nc.tensor.matmul(ps_t[:, 0, o:o + DCTX], wq[:, h, ct * P:(ct + 1) * P], a2[:, h2, pr],
                                                    start=True, stop=True)
                else:
                    return
                last.then_inc(s_mt, 1)

            def block_(k, last=False):
                up(k, 0)
                for e in range(NE):
                    if e + 1 < NE:
                        up(k, e + 1)
                        products(k, e)
                    if e == NE - 2 and not last:
                        pe.wait_ge(s_me, ME * (k + 1))
                        yT(k + 1)
                    down(k, e)
                if not last:
                    logits(k + 1)

            yT(0)
            logits(0)
            with pe.Fori(0, NBLK - 1) as k:
                block_(k)
            block_(NBLK - 1, last=True)


def attn1_phase(nc, a, g, sb, pb, sem):
    ident = g["const"][:, C_ID:C_ID + P]
    NP = H // 2
    HH = H // 2
    y = sb("y", [P, TPB, C])
    yhi = sb("yT_hi", [P, CT, BT], F32R)
    ylo = sb("yT_lo", [P, CT, BT], F32R)
    qt = sb("q_tilT", [P, NP, BT])
    kvbd = [sb(f"kv_blockdiag{u}", [P, 2, P]) for u in range(TPB)]
    kvbT = sb("kv_blockdiagT", [P, 2, P])
    z = sb("probs", [P, H, S])
    pT = sb("probsT", [P, NP, P])
    cT = sb("ctxT", [P, NP, 2, S])
    mx = sb("score_max", [P, H])
    sm = sb("prob_sum", [P, H])
    rec = sb("sum_recip", [P, H])
    raw = sb("ffn_raw", [P, 3 * 1536])
    QN = 3 * 1536 // NBLK
    p2 = sb("power_of_two", [P, QN])
    rnd = sb("rounded", [P, QN])
    ps_s = pb("ps_scores", [P, 2, 512])
    ps_pT = pb("ps_probsT", [P, NP, P])
    ps_c = pb("ps_ctxT", [P, 2, 512])
    ps_y = pb("ps_y", [P, 512])
    ps_k = pb("ps_kvT", [P, 512])

    s_v, s_raw, s_q8 = sem("dve_step"), sem("raw_loaded"), sem("fp8_step")
    s_yn, s_yt, s_yh, s_yl = sem("y_normed"), sem("y_transposed"), sem("y_hi"), sem("y_lo")
    s_q, s_qe = sem("q_ready"), sem("q_in_sbuf")
    s_kb, s_kT, s_kTe = sem("kv_ready"), sem("kv_transposed"), sem("kvT_in_sbuf")
    s_sc, s_mx, s_sh, s_ex, s_sum, s_rec, s_pr = (sem("scores_ready"), sem("max_ready"), sem("scores_shifted"),
                                                  sem("exp_ready"), sem("sum_ready"), sem("recip_ready"), sem("probs_ready"))
    s_pT, s_pTe, s_c, s_ce, s_y = (sem("probs_transposed"), sem("probsT_in_sbuf"), sem("ctx_ready"),
                                   sem("ctx_in_sbuf"), sem("y_ready"))
    s_x, s_yf = sem("x_updated"), sem("y_bank_free")
    QSTEPS = 6

    with nc.Block() as block:

        @block.sync
        def _(sp):
            for j, (name, t) in enumerate((("L1_ffn_gate_w", 2), ("L1_ffn_up_w", 2), ("L1_ffn_down_w", 6))):
                dst = raw[:, j * 1536:(j + 1) * 1536].rearrange("p (t n) -> p t n", t=t)
                sp.dma_start(dst, a[name].rearrange("(t p) n -> p t n", p=P)).then_inc(s_raw, 16)

        @block.gpsimd
        def _(pool):
            half = g["const"][:, C_HALF:C_HALF + 2]

            def keys(t, u, first=False):
                if not first:
                    pool.wait_ge(s_c, t - (TPB - 1))
                src = g["kvr"][:, bass.ds(2 * t, 2), :]
                nc.gpsimd.tensor_tensor(kvbd[u][:].rearrange("p b (h d) -> p b h d", h=2), bc(src, 2, 2),
                                        bc(bc(half, 1, 2), 3, DCTX), ALU.mult).then_inc(s_kb, 1)

            for u in range(TPB):
                keys(u, u, first=True)
            with pool.Fori(1, NBLK) as k:
                for u in range(TPB):
                    keys(TPB * k + u, u)

        @block.vector
        def _(dve):
            def const_or_snap(n):
                return n if isinstance(n, int) else dve.snap(n)

            def normed(k):
                for u in range(TPB):
                    t = TPB * k + u
                    nc.vector.tensor_scalar(y[:, u], g["x"][:, t, :], g["mean"][:, bass.ds(t, 1)], g["r"][:, 0, bass.ds(t, 1)],
                                            ALU.subtract, ALU.mult).then_inc(s_yn, 1)

            def low(k):
                dve.wait_ge(s_yh, k + 1)
                nc.vector.tensor_tensor(ylo[:], ps_c[:], yhi[:].bitcast(FP32), ALU.subtract).then_inc(s_yl, 1)

            def ffn_weights(k):
                link = Link(dve, s_q8, k * QSTEPS)
                w = raw[:, bass.ds(k * QN, QN)]
                link(nc.vector.tensor_scalar(p2[:].bitcast(I32), w.bitcast(I32), 0x7F800000, None, ALU.bitwise_and))
                link(nc.vector.tensor_scalar(p2[:], p2[:], 2.0 ** -6, 1.5 * 2.0 ** 20, ALU.max, ALU.mult))
                link(nc.vector.tensor_tensor(rnd[:], w, p2[:], ALU.add))
                link(nc.vector.tensor_tensor(rnd[:], rnd[:], p2[:], ALU.subtract))
                link(nc.vector.tensor_scalar(p2[:], rnd[:], OVERFLOW, 0.0, ALU.mult, ALU.mult))
                link(nc.vector.tensor_tensor(g["wq8"][:, bass.ds(k * QN, QN)], rnd[:], p2[:], ALU.add))
                assert link.n == QSTEPS

            def shift(t, j):
                n = const_or_snap(2 * t + (j + 1))
                hs = slice(HH * j, HH * (j + 1))
                sv = ps_s[:, j].rearrange("p (h k) -> p h k", k=S)
                dve.wait_ge(s_sc, n)
                nc.vector.tensor_reduce(mx[:, hs], sv, AX.X, ALU.max).then_inc(s_mx, 1)
                dve.wait_ge(s_mx, n)
                nc.vector.tensor_tensor(z[:, hs], sv, bc(mx[:, hs], 2, S), ALU.subtract).then_inc(s_sh, 1)

            def normalise(t, j):
                n = const_or_snap(2 * t + (j + 1))
                hs = slice(HH * j, HH * (j + 1))
                dve.wait_ge(s_ex, n)
                nc.vector.tensor_reduce(sm[:, hs], z[:, hs], AX.X, ALU.add).then_inc(s_sum, 1)
                dve.wait_ge(s_sum, n)
                nc.vector.reciprocal(rec[:, hs], sm[:, hs]).then_inc(s_rec, 1)
                dve.wait_ge(s_rec, n)
                nc.vector.tensor_tensor(z[:, hs], z[:, hs], bc(rec[:, hs], 2, S), ALU.mult).then_inc(s_pr, 1)

            def residual(t):
                n = const_or_snap(t + 1)
                dve.wait_ge(s_y, n)
                nc.vector.scalar_tensor_tensor(g["x"][:, t, :], ps_y[:, 0:C], g["tg"][:, 1:2], g["x"][:, t, :],
                                               ALU.mult, ALU.add).then_inc(s_x, 1)
                dve.wait_ge(s_x, n)
                nc.vector.bn_stats(g["bn"][:, t, :], g["x"][:, t, :]).then_inc(s_yf, 1)

            def block_(k, last=False):
                for u in range(TPB):
                    t = TPB * k + u
                    if u == 2 and not last:
                        low(k + 1)
                    if u == 3 and not last:
                        ffn_weights(k + 1)
                    if not (last and u == TPB - 1):
                        for j in range(2):
                            shift(t + 1, j)
                            normalise(t + 1, j)
                    residual(t)
                    if u == 1 and not last:
                        normed(k + 1)

            dve.sem_inc(s_yf, 1)
            ln_rstd(nc, g, Link(dve, s_v))
            normed(0)
            low(0)
            dve.wait_ge(s_raw, 48)
            ffn_weights(0)
            for j in range(2):
                shift(0, j)
                normalise(0, j)
            with dve.Fori(0, NBLK - 1) as k:
                block_(k)
            block_(NBLK - 1, last=True)

        @block.scalar
        def _(act):
            def high(k):
                act.wait_ge(s_yt, k + 1)
                nc.scalar.activation(yhi[:], ps_c[:], ACT.Copy).then_inc(s_yh, 1)

            def queries(k):
                for p in range(NP):
                    act.wait_ge(s_q, NP * k + (p + 1))
                    nc.scalar.activation(qt[:, p], ps_c[:, p % 2], ACT.Copy).then_inc(s_qe, 1)

            def kvT(t):
                act.wait_ge(s_kT, t + 1)
                nc.scalar.activation(kvbT[:], ps_k[:, 0:2 * P], ACT.Copy).then_inc(s_kTe, 1)

            def probsT(t):
                act.wait_ge(s_pT, t + 1)
                nc.scalar.activation(pT[:], ps_pT[:], ACT.Copy).then_inc(s_pTe, 1)

            def exps(t, j):
                act.wait_ge(s_sh, 2 * t + (j + 1))
                hs = slice(HH * j, HH * (j + 1))
                nc.scalar.activation(z[:, hs], z[:, hs], ACT.Exp).then_inc(s_ex, 1)

            def ctxT(t):
                act.wait_ge(s_c, t + 1)
                nc.scalar.activation(cT[:].rearrange("p q b s -> p b q s"), ps_c[:].rearrange("p b (q s) -> p b q s", q=NP),
                                     ACT.Copy).then_inc(s_ce, 1)

            def block_(k, last=False):
                for u in range(TPB):
                    t = TPB * k + u
                    more = not (last and u == TPB - 1)
                    probsT(t)
                    if u == 2 and not last:
                        high(k + 1)
                    if u == 3 and not last:
                        queries(k + 1)
                    if more:
                        exps(t + 1, 0)
                    ctxT(t)
                    if not (last and u >= 2):
                        kvT(t + 2)
                    if more:
                        exps(t + 1, 1)

            high(0)
            queries(0)
            kvT(0)
            exps(0, 0)
            exps(0, 1)
            kvT(1)
            with act.Fori(0, NBLK - 1) as k:
                block_(k)
            block_(NBLK - 1, last=True)

        @block.tensor
        def _(pe):
            def yT(k):
                for u in range(TPB):
                    pe.wait_ge(s_yn, TPB * k + (u + 1))
                    for c in range(CT):
                        last = nc.tensor.transpose(ps_c[:, c, u * P:(u + 1) * P], y[:, u, c * P:(c + 1) * P], ident)
                last.then_inc(s_yt, 1)

            def queries(k):
                for p in range(NP):
                    if p >= 2:
                        pe.wait_ge(s_qe, NP * k + (p - 1))
                    for j, (w, yy) in enumerate(split_passes((g["mhi"], yhi), (g["mlo"], ylo))):
                        for c in range(CT):
                            last = nc.tensor.matmul(ps_c[:, p % 2], w[:, c, p * P:(p + 1) * P], yy[:, c],
                                                    start=(j + c == 0), stop=(j == 2 and c == 1))
                    last.then_inc(s_q, 1)

            def kvT(t, u):
                pe.wait_ge(s_kb, t + 1)
                for b2 in range(2):
                    last = nc.tensor.transpose(ps_k[:, b2 * P:(b2 + 1) * P], kvbd[u][:, b2], ident)
                last.then_inc(s_kT, 1)

            def scores(u, j):
                for p in range(4 * j, 4 * j + 4):
                    for b2 in range(2):
                        c = u * P + 64 * b2
                        last = nc.tensor.matmul(ps_s[64 * b2:64 * b2 + 64, j, (p % 4) * P:(p % 4 + 1) * P],
                                                qt[:, p, c:c + 64], kvbT[:, b2], start=True, stop=True)
                last.then_inc(s_sc, 1)

            def probsT(t):
                pe.wait_ge(s_pr, 2 * t + 2)
                for p in range(NP):
                    last = nc.tensor.transpose(ps_pT[:, p], z[:, 2 * p:2 * p + 2].rearrange("p h k -> p (h k)"), ident)
                last.then_inc(s_pT, 1)

            def ctxT(t, u):
                pe.wait_ge(s_pTe, t + 1)
                for b2 in range(2):
                    last = nc.tensor.matmul(ps_c[:, b2], kvbd[u][:, b2], pT[:, :, 64 * b2:64 * b2 + 64],
                                            start=True, stop=True)
                last.then_inc(s_c, 1)

            def project(t):
                pe.wait_ge(s_ce, t + 1)
                pe.wait_ge(s_yf, t + 1)
                for p in range(NP):
                    last = nc.tensor.matmul(ps_y[:, 0:C], cT[:, p].rearrange("p b s -> p (b s)"), g["pm"][:, p],
                                            start=(p == 0), stop=(p == NP - 1))
                last.then_inc(s_y, 1)

            def block_(k, last=False):
                for u in range(TPB):
                    t = TPB * k + u
                    more = not (last and u == TPB - 1)
                    un = (u + 1) % TPB
                    probsT(t)
                    if u == 2 and not last:
                        yT(k + 1)
                    if u == 3 and not last:
                        queries(k + 1)
                        pe.wait_ge(s_qe, NP * (k + 2))
                    if more:
                        pe.wait_ge(s_kTe, t + 2)
                        scores(un, 0)
                    if u == 2 and not last:
                        pe.wait_ge(s_yl, k + 2)
                    ctxT(t, u)
                    if more:
                        scores(un, 1)
                    if not (last and u >= 2):
                        kvT(t + 2, (u + 2) % TPB)
                    project(t)

            yT(0)
            pe.wait_ge(s_yl, 1)
            queries(0)
            kvT(0, 0)
            pe.wait_ge(s_kTe, 1)
            pe.wait_ge(s_qe, NP)
            scores(0, 0)
            scores(0, 1)
            kvT(1, 1)
            with pe.Fori(0, NBLK - 1) as k:
                block_(k)
            block_(NBLK - 1, last=True)


def ffn_phase(nc, a, g, out, sb, pb, sem):
    ident = g["const"][:, C_ID:C_ID + P]
    wg, wu, wd = (g["wq8"][:, j * 1536:(j + 1) * 1536] for j in range(3))
    y = sb("y", [P, TPB, C])
    yhi = sb("yT_hi", [P, CT, BT], F32R)
    ylo = sb("yT_lo", [P, CT, BT], F32R)
    sg = sb("silu", [P, 2, BT])
    ac = sb("act", [P, 2, BT])
    ahi = sb("act_hi", [P, FT, BT], F32R)
    alo = sb("act_lo", [P, FT, BT], F32R)
    ot = sb("scaled", [P, TPB, C])
    ps_g = [pb(f"ps_gate{f}", [P, BT]) for f in range(2)]
    ps_u = [pb(f"ps_up{f}", [P, BT]) for f in range(2)]
    ps_t = pb("ps_yT", [P, CT, BT])
    ps_d = pb("ps_down", [P, TPB, C])
    s_v = sem("dve_step")
    s_yn, s_yt, s_yh, s_yl = sem("y_normed"), sem("y_transposed"), sem("y_hi"), sem("y_lo")
    s_gu, s_sg, s_ac, s_ah, s_al = sem("gate_up_ready"), sem("silu_ready"), sem("act_ready"), sem("act_hi"), sem("act_lo")
    s_dn, s_sc, s_x, s_out = sem("down_ready"), sem("scaled"), sem("x_final"), sem("stored")

    with nc.Block() as block:

        @block.sync
        def _(sp):
            ov = out.rearrange("(t b) s c -> t (b s) c", b=2)
            with sp.Fori(0, NT) as t:
                sp.wait_ge(s_x, t + 1)
                sp.dma_start(ov[bass.ds(t, 1)].rearrange("t p c -> (t p) c"), g["x"][:, t, :]).then_inc(s_out, 16)
            sp.wait_ge(s_out, 16 * NT)

        @block.vector
        def _(dve):
            def normed(k):
                for u in range(TPB):
                    t = TPB * k + u
                    nc.vector.tensor_scalar(y[:, u], g["x"][:, t, :], g["mean"][:, bass.ds(t, 1)], g["r"][:, 0, bass.ds(t, 1)],
                                            ALU.subtract, ALU.mult).then_inc(s_yn, 1)

            def low(k):
                dve.wait_ge(s_yh, k + 1)
                nc.vector.tensor_tensor(ylo[:], ps_t[:], yhi[:].bitcast(FP32), ALU.subtract).then_inc(s_yl, 1)

            def block_(k, last=False):
                for f in range(FT):
                    m = FT * k + (f + 1)
                    dve.wait_ge(s_sg, m)
                    nc.vector.scalar_tensor_tensor(ac[:, f % 2], ps_u[f % 2][:], g["fus"][:, f:f + 1], sg[:, f % 2],
                                                   ALU.mult, ALU.mult).then_inc(s_ac, 1)
                    dve.wait_ge(s_ah, m)
                    nc.vector.tensor_tensor(alo[:, f], ac[:, f % 2], ahi[:, f].bitcast(FP32), ALU.subtract).then_inc(s_al, 1)
                    if f == 2 and not last:
                        normed(k + 1)
                if not last:
                    low(k + 1)
                for u in range(TPB):
                    t = TPB * k + u
                    if u % 2 == 0:
                        dve.wait_ge(s_dn, 2 * k + (u // 2 + 1))
                    nc.vector.tensor_tensor(ot[:, u], ps_d[:, u], g["dsg"][:], ALU.mult).then_inc(s_sc, 1)
                for u in range(TPB):
                    t = TPB * k + u
                    dve.wait_ge(s_sc, TPB * k + (u + 1))
                    nc.vector.tensor_tensor(g["x"][:, t, :], g["x"][:, t, :], ot[:, u], ALU.add).then_inc(s_x, 1)

            ln_rstd(nc, g, Link(dve, s_v))
            normed(0)
            low(0)
            with dve.Fori(0, NBLK - 1) as k:
                block_(k)
            block_(NBLK - 1, last=True)

        @block.scalar
        def _(act):
            def high(k):
                act.wait_ge(s_yt, k + 1)
                nc.scalar.activation(yhi[:], ps_t[:], ACT.Copy).then_inc(s_yh, 1)

            def block_(k, last=False):
                for f in range(FT):
                    m = FT * k + (f + 1)
                    act.wait_ge(s_gu, m)
                    nc.scalar.activation(sg[:, f % 2], ps_g[f % 2][:], ACT.Silu, scale=g["fgs"][:, f:f + 1]).then_inc(s_sg, 1)
                    act.wait_ge(s_ac, m)
                    nc.scalar.activation(ahi[:, f], ac[:, f % 2], ACT.Copy).then_inc(s_ah, 1)
                if not last:
                    high(k + 1)

            high(0)
            with act.Fori(0, NBLK - 1) as k:
                block_(k)
            block_(NBLK - 1, last=True)

        @block.tensor
        def _(pe):
            def yT(k):
                for u in range(TPB):
                    pe.wait_ge(s_yn, TPB * k + (u + 1))
                    for c in range(CT):
                        last = nc.tensor.transpose(ps_t[:, c, u * P:(u + 1) * P], y[:, u, c * P:(c + 1) * P], ident)
                last.then_inc(s_yt, 1)

            def block_(k, last=False):
                for f in range(FT):
                    if f >= 2:
                        pe.wait_ge(s_ac, FT * k + (f - 1))
                    if f == 0:
                        pe.wait_ge(s_yl, k + 1)
                    for ps, w in ((ps_g[f % 2], wg), (ps_u[f % 2], wu)):
                        for j, yy in enumerate((yhi, ylo)):
                            for c in range(CT):
                                last_ = nc.tensor.matmul(ps[:], w[:, c * FI + f * P:c * FI + (f + 1) * P], yy[:, c],
                                                         start=(j + c == 0), stop=(j + c == 2))
                    last_.then_inc(s_gu, 1)
                if not last:
                    yT(k + 1)
                pe.wait_ge(s_al, FT * (k + 1))
                for u in range(TPB):
                    for f in range(FT):
                        for j, aa in enumerate((ahi, alo)):
                            last_ = nc.tensor.matmul(ps_d[:, u], aa[:, f, u * P:(u + 1) * P], wd[:, f * C:(f + 1) * C],
                                                     start=(j + f == 0), stop=(j + f == FT))
                    if u % 2:
                        last_.then_inc(s_dn, 1)

            yT(0)
            with pe.Fori(0, NBLK - 1) as k:
                block_(k)
            block_(NBLK - 1, last=True)


OVERFLOW = 3.4028234663852886e38 / FP8_EDGE


_INS = ['x', 'ctx_512', 'g_xattn', 'g_ffn', 'L0_xattn_q_norm_w', 'L0_xattn_k_norm_w', 'L0_xattn_w_out',
        'L0_ffn_router_scale', 'L0_ffn_gate_w', 'L0_ffn_gate_up', 'L0_ffn_down', 'L0_ffn_per_expert_scale',
        'L1_xattn_Wq', 'L1_xattn_w_kc_q', 'L1_xattn_w_kc_kv', 'L1_xattn_W_qr', 'L1_xattn_W_kr', 'L1_xattn_Wo',
        'L1_ffn_gate_w', 'L1_ffn_up_w', 'L1_ffn_down_w', 'L1_ffn_gate_scale', 'L1_ffn_up_scale', 'L1_ffn_down_scale']


def constants():
    import numpy as np

    c = np.zeros((P, C_END), np.float32)
    p = np.arange(P)
    c[:, C_ID:C_ID + P] = np.eye(P, dtype=np.float32)
    causal = np.arange(S)[None, :] > (p % S)[:, None]
    c[:, C_MASK:C_MASK + 512] = np.tile(np.where(causal, np.float32(-1e30), np.float32(0)), (1, 8))
    c[p, C_NSEL + (p // HD) % 4] = 1
    c[p, C_HALF + p // S] = 1
    pos = np.arange(S, dtype=np.float32)

    def table(dim, order):
        inv = (np.float32(1) / np.float32(10000.0) ** (np.arange(0, dim, 2, dtype=np.float32) / np.float32(dim)))
        f = pos[:, None] * inv.astype(np.float32)[None, :]
        cos, sin = np.cos(f)[:, order], np.sin(f)[:, order]
        sin[:, :dim // 2] = -sin[:, :dim // 2]
        return np.tile(cos, (2, 1)), np.tile(sin, (2, 1))

    c[:, C_COS0:C_COS0 + HD], c[:, C_SIN0:C_SIN0 + HD] = table(HD, np.tile(np.arange(HD // 2), 2))
    c[:, C_COS1:C_COS1 + DCTX], c[:, C_SIN1:C_SIN1 + DCTX] = table(DCTX, np.repeat(np.arange(DCTX // 2), 2))
    c[:, C_IOTA:C_IOTA + NE] = np.arange(NE)
    return c


def kernel(**inputs):
    import numpy as _np
    import concourse.bacc as _bacc
    from concourse import mybir as _mybir
    from concourse.bass_utils import run_bass_kernel_spmd as _run

    nc = _bacc.Bacc("TRN2", target_bir_lowering=False, num_devices=1)
    arrays, aps = {}, {}
    for name in _INS + ["const"]:
        v = constants() if name == "const" else _np.ascontiguousarray(inputs[name])
        arrays[f"in_{name}_dram"] = v
        aps[name] = nc.dram_tensor(f"in_{name}_dram", v.shape, _mybir.dt.from_np(v.dtype), kind="ExternalInput").ap()
    out = nc.dram_tensor("out_0_dram", (B, S, C), FP32, kind="ExternalOutput").ap()
    stack_kernel(nc, aps, out)
    r = _run(nc, [arrays], core_ids=[0])
    return r.results[0]["out_0_dram"]
```

```python
import concourse.bass as bass
from concourse import mybir
from contextlib import ExitStack

FP32 = mybir.dt.float32
F32R = mybir.dt.float32r
BF16 = mybir.dt.bfloat16
I32 = mybir.dt.int32
U32 = mybir.dt.uint32
ALU = mybir.AluOpType
ACT = mybir.ActivationFunctionType
AX = mybir.AxisListType

B, S, C, DCTX = 32, 64, 256, 64
P = 128
NT = B * S // P
NBLK, TPB = NT // 4, 4
BT = TPB * P
CT = C // P
H, HD, KVH = 16, 16, 4
NE, ED = 8, 256
KD, DCQ, R = 128, 192, 64
FI, FT = 768, 768 // 128
GH = 4
LN_EPS, RMS_EPS, ROUTER_EPS = 1e-5, 1e-5, 1e-6
FP8_EDGE = 464.0

C_ID, C_NSEL, C_COS0, C_SIN0, C_COS1, C_SIN1, C_IOTA, C_HALF = 0, 128, 132, 148, 164, 228, 292, 300
C_END = C_HALF + 2


def bc(ap, axis, n):
    shape = list(ap.shape)
    shape.insert(axis, n)
    return ap.unsqueeze(axis).broadcast_to(shape)



def normed_tile(nc, g, t, u):
    return nc.vector.tensor_scalar(g["y"][:, u], g["x"][:, t, :], g["mean"][:, at(t)], g["r"][:, 0, at(t)],
                                   ALU.subtract, ALU.mult)


def transpose_y(nc, g, pe, ps, ident, s_yn, s_yt, n):
    for u in range(TPB):
        pe.wait_ge(s_yn, TPB * n + (u + 1))
        for c in range(CT):
            last = nc.tensor.transpose(ps[:, c, u * P:(u + 1) * P], g["y"][:, u, c * P:(c + 1) * P], ident)
    last.then_inc(s_yt, 1)


def at(t):
    return slice(t, t + 1) if isinstance(t, int) else bass.ds(t, 1)


class Link:

    def __init__(self, eng, sem, base=0):
        self.eng, self.sem, self.base, self.n = eng, sem, base, 0

    def __call__(self, ins):
        ins.then_inc(self.sem, 1)
        self.n += 1
        self.eng.wait_ge(self.sem, self.base + self.n)


def rsqrt(eng, link, y, v, tmp, fused=False):
    estimate = 0x5F3759DF - (3 << 23) - (1 << 31)
    link(eng.tensor_scalar(y.bitcast(I32), v.bitcast(I32), -0.5, float(estimate), ALU.mult, ALU.add))
    for i in range(3):
        if fused:
            link(eng.scalar_tensor_tensor(tmp, v, 4.0 ** (3 - i), y, ALU.mult, ALU.mult))
            link(eng.tensor_tensor(tmp, tmp, y, ALU.mult))
            link(eng.scalar_tensor_tensor(y, tmp, -3.0, y, ALU.add, ALU.mult))
            continue
        link(eng.tensor_tensor(tmp, v, y, ALU.mult))
        link(eng.tensor_tensor(tmp, tmp, y, ALU.mult))
        link(eng.tensor_scalar(tmp, tmp, 4.0 ** (3 - i), -3.0, ALU.mult, ALU.add))
        link(eng.tensor_tensor(y, y, tmp, ALU.mult))


def split_passes(hi, lo):
    return ((hi[0], hi[1]), (lo[0], hi[1]), (hi[0], lo[1]))


def ln_rstd(eng, g, link, first, end, second_eps=None, fused=False):
    ts = slice(first, end)
    bn, mean, var, r, r2 = g["bn"][:, ts], g["mean"][:, ts], g["var"][:, ts], g["r"][:, :, ts], g["r2"][:, ts]
    v, tmp = g["ta"][:, :, ts], g["tb"][:, :, ts]
    d = v[:, 0]
    link(eng.tensor_tensor(d, bn[:, :, 1], bn[:, :, 4], ALU.subtract))
    link(eng.tensor_tensor(var, bn[:, :, 2], bn[:, :, 5], ALU.add))
    link(eng.tensor_tensor(mean, bn[:, :, 1], bn[:, :, 4], ALU.add))
    link(eng.tensor_tensor(d, d, d, ALU.mult))
    link(eng.tensor_scalar(mean, mean, 0.5, None, ALU.mult))
    link(eng.tensor_scalar(var, var, 1.0 / C, None, ALU.mult))
    link(eng.tensor_scalar(d, d, 0.25, None, ALU.mult))
    link(eng.tensor_tensor(var, var, d, ALU.add))
    link(eng.tensor_scalar(v[:, 0], var, LN_EPS, None, ALU.add))
    if second_eps is None:
        rsqrt(eng, link, r[:, 0], v[:, 0], tmp[:, 0])
    else:
        link(eng.tensor_scalar(v[:, 1], var, 1.0 + second_eps, LN_EPS * second_eps, ALU.mult, ALU.add))
        rsqrt(eng, link, r, v, tmp, fused)
        link(eng.tensor_tensor(v[:, 0], v[:, 0], r[:, 0], ALU.mult))
        link(eng.tensor_tensor(r2, v[:, 0], r[:, 1], ALU.mult))


def stack_kernel(nc, a, out):
    top = ExitStack()

    def scope(stack, phase=""):
        def sb(name, shape, dt=FP32):
            return stack.enter_context(nc.sbuf_tensor(phase + name, shape, dt))

        def pb(name, shape, dt=FP32):
            return stack.enter_context(nc.psum_tensor(phase + name, shape, dt))

        def sem(name):
            return stack.enter_context(nc.semaphore(phase + name))

        return sb, pb, sem

    with top:
        sb, _, _ = scope(top)
        g = {
            "x": sb("x_res", [P, NT, C]),
            "const": sb("const", [P, C_END]),
            "ctxdup": sb("ctxdup", [P, B, DCTX]),
            "y": sb("y", [P, TPB, C]),
            "yhi": sb("yT_hi", [P, CT, BT], F32R),
            "ylo": sb("yT_lo", [P, CT, BT], F32R),
            "mhi": sb("m_hi", [P, CT, H * DCTX], F32R),
            "mlo": sb("m_lo", [P, CT, H * DCTX], F32R),
            "pm": sb("p_out", [P, H // 2, C]),
            "tg": sb("tanh_gates", [P, 4]),
            "gws": sb("router_hi_lo", [P, CT, 2, NE], F32R),
            "pes": sb("expert_scale", [P, NE]),
            "fgs": sb("ffn_gate_scale", [P, FT]),
            "fus": sb("ffn_up_scale", [P, FT]),
            "dsg": sb("ffn_down_scale", [P, C]),
            "bn": sb("bn_stats", [P, NT, 6]),
            "mean": sb("mean", [P, NT]),
            "var": sb("variance", [P, NT]),
            "r": sb("rstd", [P, 2, NT]),
            "r2": sb("second_rstd", [P, NT]),
            "ta": sb("small_a", [P, 2, NT]),
            "tb": sb("small_b", [P, 2, NT]),
        }
        with ExitStack() as es:
            sbm, _, _ = scope(es)
            g["whi"] = sbm("moe_hi", [P, NE, 1536], F32R)
            g["wlo"] = sbm("moe_lo", [P, NE, 1536], F32R)
            with ExitStack() as es0:
                sb0, _, _ = scope(es0)
                g["maskb"] = sb0("identity_mask_bf16", [P, P + 512], BF16)
                g["kr"] = sb0("k_roped", [P, NT, DCTX])
                g["gw"] = sb0("router_w", [P, CT, NE])
                g["rsc"] = sb0("router_scale", [P, CT])
                g["woutT"] = sb0("woutT", [P, 2, C])
                g["cqw"] = sb0("cos_qw", [P, C])
                g["sqw"] = sb0("sin_qw", [P, C])
                with ExitStack() as es2:
                    setup_phase(nc, a, g, *scope(es2, "setup_"))
                with ExitStack() as es2:
                    attn0_phase(nc, a, g, *scope(es2, "attn0_"))
            with ExitStack() as es2:
                moe_phase(nc, a, g, *scope(es2, "moe_"))
        g["wq8"] = sb("ffn_w", [P, 3 * 1536], F32R)
        with ExitStack() as es:
            attn1_phase(nc, a, g, *scope(es, "attn1_"))
        with ExitStack() as es:
            ffn_phase(nc, a, g, out, *scope(es, "ffn_"))


def setup_phase(nc, a, g, sb, pb, sem):
    ident = g["const"][:, C_ID:C_ID + P]
    ctx = sb("ctx_tok", [P, NT, DCTX])
    kn = sb("k_normed", [P, NT, DCTX])
    rk = sb("k_rstd", [P, NT])
    ms = sb("k_mean_sq", [P, NT])
    tmp = sb("newton", [P, NT])
    kt1 = sb("k_cos", [P, NT, DCTX])
    kt2 = sb("k_sin", [P, NT, DCTX])
    qw = sb("q_norm_b", [P, C])
    kw = sb("k_norm_b", [P, DCTX])
    ckw = sb("cos_kw", [P, DCTX])
    skw = sb("sin_kw", [P, DCTX])
    wout = sb("w_out", [P, 2, C])
    graw = sb("gates_raw", [P, 4])
    gw, rsc = g["gw"], g["rsc"]
    mask = sb("mask", [P, 512])
    ps_w = pb("ps_woutT", [P, 512])

    s_const, s_ctx, s_dup = sem("const_in"), sem("ctx_in"), sem("ctxdup_in")
    s_x, s_mask = [sem(f"x_in{q}") for q in range(4)], sem("mask_in")
    s_nw, s_wo, s_small = sem("norm_w_in"), sem("w_out_in"), sem("small_in")
    s_wt, s_v, s_g, s_kw = sem("woutT_ps"), sem("dve_step"), sem("pool_step"), sem("k_scales_ready")

    with nc.Block() as block:

        @block.sync
        def _(sp):
            sp.dma_start(ctx[:], a["ctx_512"].rearrange("(t b) s c -> (b s) t c", b=2)).then_inc(s_ctx, 16)
            xv = a["x"].rearrange("(t b) s c -> (b s) t c", b=2)
            for q in range(4):
                sp.dma_start(g["x"][:, 4 * q:4 * q + 4], xv[:, 4 * q:4 * q + 4]).then_inc(s_x[q], 16)
            for d in range(2):
                sp.dma_start(g["ctxdup"][64 * d:64 * d + 64], a["ctx_512"].rearrange("b k c -> k b c")).then_inc(s_dup, 16)

        @block.scalar
        def _(act):
            act.dma_start(g["const"][:], a["const"]).then_inc(s_const, 16)
            act.dma_start(qw[:], a["L0_xattn_q_norm_w"].partition_broadcast(P)).then_inc(s_nw, 16)
            act.dma_start(kw[:], a["L0_xattn_k_norm_w"].partition_broadcast(P)).then_inc(s_nw, 16)
            wv = a["L0_xattn_w_out"].rearrange("(t o) (ct g2 nd) -> t g2 o ct nd", o=P, ct=2, g2=2)
            for ot in range(2):
                for g2 in range(2):
                    dst = wout[:, ot, g2 * P:(g2 + 1) * P].rearrange("p (ct nd) -> p ct nd", ct=2)
                    act.dma_start(dst, wv[ot, g2]).then_inc(s_wo, 16)
            act.dma_start(mask[:], a["mask"]).then_inc(s_mask, 16)
            act.dma_start(graw[:, 0:2], a["g_xattn"].partition_broadcast(P)).then_inc(s_small, 16)
            act.dma_start(graw[:, 2:4], a["g_ffn"].partition_broadcast(P)).then_inc(s_small, 16)
            act.dma_start(gw[:], a["L0_ffn_gate_w"].rearrange("(t p) e -> p t e", p=P)).then_inc(s_small, 16)
            act.dma_start(rsc[:], a["L0_ffn_router_scale"].rearrange("(t p) -> p t", p=P),
                          allow_slow_non_contiguous=True).then_inc(s_small, 16)
            act.dma_start(g["pes"][:], a["L0_ffn_per_expert_scale"].partition_broadcast(P)).then_inc(s_small, 16)
            act.dma_start(g["fgs"][:], a["L1_ffn_gate_scale"].rearrange("(t p) -> p t", p=P),
                          allow_slow_non_contiguous=True).then_inc(s_small, 16)
            act.dma_start(g["fus"][:], a["L1_ffn_up_scale"].rearrange("(t p) -> p t", p=P),
                          allow_slow_non_contiguous=True).then_inc(s_small, 16)
            act.dma_start(g["dsg"][:], a["L1_ffn_down_scale"].partition_broadcast(P)).then_inc(s_small, 16)
            act.wait_ge(s_const, 16)
            act.activation(g["maskb"][:, 0:P], ident, ACT.Copy)
            act.wait_ge(s_mask, 16)
            act.activation(g["maskb"][:, P:P + 512], mask[:], ACT.Copy)
            act.wait_ge(s_wt, 1)
            act.activation(g["woutT"][:], ps_w[:], ACT.Copy)
            act.wait_ge(s_small, 8 * 16)
            act.activation(g["tg"][:], graw[:], ACT.Tanh)

        @block.tensor
        def _(pe):
            pe.wait_ge(s_const, 16)
            pe.wait_ge(s_wo, 4 * 16)
            for g2 in range(2):
                for ot in range(2):
                    last = nc.tensor.transpose(ps_w[:, (2 * g2 + ot) * P:(2 * g2 + ot + 1) * P],
                                               wout[:, ot, g2 * P:(g2 + 1) * P], ident)
            last.then_inc(s_wt, 1)

        @block.vector
        def _(dve):
            link = Link(dve, s_v)
            dve.wait_ge(s_ctx, 16)
            link(nc.vector.tensor_tensor(kn[:], ctx[:], ctx[:], ALU.mult))
            link(nc.vector.tensor_reduce(ms[:], kn[:], AX.X, ALU.add))
            link(nc.vector.tensor_scalar(ms[:], ms[:], 1.0 / DCTX, RMS_EPS, ALU.mult, ALU.add))
            rsqrt(nc.vector, link, rk[:], ms[:], tmp[:], fused=True)
            dve.wait_ge(s_const, 16)
            dve.wait_ge(s_nw, 32)
            cos0, sin0 = g["const"][:, C_COS0:C_COS0 + HD], g["const"][:, C_SIN0:C_SIN0 + HD]
            for w, nh, cw, sw in ((qw, H, g["cqw"], g["sqw"]), (kw, KVH, ckw, skw)):
                wv, cv, sv = (t[:].rearrange("p (h d) -> p h d", d=HD) for t in (w, cw, sw))
                nc.vector.tensor_tensor(cv, wv, bc(cos0, 1, nh), ALU.mult)
                nc.vector.tensor_tensor(sv[:, :, 0:8], wv[:, :, 8:16], bc(sin0[:, 0:8], 1, nh), ALU.mult)
                link(nc.vector.tensor_tensor(sv[:, :, 8:16], wv[:, :, 0:8], bc(sin0[:, 8:16], 1, nh), ALU.mult))
            dve.sem_inc(s_kw, 1)
            for q in range(4):
                dve.wait_ge(s_x[q], 16)
                for t in range(4 * q, 4 * q + 4):
                    last = nc.vector.bn_stats(g["bn"][:, t, :], g["x"][:, t, :])
            link(last)
            ln_rstd(nc.vector, g, link, 0, NT, RMS_EPS, fused=True)

        @block.gpsimd
        def _(pool):
            link = Link(pool, s_g)
            pool.wait_ge(s_ctx, 16)
            pool.wait_ge(s_kw, 1)
            link(nc.gpsimd.tensor_tensor(kn[:], ctx[:], bc(rk[:], 2, DCTX), ALU.mult))
            link(nc.gpsimd.tensor_tensor(kt1[:], kn[:], bc(ckw[:], 1, NT), ALU.mult))
            k4, s4 = (v.rearrange("p t (h d) -> p t h d", d=HD) for v in (kn[:], kt2[:]))
            w4 = bc(skw[:].rearrange("p (h d) -> p h d", d=HD), 1, NT)
            link(nc.gpsimd.tensor_tensor(s4[:, :, :, 0:8], k4[:, :, :, 8:16], w4[:, :, :, 0:8], ALU.mult))
            link(nc.gpsimd.tensor_tensor(s4[:, :, :, 8:16], k4[:, :, :, 0:8], w4[:, :, :, 8:16], ALU.mult))
            link(nc.gpsimd.tensor_tensor(g["kr"][:], kt1[:], kt2[:], ALU.add))
            pool.wait_ge(s_dup, 32)


def attn0_phase(nc, a, g, sb, pb, sem):
    ident = g["const"][:, C_ID:C_ID + P]
    VW = HD + 1
    HH = H // 2
    qn = sb("q_normed", [P, C])
    qc = sb("q_cos", [P, C])
    qs = sb("q_sin", [P, C])
    qr = sb("q_roped", [P, C])
    krep = sb("k_repeated", [P, KVH, 4, HD])
    qT = sb("qT", [P, 2, P])
    kbd = sb("k_blockdiag", [P, 4, 4, S])
    pr_ = sb("probs", [P, H, S])
    pT = sb("probsT", [P, H // 2, P])
    vbd = sb("v_blockdiag", [P, 2, KVH, 2 * VW])
    on = sb("heads_out", [P, H, HD])
    oT = sb("heads_outT", [P, 2, P])
    mx = sb("score_max", [P, H])
    rec = sb("sum_recip", [P, H])
    stage = sb("moe_stage", [P, 1536])
    ps_s = pb("ps_scores", [P, 2, 512])
    ps_pT = pb("ps_probsT", [P, H // 2, P])
    ps_qk = pb("ps_qkT", [P, 4, P])
    ps_o = pb("ps_heads", [P, 512])
    ps_oT = pb("ps_headsT", [P, 512])
    ps_y = pb("ps_y", [P, 512])
    pso = ps_o[:, 0:H * VW]
    yT_banks = ps_pT[:].rearrange("p (c q) k -> p c (q k)", c=CT)

    s_qn, s_qc, s_rot, s_qr = sem("q_normed"), sem("q_cos"), sem("q_rotated"), sem("q_roped")
    s_k, s_vb, s_v0 = sem("k_repeated"), sem("v_ready"), sem("v_ones")
    s_qkT, s_qkE, s_sc, s_mx = sem("qk_transposed"), sem("qk_in_sbuf"), sem("scores_ready"), sem("max_ready")
    s_sh, s_pr, s_pT, s_pTe = sem("scores_shifted"), sem("probs_ready"), sem("probs_transposed"), sem("probsT_in_sbuf")
    s_pv, s_rec, s_on = sem("heads_ready"), sem("recip_ready"), sem("heads_normed")
    s_oT, s_oTe, s_y, s_x = sem("heads_transposed"), sem("headsT_in_sbuf"), sem("y_ready"), sem("x_updated")
    s_yn, s_yt, s_yh = sem("y_normed"), sem("y_transposed"), sem("y_hi")
    s_bn, s_rs, s_rd, s_small = sem("statistics"), sem("rstd_step"), sem("rstd_ready"), sem("small_step")
    s_wl, s_whi, s_wlo = ([sem(f"{n}_{w}") for n in ("gate_up", "down")] for w in ("loaded", "hi", "lo"))
    part = (slice(0, 1024), slice(1024, 1536))

    with nc.Block() as block:

        @block.sync
        def _(sp):
            srcs = [a[n].rearrange("e (t p) f -> e p t f", p=P) for n in ("L0_ffn_gate_up", "L0_ffn_down")]

            def load(e, j):
                st = stage[:, part[j]].rearrange("p (t f) -> p t f", t=2)
                sp.dma_start(st, srcs[j][bass.ds(e, 1)].rearrange("e p t f -> (e p) t f")).then_inc(s_wl[j], 16)

            load(0, 0)
            load(0, 1)
            with sp.Fori(1, NE) as e:
                sp.wait_ge(s_wlo[0], 2 * e)
                load(e, 0)
                sp.wait_ge(s_wlo[1], e)
                load(e, 1)

        @block.gpsimd
        def _(pool):
            half = g["const"][:, C_HALF:C_HALF + 2]

            def rotate(t):
                pool.wait_ge(s_qn, t + 1)
                q, s, w = (v[:].rearrange("p (h d) -> p h d", d=HD) for v in (qn, qs, g["sqw"]))
                nc.gpsimd.tensor_tensor(s[:, :, 0:8], q[:, :, 8:16], w[:, :, 0:8], ALU.mult).then_inc(s_rot, 1)
                nc.gpsimd.tensor_tensor(s[:, :, 8:16], q[:, :, 0:8], w[:, :, 8:16], ALU.mult).then_inc(s_rot, 1)

            def repeat_k(t, first=False):
                if not first:
                    pool.wait_ge(s_qkT, t)
                kv = g["kr"][:, t, :].rearrange("p (g d) -> p g d", d=HD)
                nc.gpsimd.tensor_copy(krep[:], bc(kv, 2, 4)).then_inc(s_k, 1)

            def values(t, first=False):
                if not first:
                    pool.wait_ge(s_pv, t)
                dst = vbd[:].rearrange("p b g (h w) -> p (b g) h w", w=VW)[:, :, :, 0:HD]
                src = g["ctxdup"][:, bass.ds(2 * t, 2), :].rearrange("p b (g d) -> p (b g) d", d=HD)
                nc.gpsimd.tensor_tensor(dst, bc(src, 2, 2), bc(bc(half, 1, 2 * KVH), 3, HD), ALU.mult).then_inc(s_vb, 1)

            def expert(e, piece):
                j = piece // 2
                cols = slice(512 * piece, 512 * (piece + 1))
                pool.wait_ge(s_whi[j], e + 1)
                nc.gpsimd.tensor_tensor(g["wlo"][:, e, cols], stage[:, cols], g["whi"][:, e, cols].bitcast(FP32),
                                        ALU.subtract).then_inc(s_wlo[j], 1)

            ones = vbd[:].rearrange("p b g (h w) -> p (b g) h w", w=VW)[:, :, :, HD]
            nc.gpsimd.tensor_copy(ones, bc(half, 1, 2 * KVH)).then_inc(s_v0, 1)
            repeat_k(0, first=True)
            rotate(0)
            repeat_k(1)
            rotate(1)
            rotate(2)

            def step(t, e, pieces, first=False, rope=True):
                repeat_k(t + 2)
                values(t, first)
                expert(e, pieces[0])
                if rope:
                    rotate(t + 3)
                for piece in pieces[1:]:
                    expert(e, piece)

            step(0, 0, (0, 1), first=True)
            with pool.Fori(0, 6) as i:
                step(2 * i + 1, i, (2,))
                step(2 * i + 2, i + 1, (0, 1))
            step(13, 6, (2,), rope=False)
            values(14)
            pool.wait_ge(s_bn, NT - TPB)
            ln_rstd(nc.gpsimd, g, Link(pool, s_rs), 0, NT - TPB, ROUTER_EPS)
            pool.sem_inc(s_rd, 1)
            values(15)
            for piece in range(3):
                expert(7, piece)
            link = Link(pool, s_small)
            gw, hi, lo = g["gw"], g["gws"][:, :, 0], g["gws"][:, :, 1]
            for t in range(CT):
                link(nc.gpsimd.tensor_scalar(gw[:, t], gw[:, t], g["rsc"][:, t:t + 1], float(C) ** -0.5, ALU.mult, ALU.mult))
            link(nc.gpsimd.tensor_copy(hi, gw[:]))
            link(nc.gpsimd.tensor_tensor(lo, gw[:], hi.bitcast(FP32), ALU.subtract))
            link(nc.gpsimd.tensor_scalar(g["pes"][:], g["pes"][:], g["tg"][:, 2:3], None, ALU.mult))
            link(nc.gpsimd.tensor_scalar(g["dsg"][:], g["dsg"][:], g["tg"][:, 3:4], None, ALU.mult))

        @block.vector
        def _(dve):
            def rope_norm(t, first=False):
                if not first:
                    dve.wait_ge(s_qr, t)
                nc.vector.tensor_scalar(qn[:], g["x"][:, t, :], g["mean"][:, bass.ds(t, 1)], g["r"][:, 1, bass.ds(t, 1)],
                                        ALU.subtract, ALU.mult).then_inc(s_qn, 1)
                dve.wait_ge(s_qn, t + 1)
                nc.vector.tensor_tensor(qc[:], qn[:], g["cqw"][:], ALU.mult).then_inc(s_qc, 1)

            def rope_sum(t, first=False):
                dve.wait_ge(s_qc, t + 1)
                dve.wait_ge(s_rot, 2 * (t + 1))
                if not first:
                    dve.wait_ge(s_qkT, t)
                nc.vector.tensor_tensor(qr[:], qc[:], qs[:], ALU.add).then_inc(s_qr, 1)

            def shift(t, j):
                n = 2 * t + j + 1
                if not isinstance(n, int):
                    n = dve.snap(n)
                dve.wait_ge(s_sc, n)
                hs = slice(HH * j, HH * (j + 1))
                sv = ps_s[:, j].rearrange("p (h k) -> p h k", k=S)
                nc.vector.tensor_reduce(mx[:, hs], sv, AX.X, ALU.max).then_inc(s_mx, 1)
                dve.wait_ge(s_mx, n)
                nc.vector.tensor_tensor(pr_[:, hs], sv, bc(mx[:, hs], 2, S), ALU.subtract).then_inc(s_sh, 1)

            def finish(t):
                dve.wait_ge(s_pv, t + 1)
                ov = pso.rearrange("p (h w) -> p h w", w=VW)
                nc.vector.reciprocal(rec[:], ov[:, :, HD]).then_inc(s_rec, 1)
                dve.wait_ge(s_rec, t + 1)
                nc.vector.tensor_tensor(on[:], ov[:, :, 0:HD], bc(rec[:], 2, HD), ALU.mult).then_inc(s_on, 1)

            def residual(t):
                dve.wait_ge(s_y, t + 1)
                nc.vector.scalar_tensor_tensor(g["x"][:, t, :], ps_y[:, 0:C], g["tg"][:, 0:1], g["x"][:, t, :],
                                               ALU.mult, ALU.add).then_inc(s_x, 1)
                dve.wait_ge(s_x, t + 1)
                nc.vector.bn_stats(g["bn"][:, t, :], g["x"][:, t, :]).then_inc(s_bn, 1)

            rope_norm(0, first=True)
            rope_sum(0, first=True)
            rope_norm(1)
            rope_sum(1)
            rope_norm(2)
            shift(0, 0)
            shift(0, 1)

            def step(t, first=False, rope=True, next_rope=True, scores=True, last=False):
                if rope:
                    rope_sum(t + 2)
                if scores:
                    shift(t + 1, 0)
                    shift(t + 1, 1)
                if not first:
                    residual(t - 1)
                if last:
                    dve.wait_ge(s_rd, 1)
                    for u in range(TPB):
                        normed_tile(nc, g, u, u).then_inc(s_yn, 1)
                finish(t)
                if next_rope:
                    rope_norm(t + 3)

            step(0, first=True)
            with dve.Fori(1, NT - 3) as t:
                step(t)
            step(NT - 3, next_rope=False)
            step(NT - 2, rope=False, next_rope=False)
            step(NT - 1, rope=False, next_rope=False, scores=False, last=True)
            dve.wait_ge(s_yh, 1)
            nc.vector.tensor_tensor(g["ylo"][:], yT_banks, g["yhi"][:].bitcast(FP32), ALU.subtract)
            residual(NT - 1)

        @block.scalar
        def _(act):
            def qk(t, part):
                if part == 0:
                    act.wait_ge(s_qkT, t + 1)
                    nc.scalar.activation(qT[:], ps_qk[:, 0:2], ACT.Copy)
                for n in ((0,), (1, 2, 3))[part]:
                    sel = g["const"][:, C_NSEL + n:C_NSEL + n + 1]
                    last = nc.scalar.activation(kbd[:, :, n, :], ps_qk[:, 2:4].rearrange("p c (b k) -> p (c b) k", b=2),
                                                ACT.Copy, scale=sel)
                if part == 1:
                    last.then_inc(s_qkE, 1)

            def exps(t, j):
                act.wait_ge(s_sh, 2 * t + j + 1)
                hs = slice(HH * j, HH * (j + 1))
                nc.scalar.activation(pr_[:, hs], pr_[:, hs], ACT.Exp, scale=float(HD) ** -0.5).then_inc(s_pr, 1)

            def probsT(t):
                act.wait_ge(s_pT, t + 1)
                nc.scalar.activation(pT[:], ps_pT[:], ACT.Copy).then_inc(s_pTe, 1)

            def headsT(t):
                act.wait_ge(s_oT, t + 1)
                nc.scalar.activation(oT[:], ps_oT[:, 0:2 * P], ACT.Copy).then_inc(s_oTe, 1)

            def expert(e, j):
                act.wait_ge(s_wl[j], 16 * (e + 1))
                nc.scalar.activation(g["whi"][:, e, part[j]], stage[:, part[j]], ACT.Copy).then_inc(s_whi[j], 1)

            def step(t, e, j, first=False, scores=True, keys=True):
                probsT(t)
                if not first:
                    headsT(t - 1)
                expert(e, j)
                if scores:
                    exps(t + 1, 0)
                if keys:
                    qk(t + 2, 0)
                if scores:
                    exps(t + 1, 1)
                if keys:
                    qk(t + 2, 1)

            qk(0, 0)
            qk(0, 1)
            exps(0, 0)
            qk(1, 0)
            exps(0, 1)
            qk(1, 1)
            step(0, 0, 0, first=True)
            with act.Fori(0, 6) as i:
                step(2 * i + 1, i, 1)
                step(2 * i + 2, i + 1, 0)
            step(13, 6, 1)
            step(14, 7, 0, keys=False)
            step(15, 7, 1, scores=False, keys=False)
            act.wait_ge(s_yt, 1)
            nc.scalar.activation(g["yhi"][:], yT_banks, ACT.Copy).then_inc(s_yh, 1)
            headsT(15)

        @block.tensor
        def _(pe):
            def qkT(t):
                pe.wait_ge(s_qr, t + 1)
                pe.wait_ge(s_k, t + 1)
                kr = krep[:].rearrange("p g n d -> p (g n d)")
                for c in range(2):
                    nc.tensor.transpose(ps_qk[:, c], qr[:, c * P:(c + 1) * P], ident)
                for c in range(2):
                    last = nc.tensor.transpose(ps_qk[:, 2 + c], kr[:, c * P:(c + 1) * P], ident)
                last.then_inc(s_qkT, 1)

            def scores(t):
                pe.wait_ge(s_qkE, t + 1)
                for g2 in range(2):
                    nc.tensor.matmul(ps_s[:, g2], g["maskb"][:, 0:P], g["maskb"][:, P:P + 512], start=True, stop=False,
                                     skip_group_check=True)
                    for b2 in range(2):
                        for ct in range(2):
                            o = ct * 256
                            last = nc.tensor.matmul(ps_s[64 * b2:64 * b2 + 64, g2, o:o + 256],
                                                    qT[64 * g2:64 * g2 + 64, ct, 64 * b2:64 * b2 + 64],
                                                    kbd[64 * g2:64 * g2 + 64, 2 * ct + b2],
                                                    start=False, stop=True, skip_group_check=True)
                    last.then_inc(s_sc, 1)

            def probsT(t):
                pe.wait_ge(s_pr, 2 * t + 2)
                for q in range(H // 2):
                    last = nc.tensor.transpose(ps_pT[:, q], pr_[:, 2 * q:2 * q + 2].rearrange("p h k -> p (h k)"), ident)
                last.then_inc(s_pT, 1)

            def heads(t):
                pe.wait_ge(s_pTe, t + 1)
                pe.wait_ge(s_vb, t + 1)
                for b2 in range(2):
                    for q in range(H // 2):
                        kvh = 2 * ((q // 2) % 2) + q // 4
                        last = nc.tensor.matmul(pso[64 * b2:64 * b2 + 64, q * 2 * VW:(q + 1) * 2 * VW],
                                                pT[:, q, 64 * b2:64 * b2 + 64], vbd[:, b2, kvh],
                                                start=True, stop=True)
                last.then_inc(s_pv, 1)

            def headsT(t):
                pe.wait_ge(s_on, t + 1)
                ov = on[:].rearrange("p (c h) d -> p c (h d)", c=2)
                for c in range(2):
                    last = nc.tensor.transpose(ps_oT[:, c * P:(c + 1) * P], ov[:, c], ident)
                last.then_inc(s_oT, 1)

            def project(t):
                pe.wait_ge(s_oTe, t + 1)
                for c in range(2):
                    last = nc.tensor.matmul(ps_y[:, 0:C], oT[:, c], g["woutT"][:, c], start=(c == 0), stop=(c == 1))
                last.then_inc(s_y, 1)

            def step(t, first=False, next_scores=True, keys=True):
                probsT(t)
                if not first:
                    headsT(t - 1)
                if next_scores:
                    scores(t + 1)
                if not first:
                    project(t - 1)
                if keys:
                    qkT(t + 2)
                heads(t)

            pe.wait_ge(s_v0, 1)
            qkT(0)
            scores(0)
            qkT(1)
            step(0, first=True)
            with pe.Fori(1, NT - 2) as t:
                step(t)
            step(NT - 2, keys=False)
            step(NT - 1, next_scores=False, keys=False)
            transpose_y(nc, g, pe, yT_banks, ident, s_yn, s_yt, 0)
            headsT(NT - 1)
            project(NT - 1)


def moe_phase(nc, a, g, sb, pb, sem):
    ident = g["const"][:, C_ID:C_ID + P]
    y, yhi, ylo = g["y"], g["yhi"], g["ylo"]
    gl = sb("gelu", [P, 2, BT])
    ac = sb("act", [P, 2, BT])
    ahi = sb("act_hi", [P, 2, 2, BT], F32R)
    alo = sb("act_lo", [P, 2, 2, BT], F32R)
    lg = sb("logits", [P, TPB, NE])
    pb_ = sb("router_probs", [P, TPB, NE])
    m4 = sb("router_max", [P, TPB])
    s4 = sb("router_sum", [P, TPB])
    top8 = sb("top8", [P, TPB, 8])
    ix8 = sb("top8_index", [P, TPB, 8], U32)
    ixf = sb("top8_indexf", [P, TPB, 8])
    tw = sb("top_w", [P, TPB, 2])
    c0 = sb("comb0", [P, TPB, NE])
    c1 = sb("comb1", [P, TPB, NE])
    comb = sb("comb", [P, TPB, NE])
    wkcq = sb("w_kc_q", [P, GH, DCQ])
    wqr = sb("w_qr", [96, 2, GH, R])
    wkr = sb("w_kr", [DCTX, GH, R])
    wq = sb("w_q", [P, GH, C])
    wkv = sb("w_kc_kv", [P, GH, DCTX])
    wo = sb("w_o", [P, 2, GH * KD])
    derived = sb("products", [P, 1024])
    kcqT = derived[0:96, :].rearrange("p (t h k) -> p t h k", t=2, h=GH)
    woT = derived[:].rearrange("p (h c) -> p h c", h=GH)
    RB = 2
    kvc = sb("kv_cos", [P, RB, DCTX])
    kvs = sb("kv_sin", [P, RB, DCTX])
    s_rp, s_rw = sem("rope_step"), sem("rope_wait")
    krT = sb("krT", [P, 2, DCTX])
    a1T = sb("a1T", [P, 2, KD])
    a2 = sb("a2", [P, 2, 2, DCTX])
    ps_g = [pb(f"ps_gate{f}", [P, BT]) for f in range(2)]
    ps_u = [pb(f"ps_up{f}", [P, BT]) for f in range(2)]
    ps_t = pb("ps_yT", [P, CT, BT])
    ps_d = pb("ps_down", [P, TPB, C])

    s_bn, s_rs, s_rd = sem("statistics"), sem("rstd_step"), sem("rstd_ready")
    s_yn, s_yt, s_yh, s_yl = sem("y_normed"), sem("y_transposed"), sem("y_hi"), sem("y_lo")
    s_lg, s_rx, s_re = sem("logits_ready"), sem("router_shifted"), sem("router_exp")
    s_gu, s_gl, s_ac, s_ah, s_al = sem("gate_up_ready"), sem("gelu_ready"), sem("act_ready"), sem("act_hi"), sem("act_lo")
    s_dn, s_mix = sem("down_ready"), sem("mixed")
    s_rt, s_pw, s_wl = sem("router_step"), sem("router_wait"), sem("weights_loaded")
    s_mt, s_me = sem("products_ready"), sem("products_read")
    STEPS = 20
    LOADS = 7
    MT, ME = 5, 7

    with nc.Block() as block:

        @block.sync
        def _(sp):
            def load(gr):
                hs = bass.ds(GH * gr, GH)
                hk = bass.ds(KD * GH * gr, KD * GH)
                sp.dma_start(wkcq[:], a["L1_xattn_w_kc_q"][hs].rearrange("h k q -> k h q")).then_inc(s_wl, 16)
                for t in range(2):
                    src = a["L1_xattn_W_qr"][hs, 96 * t:96 * t + 96, :].rearrange("h q r -> q h r")
                    sp.dma_start(wqr[:, t], src).then_inc(s_wl, 16)
                sp.dma_start(wkr[:], a["L1_xattn_W_kr"][hs].rearrange("h d r -> d h r")).then_inc(s_wl, 16)
                src = a["L1_xattn_Wq"].rearrange("(h k) c -> k h c", k=KD)[:, hs, :]
                sp.dma_start(wq[:], src).then_inc(s_wl, 16)
                sp.dma_start(wkv[:], a["L1_xattn_w_kc_kv"][hs].rearrange("h k d -> k h d")).then_inc(s_wl, 16)
                src = a["L1_xattn_Wo"].rearrange("(t o) n -> o t n", o=P)[:, :, hk]
                sp.dma_start(wo[:], src).then_inc(s_wl, 16)

            load(0)
            with sp.Fori(1, NBLK) as k:
                sp.wait_ge(s_mt, MT * k)
                load(k)

        @block.gpsimd
        def _(pool):
            link = Link(pool, s_rs)
            ln_rstd(nc.gpsimd, g, link, NT - TPB, NT, ROUTER_EPS)
            pool.sem_inc(s_rd, 1)
            cos1, sin1 = (bc(g["const"][:, c:c + DCTX], 1, RB) for c in (C_COS1, C_SIN1))
            with pool.Fori(0, B // RB) as i:
                kv = g["ctxdup"][:, bass.ds(RB * i, RB), :]
                nc.gpsimd.tensor_tensor(kvs[:, :, 0:32], kv[:, :, 32:64], sin1[:, :, 0:32], ALU.mult).then_inc(s_rp, 1)
                nc.gpsimd.tensor_tensor(kvs[:, :, 32:64], kv[:, :, 0:32], sin1[:, :, 32:64], ALU.mult).then_inc(s_rp, 1)
                nc.gpsimd.tensor_tensor(kvc[:], kv, cos1, ALU.mult).then_inc(s_rp, 1)
                pool.wait_ge(s_rp, 4 * i + 3)
                pool.sem_inc(s_rw, 1)
                nc.gpsimd.tensor_tensor(kv, kvc[:], kvs[:], ALU.add).then_inc(s_rp, 1)
                pool.wait_ge(s_rp, 4 * i + 4)
                pool.sem_inc(s_rw, 1)
            pool.wait_ge(s_bn, NT - TPB)
            ln_rstd(nc.gpsimd, g, link, 0, NT - TPB)
            pool.sem_inc(s_rd, 1)

        @block.vector
        def _(dve):
            def normed(k):
                for u in range(TPB):
                    normed_tile(nc, g, TPB * k + u, u).then_inc(s_yn, 1)

            def low(n):
                dve.wait_ge(s_yh, n + 1)
                nc.vector.tensor_tensor(ylo[:], ps_t[:], yhi[:].bitcast(FP32), ALU.subtract).then_inc(s_yl, 1)

            def shift(k):
                link = Link(dve, s_rt, k * STEPS)
                r2 = bc(g["r2"][:, bass.ds(TPB * k, TPB)], 2, NE)
                dve.wait_ge(s_lg, k + 1)
                lv = ps_t[:, 0, 0:TPB * 2 * NE].rearrange("p (u j e) -> p j u e", j=2, e=NE)
                link(nc.vector.tensor_tensor(c1[:], lv[:, 0], r2, ALU.mult))
                link(nc.vector.tensor_tensor(lg[:], lv[:, 1], r2, ALU.mult))
                link(nc.vector.tensor_tensor(lg[:], lg[:], c1[:], ALU.add))
                link(nc.vector.tensor_reduce(m4[:], lg[:], AX.X, ALU.max))
                nc.vector.tensor_tensor(lg[:], lg[:], bc(m4[:], 2, NE), ALU.subtract).then_inc(s_rx, 1)

            def router(k):
                link = Link(dve, s_rt, k * STEPS + 4)
                dve.wait_ge(s_re, k + 1)
                link(nc.vector.tensor_reduce(s4[:], pb_[:], AX.X, ALU.add))
                link(nc.vector.reciprocal(m4[:], s4[:]))
                link(nc.vector.tensor_tensor(pb_[:], pb_[:], bc(m4[:], 2, NE), ALU.mult))
                dve.sem_inc(s_pw, 1)
                for u in range(TPB):
                    last = nc.vector.max(top8[:, u], pb_[:, u])
                link(last)
                link(nc.vector.tensor_tensor(s4[:], top8[:, :, 0], top8[:, :, 1], ALU.add))
                dve.sem_inc(s_pw, 1)
                for u in range(TPB):
                    last = nc.vector.max_index(ix8[:, u], top8[:, u], pb_[:, u])
                link(last)
                link(nc.vector.tensor_copy(ixf[:], ix8[:]))
                link(nc.vector.tensor_scalar(s4[:], s4[:], 1e-12, None, ALU.max))
                link(nc.vector.reciprocal(m4[:], s4[:]))
                link(nc.vector.tensor_tensor(tw[:], top8[:, :, 0:2], bc(m4[:], 2, 2), ALU.mult))
                iota = bc(g["const"][:, C_IOTA:C_IOTA + NE], 1, TPB)
                for c, j in ((c0, 0), (c1, 1)):
                    link(nc.vector.tensor_tensor(c[:], iota, bc(ixf[:, :, j], 2, NE), ALU.is_equal))
                    link(nc.vector.tensor_tensor(c[:], c[:], bc(tw[:, :, j], 2, NE), ALU.mult))
                link(nc.vector.tensor_tensor(c0[:], c0[:], c1[:], ALU.add))
                assert link.n == STEPS - 5, link.n

            def weights(k):
                nc.vector.tensor_tensor(comb[:], c0[:], bc(g["pes"][:], 1, TPB), ALU.mult).then_inc(s_rt, 1)
                dve.wait_ge(s_rt, STEPS * (k + 1))

            def mix(k, e):
                for u in range(TPB):
                    t = TPB * k + u
                    if u % 2 == 0:
                        dve.wait_ge(s_dn, 2 * NE * k + (2 * e + u // 2 + 1))
                    if e:
                        dve.wait_ge(s_mix, TPB * NE * k + (TPB * (e - 1) + u + 1))
                    nc.vector.scalar_tensor_tensor(g["x"][:, t, :], ps_d[:, u], comb[:, u, e:e + 1], g["x"][:, t, :],
                                                   ALU.mult, ALU.add).then_inc(s_mix, 1)

            def statistics(k):
                for u in range(TPB):
                    t = TPB * k + u
                    dve.wait_ge(s_mix, TPB * NE * k + (TPB * (NE - 1) + u + 1))
                    nc.vector.bn_stats(g["bn"][:, t, :], g["x"][:, t, :]).then_inc(s_bn, 1)

            def products(k, e):
                n = MT * k + (e + 1)
                if e == 0:
                    dve.wait_ge(s_mt, n)
                    nc.vector.tensor_copy(kcqT, ps_t[0:96].rearrange("p t (h k) -> p t h k", h=GH)).then_inc(s_me, 1)
                elif e == 1:
                    dve.wait_ge(s_mt, n)
                    nc.vector.tensor_copy(a1T[:], ps_t[:, 0, 0:2 * KD].rearrange("p (h k) -> p h k", h=2)).then_inc(s_me, 1)
                elif e == 3:
                    dve.wait_ge(s_mt, n)
                    nc.vector.tensor_copy(a2[:], ps_t[:, :, 0:2 * DCTX].rearrange("p h (q d) -> p h q d", q=2)).then_inc(s_me, 1)
                elif e == 4:
                    dve.wait_ge(s_me, ME * k + 6)
                    nc.vector.tensor_tensor(g["mlo"][:, :, bass.ds(k * 256, 256)], ps_t[:, 0].rearrange("p (t n) -> p t n", t=CT),
                                            g["mhi"][:, :, bass.ds(k * 256, 256)].bitcast(FP32),
                                            ALU.subtract).then_inc(s_me, 1)

            def act_(k, e, f, then_low=None):
                m = 2 * NE * k + (2 * e + f + 1)
                if not isinstance(m, int):
                    m = dve.snap(m)
                dve.wait_ge(s_gl, m)
                nc.vector.tensor_tensor(ac[:, f], gl[:, f], ps_u[f][:], ALU.mult).then_inc(s_ac, 1)
                if then_low is not None:
                    low(then_low)
                dve.wait_ge(s_ah, m)
                nc.vector.tensor_tensor(alo[:, e % 2, f], ac[:, f], ahi[:, e % 2, f].bitcast(FP32),
                                        ALU.subtract).then_inc(s_al, 1)

            def block_(k, last=False):
                for e in range(NE - 1):
                    act_(k, e + 1, 0)
                    act_(k, e + 1, 1, then_low=k if e == NE - 2 and not last else None)
                    products(k, e)
                    mix(k, e)
                    if e == 4 and last:
                        dve.wait_ge(s_rd, 2)
                    if e == 4:
                        normed(0 if last else k + 1)
                if last:
                    low(k)
                    mix(k, NE - 1)
                else:
                    shift(k + 1)
                    act_(k + 1, 0, 0)
                    router(k + 1)
                    act_(k + 1, 0, 1)
                    mix(k, NE - 1)
                if not last:
                    statistics(k)
                    weights(k + 1)

            act_(0, 0, 0)
            act_(0, 0, 1)
            shift(0)
            router(0)
            weights(0)
            dve.wait_ge(s_rd, 1)
            with dve.Fori(0, NBLK - 1) as k:
                block_(k)
            block_(NBLK - 1, last=True)

        @block.scalar
        def _(act):
            def high(n):
                act.wait_ge(s_yt, n + 1)
                nc.scalar.activation(yhi[:], ps_t[:], ACT.Copy).then_inc(s_yh, 1)

            def router(k):
                act.wait_ge(s_rx, k + 1)
                nc.scalar.activation(pb_[:], lg[:], ACT.Exp).then_inc(s_re, 1)

            def products(k, e):
                n = MT * k + (e + 1)
                if e == 1:
                    act.wait_ge(s_mt, n)
                    nc.scalar.activation(krT[:], ps_t[:, 1, 0:2 * DCTX], ACT.Copy).then_inc(s_me, 1)
                elif e == 2:
                    act.wait_ge(s_mt, n)
                    nc.scalar.activation(woT, ps_t[:].rearrange("p t (h c) -> p (t h) c", h=2), ACT.Copy).then_inc(s_me, 1)
                elif e == 4:
                    act.wait_ge(s_mt, n)
                    nc.scalar.activation(g["pm"][:, bass.ds(k * 2, 2), :], ps_t[:, 1].rearrange("p (t n) -> p t n", t=2), ACT.Copy)
                    nc.scalar.activation(g["mhi"][:, :, bass.ds(k * 256, 256)], ps_t[:, 0].rearrange("p (t n) -> p t n", t=CT),
                                         ACT.Copy).then_inc(s_me, 1)

            def act_(k, e, then_high=None):
                for f in range(2):
                    m = 2 * NE * k + (2 * e + f + 1)
                    if not isinstance(m, int):
                        m = act.snap(m)
                    act.wait_ge(s_gu, m)
                    nc.scalar.activation(gl[:, f], ps_g[f][:], ACT.Gelu).then_inc(s_gl, 1)
                    if f == 1 and then_high is not None:
                        high(then_high)
                    act.wait_ge(s_ac, m)
                    nc.scalar.activation(ahi[:, e % 2, f], ac[:, f], ACT.Copy).then_inc(s_ah, 1)

            def block_(k, last=False):
                for e in range(NE - 1):
                    act_(k, e + 1, then_high=k if e == NE - 2 and not last else None)
                    products(k, e)
                if last:
                    high(k)
                else:
                    router(k + 1)
                    act_(k + 1, 0)

            act_(0, 0)
            router(0)
            with act.Fori(0, NBLK - 1) as k:
                block_(k)
            block_(NBLK - 1, last=True)

        @block.tensor
        def _(pe):
            whi, wlo = g["whi"], g["wlo"]

            def logits(k):
                for u in range(TPB):
                    for j, yy in enumerate((yhi, ylo)):
                        for c in range(CT):
                            last = nc.tensor.matmul(ps_t[:, 0, u * 2 * NE:(u + 1) * 2 * NE], yy[:, c, u * P:(u + 1) * P],
                                                    g["gws"][:, c].rearrange("p j e -> p (j e)"),
                                                    start=(j + c == 0), stop=(j + c == 2))
                last.then_inc(s_lg, 1)

            def up(k, e, first=False):
                for f in range(2):
                    if not first:
                        pe.wait_ge(s_ac, 2 * NE * k + 2 * (e - 1) + (f + 1))
                    for ps, o in ((ps_g[f], f * P), (ps_u[f], ED + f * P)):
                        for j, (w, yy) in enumerate(split_passes((whi, yhi), (wlo, ylo))):
                            for c in range(CT):
                                last = nc.tensor.matmul(ps[:], w[:, e, c * 512 + o:c * 512 + o + P], yy[:, c],
                                                        start=(j + c == 0), stop=(j == 2 and c == 1))
                    last.then_inc(s_gu, 1)

            def down(k, e, first=False):
                pe.wait_ge(s_al, 2 * NE * k + 2 * (e + 1))
                for u in range(TPB):
                    if not first and u % 2 == 0:
                        pe.wait_ge(s_mix, TPB * NE * k + TPB * (e - 1) + (u + 2))
                    for j, (w, aa) in enumerate(split_passes((whi, ahi), (wlo, alo))):
                        for f in range(2):
                            last = nc.tensor.matmul(ps_d[:, u], aa[:, e % 2, f, u * P:(u + 1) * P],
                                                    w[:, e, 1024 + f * C:1024 + (f + 1) * C],
                                                    start=(j + f == 0), stop=(j == 2 and f == 1))
                    if u % 2:
                        last.then_inc(s_dn, 1)

            def products(k, e):
                heads = [(h, h // 2, h % 2) for h in range(GH)]
                if e == 0:
                    pe.wait_ge(s_wl, 16 * LOADS * (k + 1))
                    pe.wait_ge(s_rt, STEPS * k + 2)
                    for t in range(2):
                        for h in range(GH):
                            last = nc.tensor.transpose(ps_t[0:96, t, h * KD:(h + 1) * KD],
                                                       wkcq[:, h, 96 * t:96 * t + 96], ident)
                elif e == 1:
                    pe.wait_ge(s_me, ME * k + 1)
                    for h, pr, h2 in heads:
                        for t in range(2):
                            nc.tensor.matmul(ps_t[64 * h2:64 * h2 + 64, 0, pr * KD:(pr + 1) * KD],
                                                    wqr[:, t, h], kcqT[:, t, h], start=(t == 0), stop=(t == 1))
                    for pr in range(2):
                        last = nc.tensor.transpose(ps_t[:, 1, pr * DCTX:(pr + 1) * DCTX],
                                                   wkr[:, 2 * pr:2 * pr + 2, :].rearrange("p h r -> p (h r)"),
                                                   ident[0:DCTX, 0:DCTX])
                elif e == 2:
                    pe.wait_ge(s_me, ME * k + 3)
                    for h in range(GH):
                        for ot in range(2):
                            o = (h % 2) * C + ot * P
                            last = nc.tensor.transpose(ps_t[:, h // 2, o:o + P], wo[:, ot, h * KD:(h + 1) * KD], ident)
                elif e == 3:
                    pe.wait_ge(s_me, ME * k + 4)
                    for h, pr, h2 in sorted(heads, key=lambda v: v[2]):
                        last = nc.tensor.matmul(ps_t[:, h2, pr * DCTX:(pr + 1) * DCTX], a1T[64 * h2:64 * h2 + 64, pr],
                                                krT[64 * h2:64 * h2 + 64, pr], start=True, stop=True)
                elif e == 4:
                    pe.wait_ge(s_me, ME * k + 5)
                    for h, pr, h2 in heads:
                        nc.tensor.matmul(ps_t[64 * h2:64 * h2 + 64, 1, pr * C:(pr + 1) * C], wkv[:, h], woT[:, h],
                                         start=True, stop=True)
                    for ct in range(CT):
                        for h, pr, h2 in heads:
                            o = (ct * GH + h) * DCTX
                            last = nc.tensor.matmul(ps_t[:, 0, o:o + DCTX], wq[:, h, ct * P:(ct + 1) * P], a2[:, h2, pr],
                                                    start=True, stop=True)
                else:
                    return
                last.then_inc(s_mt, 1)

            def block_(k, first=False, last=False):
                for e in range(NE):
                    if e + 1 < NE:
                        up(k, e + 1)
                        products(k, e)
                    elif not last:
                        pe.wait_ge(s_yl, k + 1)
                        logits(k + 1)
                        up(k + 1, 0)
                    if e == NE - 2:
                        pe.wait_ge(s_me, ME * (k + 1))
                        transpose_y(nc, g, pe, ps_t, ident, s_yn, s_yt, k)
                    down(k, e, first and e == 0)

            up(0, 0, first=True)
            logits(0)
            block_(0, first=True)
            with pe.Fori(1, NBLK - 1) as k:
                block_(k)
            block_(NBLK - 1, last=True)


def attn1_phase(nc, a, g, sb, pb, sem):
    ident = g["const"][:, C_ID:C_ID + P]
    NP = H // 2
    HH = H // 2
    y, yhi, ylo = g["y"], g["yhi"], g["ylo"]
    qt = sb("q_tilT", [P, NP, BT])
    kvbd = [sb(f"kv_blockdiag{u}", [P, 2, P]) for u in range(TPB)]
    kvbT = sb("kv_blockdiagT", [P, 2, P])
    z2 = sb("probs", [P, 2, H, S])
    pT = sb("probsT", [P, NP, P])
    cT = sb("ctxT", [P, NP, 2, S])
    chi = sb("ctxT_hi", [P, 2, NP, 2, S], F32R)
    clo = sb("ctxT_lo", [P, 2, NP, 2, S], F32R)
    pmhi = sb("p_out_hi", [P, NP, C], F32R)
    pmlo = sb("p_out_lo", [P, NP, C], F32R)
    mx = sb("score_max", [P, H])
    sm = sb("prob_sum", [P, H])
    rec = sb("sum_recip", [P, H])
    raw = sb("ffn_raw", [P, 3 * 1536])
    QN = 3 * 1536 // NBLK
    p2 = sb("power_of_two", [P, QN])
    rnd = sb("rounded", [P, QN])
    ps_s = pb("ps_scores", [P, 2, 512])
    ps_pT = pb("ps_probsT", [P, NP, P])
    ps_c = pb("ps_ctxT", [P, 2, 512])
    ps_y = pb("ps_y", [P, 512])
    ps_k = pb("ps_kvT", [P, 512])

    s_raw, s_q8 = [sem(f"{n}_raw_loaded") for n in ("gate", "up", "down")], sem("fp8_step")
    s_st, s_rs, s_rd = sem("statistics"), sem("rstd_step"), sem("rstd_ready")
    s_yn, s_yt, s_yh, s_yl = sem("y_normed"), sem("y_transposed"), sem("y_hi"), sem("y_lo")
    s_q, s_qe = sem("q_ready"), sem("q_in_sbuf")
    s_kb, s_kT, s_kTe = sem("kv_ready"), sem("kv_transposed"), sem("kvT_in_sbuf")
    s_sc, s_mx, s_sh, s_ex, s_sum, s_rec, s_pr = (sem("scores_ready"), sem("max_ready"), sem("scores_shifted"),
                                                  sem("exp_ready"), sem("sum_ready"), sem("recip_ready"), sem("probs_ready"))
    s_pT, s_pTe, s_c, s_y = (sem("probs_transposed"), sem("probsT_in_sbuf"), sem("ctx_ready"),
                             sem("y_ready"))
    s_x, s_yf = sem("x_updated"), sem("y_bank_free")
    s_ch, s_cl, s_ph, s_pl = sem("ctx_hi"), sem("ctx_lo"), sem("p_out_hi"), sem("p_out_lo")
    QSTEPS = 6

    with nc.Block() as block:

        @block.sync
        def _(sp):
            for j, (name, t) in enumerate((("L1_ffn_gate_w", 2), ("L1_ffn_up_w", 2), ("L1_ffn_down_w", 6))):
                dst = raw[:, j * 1536:(j + 1) * 1536].rearrange("p (t n) -> p t n", t=t)
                sp.dma_start(dst, a[name].rearrange("(t p) n -> p t n", p=P)).then_inc(s_raw[j], 16)

        @block.gpsimd
        def _(pool):
            half = g["const"][:, C_HALF:C_HALF + 2]

            def keys(t, u, first=False):
                if not first:
                    pool.wait_ge(s_c, t - (TPB - 1))
                src = g["ctxdup"][:, bass.ds(2 * t, 2), :]
                nc.gpsimd.tensor_tensor(kvbd[u][:].rearrange("p b (h d) -> p b h d", h=2), bc(src, 2, 2),
                                        bc(bc(half, 1, 2), 3, DCTX), ALU.mult).then_inc(s_kb, 1)

            def low(t, u):
                pool.wait_ge(s_ch, t + 2)
                nc.gpsimd.tensor_tensor(clo[:, u % 2], cT[:], chi[:, u % 2].bitcast(FP32), ALU.subtract).then_inc(s_cl, 1)

            for u in range(TPB):
                keys(u, u, first=True)
            pool.wait_ge(s_ph, 1)
            nc.gpsimd.tensor_tensor(pmlo[:], g["pm"][:], pmhi[:].bitcast(FP32), ALU.subtract).then_inc(s_pl, 1)
            pool.sem_inc(s_cl, 1)
            rstd_link = Link(pool, s_rs)
            pool.wait_ge(s_st, 1)
            ln_rstd(nc.gpsimd, g, rstd_link, NT - TPB, NT)
            pool.sem_inc(s_rd, 1)
            with pool.Fori(0, NBLK - 1) as k:
                for u in range(TPB):
                    low(TPB * k + u, u)
                    keys(TPB * k + (u + TPB), u)
            for u in range(TPB):
                low(NT - TPB + u, u)
                if u == 1:
                    pool.wait_ge(s_yf, NT - TPB + 1)
                    ln_rstd(nc.gpsimd, g, rstd_link, 0, NT - TPB)
                    pool.sem_inc(s_rd, 1)

        @block.vector
        def _(dve):
            def const_or_snap(n):
                return n if isinstance(n, int) else dve.snap(n)

            def normed(k):
                for u in range(TPB):
                    normed_tile(nc, g, TPB * k + u, u).then_inc(s_yn, 1)

            def low(n):
                dve.wait_ge(s_yh, n + 1)
                nc.vector.tensor_tensor(ylo[:], ps_c[:], yhi[:].bitcast(FP32), ALU.subtract).then_inc(s_yl, 1)

            def ffn_weights(k):
                link = Link(dve, s_q8, k * QSTEPS)
                w = raw[:, bass.ds(k * QN, QN)]
                link(nc.vector.tensor_scalar(p2[:].bitcast(I32), w.bitcast(I32), 0x7F800000, None, ALU.bitwise_and))
                link(nc.vector.tensor_scalar(p2[:], p2[:], 2.0 ** -6, 1.5 * 2.0 ** 20, ALU.max, ALU.mult))
                link(nc.vector.tensor_tensor(rnd[:], w, p2[:], ALU.add))
                link(nc.vector.tensor_tensor(rnd[:], rnd[:], p2[:], ALU.subtract))
                link(nc.vector.tensor_scalar(p2[:], rnd[:], OVERFLOW, 0.0, ALU.mult, ALU.mult))
                link(nc.vector.tensor_tensor(g["wq8"][:, bass.ds(k * QN, QN)], rnd[:], p2[:], ALU.add))
                assert link.n == QSTEPS

            def shift(t, u, j):
                z = z2[:, u % 2]
                n = const_or_snap(2 * t + (j + 1))
                hs = slice(HH * j, HH * (j + 1))
                sv = ps_s[:, j].rearrange("p (h k) -> p h k", k=S)
                dve.wait_ge(s_sc, n)
                nc.vector.tensor_reduce(mx[:, hs], sv, AX.X, ALU.max).then_inc(s_mx, 1)
                dve.wait_ge(s_mx, n)
                nc.vector.tensor_tensor(z[:, hs], sv, bc(mx[:, hs], 2, S), ALU.subtract).then_inc(s_sh, 1)

            def normalise(t, u, j):
                z = z2[:, u % 2]
                n = const_or_snap(2 * t + (j + 1))
                hs = slice(HH * j, HH * (j + 1))
                dve.wait_ge(s_ex, n)
                nc.vector.tensor_reduce(sm[:, hs], z[:, hs], AX.X, ALU.add).then_inc(s_sum, 1)
                dve.wait_ge(s_sum, n)
                nc.vector.reciprocal(rec[:, hs], sm[:, hs]).then_inc(s_rec, 1)
                dve.wait_ge(s_rec, n)
                nc.vector.tensor_tensor(z[:, hs], z[:, hs], bc(rec[:, hs], 2, S), ALU.mult).then_inc(s_pr, 1)

            def residual(t):
                n = const_or_snap(t + 1)
                dve.wait_ge(s_y, n)
                nc.vector.scalar_tensor_tensor(g["x"][:, t, :], ps_y[:, 0:C], g["tg"][:, 1:2], g["x"][:, t, :],
                                               ALU.mult, ALU.add).then_inc(s_x, 1)
                dve.wait_ge(s_x, n)
                nc.vector.bn_stats(g["bn"][:, t, :], g["x"][:, t, :]).then_inc(s_yf, 1)

            def block_(k, first=False, last=False):
                for u in range(TPB):
                    t = TPB * k + u
                    if u == TPB - 1 and not last:
                        ffn_weights(k + 1)
                    if not (last and u == TPB - 1):
                        shift(t + 1, u + 1, 0)
                        if u == 2 and not last:
                            low(k)
                        shift(t + 1, u + 1, 1)
                        normalise(t + 1, u + 1, 0)
                        normalise(t + 1, u + 1, 1)
                    if last and u == TPB - 1:
                        dve.wait_ge(s_rd, 2)
                        normed(0)
                    if u == 1 and not last:
                        normed(k + 1)
                    if not (first and u == 0):
                        residual(t - 1)

            dve.sem_inc(s_yf, 1)
            for t in range(NT - TPB, NT):
                last = nc.vector.bn_stats(g["bn"][:, t, :], g["x"][:, t, :])
            last.then_inc(s_st, 1)
            dve.wait_ge(s_raw[0], 16)
            ffn_weights(0)
            shift(0, 0, 0)
            shift(0, 0, 1)
            normalise(0, 0, 0)
            normalise(0, 0, 1)
            dve.wait_ge(s_raw[1], 16)
            dve.wait_ge(s_raw[2], 16)
            block_(0, first=True)
            dve.wait_ge(s_rd, 1)
            with dve.Fori(1, NBLK - 1) as k:
                block_(k)
            block_(NBLK - 1, last=True)
            low(NBLK - 1)
            residual(NT - 1)

        @block.scalar
        def _(act):
            def high(n):
                act.wait_ge(s_yt, n + 1)
                nc.scalar.activation(yhi[:], ps_c[:], ACT.Copy).then_inc(s_yh, 1)

            def queries(k, ps):
                for p in ps:
                    act.wait_ge(s_q, NP * k + (p + 1))
                    nc.scalar.activation(qt[:, p], ps_c[:, p % 2], ACT.Copy).then_inc(s_qe, 1)

            def kvT(t):
                act.wait_ge(s_kT, t + 1)
                nc.scalar.activation(kvbT[:], ps_k[:, 0:2 * P], ACT.Copy).then_inc(s_kTe, 1)

            def probsT(t):
                act.wait_ge(s_pT, t + 1)
                nc.scalar.activation(pT[:], ps_pT[:], ACT.Copy).then_inc(s_pTe, 1)

            def exps(t, u, j):
                z = z2[:, u % 2]
                act.wait_ge(s_sh, 2 * t + (j + 1))
                hs = slice(HH * j, HH * (j + 1))
                nc.scalar.activation(z[:, hs], z[:, hs], ACT.Exp).then_inc(s_ex, 1)

            def ctxT(t, u):
                act.wait_ge(s_c, t + 1)
                act.wait_ge(s_cl, t + 1)
                src = ps_c[:].rearrange("p b (q s) -> p b q s", q=NP)
                nc.scalar.activation(cT[:].rearrange("p q b s -> p b q s"), src, ACT.Copy)
                nc.scalar.activation(chi[:, u % 2].rearrange("p q b s -> p b q s"), src, ACT.Copy).then_inc(s_ch, 1)

            def block_(k, last=False):
                for u in range(TPB):
                    t = TPB * k + u
                    if u == TPB - 1:
                        if not last:
                            queries(k + 1, range(6))
                            exps(t + 1, u + 1, 0)
                            queries(k + 1, range(6, NP))
                        probsT(t)
                        if not last:
                            kvT(t + 2)
                            exps(t + 1, u + 1, 1)
                    else:
                        if u == 2 and not last:
                            high(k)
                        probsT(t)
                        exps(t + 1, u + 1, 0)
                        if not (last and u >= 2):
                            kvT(t + 2)
                        exps(t + 1, u + 1, 1)
                    ctxT(t, u)

            act.sem_inc(s_ch, 1)
            nc.scalar.activation(pmhi[:], g["pm"][:], ACT.Copy).then_inc(s_ph, 1)
            queries(0, range(4))
            kvT(0)
            queries(0, range(4, NP))
            exps(0, 0, 0)
            kvT(1)
            exps(0, 0, 1)
            with act.Fori(0, NBLK - 1) as k:
                block_(k)
            block_(NBLK - 1, last=True)
            high(NBLK - 1)

        @block.tensor
        def _(pe):
            def queries(k, ps):
                for p in ps:
                    if p >= 2:
                        pe.wait_ge(s_qe, NP * k + (p - 1))
                    for j, (w, yy) in enumerate(split_passes((g["mhi"], yhi), (g["mlo"], ylo))):
                        for c in range(CT):
                            last = nc.tensor.matmul(ps_c[:, p % 2], w[:, c, p * P:(p + 1) * P], yy[:, c],
                                                    start=(j + c == 0), stop=(j == 2 and c == 1))
                    last.then_inc(s_q, 1)

            def kvT(t, u):
                pe.wait_ge(s_kb, t + 1)
                for b2 in range(2):
                    last = nc.tensor.transpose(ps_k[:, b2 * P:(b2 + 1) * P], kvbd[u][:, b2], ident)
                last.then_inc(s_kT, 1)

            def scores(t, u, j, first=False):
                pe.wait_ge(s_kTe, t + 1)
                if not first:
                    pe.wait_ge(s_sh, 2 * (t - 1) + (j + 1))
                for p in range(4 * j, 4 * j + 4):
                    for b2 in range(2):
                        c = u * P + 64 * b2
                        last = nc.tensor.matmul(ps_s[64 * b2:64 * b2 + 64, j, (p % 4) * P:(p % 4 + 1) * P],
                                                qt[:, p, c:c + 64], kvbT[:, b2], start=True, stop=True)
                last.then_inc(s_sc, 1)

            def probsT(t, u):
                z = z2[:, u % 2]
                pe.wait_ge(s_pr, 2 * t + 2)
                for p in range(NP):
                    last = nc.tensor.transpose(ps_pT[:, p], z[:, 2 * p:2 * p + 2].rearrange("p h k -> p (h k)"), ident)
                last.then_inc(s_pT, 1)

            def ctxT(t, u):
                pe.wait_ge(s_kb, t + 1)
                pe.wait_ge(s_pTe, t + 1)
                for b2 in range(2):
                    last = nc.tensor.matmul(ps_c[:, b2], kvbd[u][:, b2], pT[:, :, 64 * b2:64 * b2 + 64],
                                            start=True, stop=True)
                last.then_inc(s_c, 1)

            def project(t, u):
                pe.wait_ge(s_cl, t + 2)
                pe.wait_ge(s_yf, t + 1)
                for j, (cc, w) in enumerate(split_passes((chi, pmhi), (clo, pmlo))):
                    for p in range(NP):
                        last = nc.tensor.matmul(ps_y[:, 0:C], cc[:, u % 2, p].rearrange("p b s -> p (b s)"), w[:, p],
                                                start=(j + p == 0), stop=(j == 2 and p == NP - 1))
                last.then_inc(s_y, 1)

            def block_(k, first=False, last=False):
                for u in range(TPB):
                    t = TPB * k + u
                    if u < TPB - 1:
                        scores(t + 1, u + 1, 0)
                        pe.wait_ge(s_ch, t + 1)
                        if u == 2 and not last:
                            transpose_y(nc, g, pe, ps_c, ident, s_yn, s_yt, k)
                        probsT(t, u)
                        scores(t + 1, u + 1, 1)
                        if not (last and u == 2):
                            kvT(t + 2, (u + 2) % TPB)
                        if u == 2 and not last:
                            pe.wait_ge(s_yl, k + 1)
                    elif last:
                        probsT(t, u)
                        pe.wait_ge(s_ch, t + 1)
                    else:
                        pe.wait_ge(s_ch, t + 1)
                        queries(k + 1, range(5))
                        pe.wait_ge(s_qe, NP * (k + 1) + 4)
                        scores(t + 1, 0, 0)
                        queries(k + 1, range(5, NP))
                        probsT(t, u)
                        pe.wait_ge(s_qe, NP * (k + 2))
                        scores(t + 1, 0, 1)
                        kvT(t + 2, 1)
                    ctxT(t, u)
                    if not (first and u == 0):
                        project(t - 1, u - 1)

            queries(0, range(5))
            kvT(0, 0)
            pe.wait_ge(s_qe, 4)
            scores(0, 0, 0, first=True)
            queries(0, range(5, NP))
            pe.wait_ge(s_qe, NP)
            scores(0, 0, 1, first=True)
            kvT(1, 1)
            pe.wait_ge(s_pl, 1)
            block_(0, first=True)
            with pe.Fori(1, NBLK - 1) as k:
                block_(k)
            block_(NBLK - 1, last=True)
            pe.wait_ge(s_ch, NT + 1)
            transpose_y(nc, g, pe, ps_c, ident, s_yn, s_yt, NBLK - 1)
            project(NT - 1, TPB - 1)


def ffn_phase(nc, a, g, out, sb, pb, sem):
    ident = g["const"][:, C_ID:C_ID + P]
    wg, wu, wd = (g["wq8"][:, j * 1536:(j + 1) * 1536] for j in range(3))
    y, yhi, ylo = g["y"], g["yhi"], g["ylo"]
    sg = sb("silu", [P, 2, BT])
    ac = sb("act", [P, FT, BT])
    ahi = sb("act_hi", [P, FT, BT], F32R)
    alo = sb("act_lo", [P, FT, BT], F32R)
    ot = sb("scaled", [P, TPB, C])
    ps_g = [pb(f"ps_gate{f}", [P, BT]) for f in range(2)]
    ps_u = [pb(f"ps_up{f}", [P, BT]) for f in range(2)]
    ps_t = pb("ps_yT", [P, CT, BT])
    ps_d = pb("ps_down", [P, TPB, C])
    s_rs, s_rd = sem("rstd_step"), sem("rstd_ready")
    s_yn, s_yt, s_yh, s_yl = sem("y_normed"), sem("y_transposed"), sem("y_hi"), sem("y_lo")
    s_gu, s_sg, s_ac, s_ah, s_al = sem("gate_up_ready"), sem("silu_ready"), sem("act_ready"), sem("act_hi"), sem("act_lo")
    s_dn, s_sc, s_x, s_out = sem("down_ready"), sem("scaled"), sem("x_final"), sem("stored")

    with nc.Block() as block:

        @block.sync
        def _(sp):
            ov = out.rearrange("(t b) s c -> t (b s) c", b=2)
            with sp.Fori(0, NT) as t:
                sp.wait_ge(s_x, t + 1)
                sp.dma_start(ov[bass.ds(t, 1)].rearrange("t p c -> (t p) c"), g["x"][:, t, :]).then_inc(s_out, 16)
            sp.wait_ge(s_out, 16 * NT)

        @block.gpsimd
        def _(pool):
            link = Link(pool, s_rs)
            ln_rstd(nc.gpsimd, g, link, NT - TPB, NT)
            pool.sem_inc(s_rd, 1)

        @block.vector
        def _(dve):
            def low(n):
                dve.wait_ge(s_yh, n + 1)
                nc.vector.tensor_tensor(ylo[:], ps_t[:], yhi[:].bitcast(FP32), ALU.subtract).then_inc(s_yl, 1)

            def product(k, f):
                dve.wait_ge(s_sg, FT * k + (f + 1))
                nc.vector.scalar_tensor_tensor(ac[:, f], ps_u[f % 2][:], g["fus"][:, f:f + 1], sg[:, f % 2],
                                               ALU.mult, ALU.mult).then_inc(s_ac, 1)

            def product_low(k, f):
                dve.wait_ge(s_ah, FT * k + (f + 1))
                nc.vector.tensor_tensor(alo[:, f], ac[:, f], ahi[:, f].bitcast(FP32), ALU.subtract).then_inc(s_al, 1)

            def block_(k, last=False):
                product(k, 0)
                for f in range(1, FT):
                    if f == FT - 1:
                        product_low(k, f - 1)
                    product(k, f)
                    if f < FT - 1:
                        product_low(k, f - 1)
                    if f == 1 and not last:
                        dve.wait_ge(s_rd, 1)
                    if f <= TPB and not last:
                        normed_tile(nc, g, TPB * (k + 1) + (f - 1), f - 1).then_inc(s_yn, 1)
                product_low(k, FT - 1)
                if not last:
                    low(k)
                for u in range(TPB):
                    t = TPB * k + u
                    if u % 2 == 0:
                        dve.wait_ge(s_dn, 2 * k + (u // 2 + 1))
                    nc.vector.tensor_tensor(ot[:, u], ps_d[:, u], g["dsg"][:], ALU.mult).then_inc(s_sc, 1)
                for u in range(TPB):
                    t = TPB * k + u
                    dve.wait_ge(s_sc, TPB * k + (u + 1))
                    nc.vector.tensor_tensor(g["x"][:, t, :], g["x"][:, t, :], ot[:, u], ALU.add).then_inc(s_x, 1)

            with dve.Fori(0, NBLK - 1) as k:
                block_(k)
            block_(NBLK - 1, last=True)

        @block.scalar
        def _(act):
            def high(n):
                act.wait_ge(s_yt, n + 1)
                nc.scalar.activation(yhi[:], ps_t[:], ACT.Copy).then_inc(s_yh, 1)

            def silu(k, f):
                act.wait_ge(s_gu, FT * k + (f + 1))
                nc.scalar.activation(sg[:, f % 2], ps_g[f % 2][:], ACT.Silu, scale=g["fgs"][:, f:f + 1]).then_inc(s_sg, 1)

            def product_high(k, f):
                act.wait_ge(s_ac, FT * k + (f + 1))
                nc.scalar.activation(ahi[:, f], ac[:, f], ACT.Copy).then_inc(s_ah, 1)

            def block_(k, last=False):
                silu(k, 0)
                for f in range(1, FT - 1):
                    silu(k, f)
                    product_high(k, f - 1)
                product_high(k, FT - 2)
                silu(k, FT - 1)
                product_high(k, FT - 1)
                if not last:
                    high(k)

            with act.Fori(0, NBLK - 1) as k:
                block_(k)
            block_(NBLK - 1, last=True)

        @block.tensor
        def _(pe):
            def down(u, f):
                for j, aa in enumerate((ahi, alo)):
                    last_ = nc.tensor.matmul(ps_d[:, u], aa[:, f, u * P:(u + 1) * P], wd[:, f * C:(f + 1) * C],
                                             start=(j + f == 0), stop=(j == 1 and f == FT - 1))
                return last_

            def block_(k, last=False):
                for f in range(FT):
                    if f >= 2:
                        pe.wait_ge(s_ac, FT * k + (f - 1))
                    for ps, w in ((ps_g[f % 2], wg), (ps_u[f % 2], wu)):
                        for j, yy in enumerate((yhi, ylo)):
                            for c in range(CT):
                                last_ = nc.tensor.matmul(ps[:], w[:, c * FI + f * P:c * FI + (f + 1) * P], yy[:, c],
                                                         start=(j + c == 0), stop=(j + c == 2))
                    last_.then_inc(s_gu, 1)
                if not last:
                    transpose_y(nc, g, pe, ps_t, ident, s_yn, s_yt, k)
                pe.wait_ge(s_al, FT * k + (FT - 1))
                for u in (0, 2):
                    for f in range(FT - 1):
                        down(u, f)
                pe.wait_ge(s_al, FT * (k + 1))
                for u in (0, 2):
                    down(u, FT - 1)
                for u in (1, 3):
                    for f in range(FT):
                        last_ = down(u, f)
                    last_.then_inc(s_dn, 1)
                if not last:
                    pe.wait_ge(s_yl, k + 1)

            with pe.Fori(0, NBLK - 1) as k:
                block_(k)
            block_(NBLK - 1, last=True)


OVERFLOW = 3.4028234663852886e38 / FP8_EDGE


_INS = ['x', 'ctx_512', 'g_xattn', 'g_ffn', 'L0_xattn_q_norm_w', 'L0_xattn_k_norm_w', 'L0_xattn_w_out',
        'L0_ffn_router_scale', 'L0_ffn_gate_w', 'L0_ffn_gate_up', 'L0_ffn_down', 'L0_ffn_per_expert_scale',
        'L1_xattn_Wq', 'L1_xattn_w_kc_q', 'L1_xattn_w_kc_kv', 'L1_xattn_W_qr', 'L1_xattn_W_kr', 'L1_xattn_Wo',
        'L1_ffn_gate_w', 'L1_ffn_up_w', 'L1_ffn_down_w', 'L1_ffn_gate_scale', 'L1_ffn_up_scale', 'L1_ffn_down_scale']


def constants():
    import numpy as np

    c = np.zeros((P, C_END), np.float32)
    p = np.arange(P)
    c[:, C_ID:C_ID + P] = np.eye(P, dtype=np.float32)
    c[p, C_NSEL + (p // HD) % 4] = 1
    c[p, C_HALF + p // S] = 1
    pos = np.arange(S, dtype=np.float32)

    def table(dim, order):
        inv = (np.float32(1) / np.float32(10000.0) ** (np.arange(0, dim, 2, dtype=np.float32) / np.float32(dim)))
        f = pos[:, None] * inv.astype(np.float32)[None, :]
        cos, sin = np.cos(f)[:, order], np.sin(f)[:, order]
        sin[:, :dim // 2] = -sin[:, :dim // 2]
        return np.tile(cos, (2, 1)), np.tile(sin, (2, 1))

    c[:, C_COS0:C_COS0 + HD], c[:, C_SIN0:C_SIN0 + HD] = table(HD, np.tile(np.arange(HD // 2), 2))
    c[:, C_COS1:C_COS1 + DCTX], c[:, C_SIN1:C_SIN1 + DCTX] = table(DCTX, np.repeat(np.arange(DCTX // 2), 2))
    c[:, C_IOTA:C_IOTA + NE] = np.arange(NE)
    return c


def causal_mask():
    import numpy as np

    causal = np.arange(S)[None, :] > (np.arange(P) % S)[:, None]
    return np.tile(np.where(causal, np.float32(-1e30), np.float32(0)), (1, 8))


def kernel(**inputs):
    import numpy as _np
    import concourse.bacc as _bacc
    from concourse import mybir as _mybir
    from concourse.bass_utils import run_bass_kernel_spmd as _run

    nc = _bacc.Bacc("TRN2", target_bir_lowering=False, num_devices=1)
    arrays, aps = {}, {}
    made = {"const": constants, "mask": causal_mask}
    for name in _INS + list(made):
        v = made[name]() if name in made else _np.ascontiguousarray(inputs[name])
        arrays[f"in_{name}_dram"] = v
        aps[name] = nc.dram_tensor(f"in_{name}_dram", v.shape, _mybir.dt.from_np(v.dtype), kind="ExternalInput").ap()
    out = nc.dram_tensor("out_0_dram", (B, S, C), FP32, kind="ExternalOutput").ap()
    stack_kernel(nc, aps, out)
    r = _run(nc, [arrays], core_ids=[0])
    return r.results[0]["out_0_dram"]
```
